# Optimizing a Trainium2 kernel written in Bass

```python
import numpy as np
import jax
import jax.numpy as jnp

def _softmax(x, axis=-1):
    return jax.nn.softmax(x, axis=axis)

def _gelu(x):
    return jax.nn.gelu(x, approximate=True)

def _silu(x):
    return jax.nn.silu(x)

def _sigmoid(x):
    return jax.nn.sigmoid(x)

def _layernorm(x, axis=-1, eps=1e-05):
    m = jnp.mean(x, axis=axis, keepdims=True)
    v = jnp.var(x, axis=axis, keepdims=True)
    return (x - m) / jnp.sqrt(v + eps)

def _scatter_add(tgt, idx, src, axis=0):
    return tgt.at[idx].add(src)

def _segment_sum(src, seg, n):
    return jax.ops.segment_sum(src, seg, n)
kernel_name = 'mk_decoder_postln_d2_seqx_r4_c66184'

def setup_inputs(seed: int=0):
    np.random.seed(seed)
    _w = jnp.asarray

    def _rec_inputs():
        import jax
        import jax.numpy as jnp
        _rk = jax.random.key(seed)
        x = 7.22e-05 + 1 * jax.random.normal(jax.random.fold_in(_rk, 1), (1, 2048, 256), jnp.float32)
        _lenS = 2048 - jax.random.randint(jax.random.fold_in(_rk, 7), (1,), 0, max(1, 2048 // 4) + 1, jnp.int32)
        _lenS2 = 1601 - jax.random.randint(jax.random.fold_in(_rk, 8), (1,), 0, max(1, 1601 // 4) + 1, jnp.int32)
        _ctx_1024P = jax.random.normal(jax.random.fold_in(_rk, 11), (1, 16, 256), jnp.float32)
        _ctx_1024c = jax.random.dirichlet(jax.random.fold_in(_rk, 511), 0.3 * jnp.ones((16,), jnp.float32), (1, 1601))
        _ctx_1024t = jnp.einsum('bsk,bkd->bsd', _ctx_1024c, _ctx_1024P)
        _ctx_1024t = _ctx_1024t * jax.lax.rsqrt(jnp.mean(jnp.square(_ctx_1024t)) + 1e-12) * 0.953939
        ctx_1024 = 4.13588e-05 + 0.999923 * (_ctx_1024t + 0.3 * jax.random.normal(jax.random.fold_in(_rk, 611), (1, 1601, 256), jnp.float32))
        return (x, ctx_1024)
    x, ctx_1024 = _rec_inputs()

    def _L0_attn_setup():
        import jax, jax.numpy as jnp
        import numpy as np
        BATCH, SEQ, D_MODEL = (4, 512, 256)
        D_INNER, D_STATE, D_CONV, DT_RANK = (2 * D_MODEL, 16, 4, D_MODEL // 16)
        LN_EPS = 1e-05

        def _mamba_core(xn, W_in, conv_w, conv_b, W_x, W_dt, b_dt, A_log, D_skip, W_out):
            b, l, _ = xn.shape
            xz = xn @ W_in
            xi, z = jnp.split(xz, 2, axis=-1)
            xp = jnp.pad(xi, ((0, 0), (D_CONV - 1, 0), (0, 0)))
            xc = sum((xp[:, k:k + l, :] * conv_w[:, k] for k in range(D_CONV))) + conv_b
            xc = jax.nn.silu(xc)
            dbl = xc @ W_x
            dt, Bm, Cm = jnp.split(dbl, [DT_RANK, DT_RANK + D_STATE], axis=-1)
            dt = jax.nn.softplus(dt @ W_dt + b_dt)
            A = -jnp.exp(A_log)

            def step(h, inputs):
                dt_t, B_t, C_t, x_t = inputs
                h = jnp.exp(dt_t[..., None] * A) * h + (dt_t * x_t)[..., None] * B_t[:, None, :]
                y = jnp.einsum('bdn,bn->bd', h, C_t)
                return (h, y)
            h0 = jnp.zeros((b, D_INNER, D_STATE), xc.dtype)
            _, ys = jax.lax.scan(step, h0, (dt.transpose(1, 0, 2), Bm.transpose(1, 0, 2), Cm.transpose(1, 0, 2), xc.transpose(1, 0, 2)))
            y = ys.transpose(1, 0, 2) + D_skip * xc
            y = y * jax.nn.silu(z)
            return y @ W_out
        key = jax.random.key(seed)
        ks = jax.random.split(key, 10)
        s = lambda fan: 1.0 / np.sqrt(fan)
        inp = {'x': jax.random.normal(ks[0], (BATCH, SEQ, D_MODEL), jnp.float32), 'gamma': jnp.ones((D_MODEL,), jnp.float32), 'beta': jnp.zeros((D_MODEL,), jnp.float32), 'W_in': jax.random.normal(ks[1], (D_MODEL, 2 * D_INNER), jnp.float32) * s(D_MODEL), 'conv_w': jax.random.normal(ks[2], (D_INNER, D_CONV), jnp.float32) * s(D_CONV), 'conv_b': jnp.zeros((D_INNER,), jnp.float32), 'W_x': jax.random.normal(ks[3], (D_INNER, DT_RANK + 2 * D_STATE), jnp.float32) * s(D_INNER), 'W_dt': jax.random.normal(ks[4], (DT_RANK, D_INNER), jnp.float32) * s(DT_RANK), 'b_dt': jax.random.uniform(ks[5], (D_INNER,), jnp.float32, -4.0, -2.0), 'A_log': jnp.broadcast_to(jnp.log(jnp.arange(1, D_STATE + 1, dtype=jnp.float32)), (D_INNER, D_STATE)).copy(), 'D_skip': jnp.ones((D_INNER,), jnp.float32), 'W_out': jax.random.normal(ks[6], (D_INNER, D_MODEL), jnp.float32) * s(D_INNER)}
        return inp
    _L0_attn_all = _L0_attn_setup()
    _L0_attn_in = {k: v for k, v in _L0_attn_all.items() if k in ('gamma', 'beta', 'W_in', 'conv_w', 'conv_b', 'W_x', 'W_dt', 'b_dt', 'A_log', 'D_skip', 'W_out')}
    del _L0_attn_all

    def _L0_xattn_setup():
        import jax, jax.numpy as jnp
        import numpy as np
        B, S, D_MODEL, N_HEADS = (4, 512, 256, 16)
        HEAD_DIM = D_MODEL // N_HEADS
        key = jax.random.key(seed)
        kq, kk, kv, kw = jax.random.split(key, 4)
        q = jax.random.normal(kq, (B, S, D_MODEL), dtype=jnp.float32)
        k = jax.random.normal(kk, (B, S, D_MODEL), dtype=jnp.float32)
        v = jax.random.normal(kv, (B, S, D_MODEL), dtype=jnp.float32)
        W_out = jax.random.normal(kw, (D_MODEL, D_MODEL), dtype=jnp.float32) * (1.0 / np.sqrt(D_MODEL))
        return {'q': q, 'k': k, 'v': v, 'W_out': W_out}
    _L0_xattn_all = _L0_xattn_setup()
    _L0_xattn_in = {k: v for k, v in _L0_xattn_all.items() if k in ('W_out',)}
    del _L0_xattn_all

    def _L0_ffn_setup():
        import jax, jax.numpy as jnp
        import numpy as np
        B, S, H, E, K = (2, 512, 256, 8, 2)
        FF = 4 * H
        EPS = 1e-05
        key = jax.random.key(seed)
        ks = jax.random.split(key, 5)
        rn = lambda k, shape, scale: jax.random.normal(k, shape, dtype=jnp.float32) * scale
        return {'x': rn(ks[0], (B, S, H), 1.0), 'router_W': rn(ks[1], (H, E), H ** (-0.5)), 'router_b': jnp.zeros((E,), jnp.float32), 'ln_g': jnp.ones((E, H), jnp.float32), 'ln_b': jnp.zeros((E, H), jnp.float32), 'W1': rn(ks[2], (E, H, FF), H ** (-0.5)), 'b1': jnp.zeros((E, FF), jnp.float32), 'W2': rn(ks[3], (E, FF, H), FF ** (-0.5)), 'b2': jnp.zeros((E, H), jnp.float32)}
    _L0_ffn_all = _L0_ffn_setup()
    _L0_ffn_in = {k: v for k, v in _L0_ffn_all.items() if k in ('router_W', 'router_b', 'ln_g', 'ln_b', 'W1', 'b1', 'W2', 'b2')}
    del _L0_ffn_all

    def _L1_attn_setup():
        import jax, jax.numpy as jnp
        import numpy as np
        import math
        E = 256
        H = 16
        Dh = E // H
        B = 4
        T = 256
        NUM_BUCKETS = 80
        MAX_DIST = 200
        SCALING = Dh ** (-0.5)
        ALPHA = 32.0

        def _rel_bucket(rel):
            nb = NUM_BUCKETS // 2
            buckets = (rel > 0).astype(jnp.int32) * nb
            rel = jnp.abs(rel)
            max_exact = nb // 2
            is_small = rel < max_exact
            large = max_exact + (jnp.log(jnp.maximum(rel, 1).astype(jnp.float32) / max_exact) / math.log(MAX_DIST / max_exact) * (nb - max_exact)).astype(jnp.int32)
            large = jnp.minimum(large, nb - 1)
            return buckets + jnp.where(is_small, rel, large)
        key = jax.random.key(seed)
        ks = jax.random.split(key, 12)
        s = 0.02
        return {'query': jax.random.normal(ks[0], (T, B, E), jnp.float32), 'wq': jax.random.normal(ks[1], (E, E), jnp.float32) * s, 'bq': jnp.zeros((E,), jnp.float32), 'wk': jax.random.normal(ks[2], (E, E), jnp.float32) * s, 'bk': jnp.zeros((E,), jnp.float32), 'wv': jax.random.normal(ks[3], (E, E), jnp.float32) * s, 'bv': jnp.zeros((E,), jnp.float32), 'wo': jax.random.normal(ks[4], (E, E), jnp.float32) * s, 'bo': jnp.zeros((E,), jnp.float32), 'rel_emb': jax.random.normal(ks[5], (NUM_BUCKETS, H), jnp.float32) * s, 'grep_w': jax.random.normal(ks[6], (8, Dh), jnp.float32) * s, 'grep_b': jnp.zeros((8,), jnp.float32), 'grep_a': jnp.ones((1, H, 1, 1), jnp.float32)}
    _L1_attn_all = _L1_attn_setup()
    _L1_attn_in = {k: v for k, v in _L1_attn_all.items() if k in ('wq', 'bq', 'wk', 'bk', 'wv', 'bv', 'wo', 'bo', 'rel_emb', 'grep_w', 'grep_b', 'grep_a')}
    del _L1_attn_all

    def _L1_xattn_setup():
        import jax, jax.numpy as jnp
        import numpy as np
        D_MODEL = 256
        N_HEADS = 16
        D_HEAD = D_MODEL // N_HEADS
        CAUSAL = True
        key = jax.random.key(seed)
        ks = jax.random.split(key, 7)
        B, T = (2, 512)
        scale = 1.0 / np.sqrt(D_MODEL)
        return {'q': jax.random.normal(ks[0], (B, T, D_MODEL), dtype=jnp.float32), 'k': jax.random.normal(ks[1], (B, T, D_MODEL), dtype=jnp.float32), 'v': jax.random.normal(ks[2], (B, T, D_MODEL), dtype=jnp.float32), 'w_q': jax.random.normal(ks[3], (D_MODEL, D_MODEL), dtype=jnp.float32) * scale, 'w_k': jax.random.normal(ks[4], (D_MODEL, D_MODEL), dtype=jnp.float32) * scale, 'w_v': jax.random.normal(ks[5], (D_MODEL, D_MODEL), dtype=jnp.float32) * scale, 'w_o': jax.random.normal(ks[6], (D_MODEL, D_MODEL), dtype=jnp.float32) * scale}
    _L1_xattn_all = _L1_xattn_setup()
    _L1_xattn_in = {k: v for k, v in _L1_xattn_all.items() if k in ('w_q', 'w_k', 'w_v', 'w_o')}
    del _L1_xattn_all

    def _L1_ffn_setup():
        import jax, jax.numpy as jnp
        import numpy as np
        B, T, C, H, E = (4, 512, 256, 512, 8)
        CAPACITY_FACTOR = 1.0
        key = jax.random.key(seed)
        ks = jax.random.split(key, 5)
        scale = 0.02
        return {'x': jax.random.normal(ks[0], (B, T, C), dtype=jnp.float32), 'Wg': jax.random.normal(ks[1], (E, C), dtype=jnp.float32) * scale, 'W1': jax.random.normal(ks[2], (E, H, C), dtype=jnp.float32) * scale, 'W2': jax.random.normal(ks[3], (E, C, H), dtype=jnp.float32) * scale, 'W3': jax.random.normal(ks[4], (E, H, C), dtype=jnp.float32) * scale}
    _L1_ffn_all = _L1_ffn_setup()
    _L1_ffn_in = {k: v for k, v in _L1_ffn_all.items() if k in ('Wg', 'W1', 'W2', 'W3')}
    del _L1_ffn_all
    return {'x': x, 'ctx_1024': ctx_1024, 'L0_attn_gamma': _L0_attn_in['gamma'], 'L0_attn_beta': _L0_attn_in['beta'], 'L0_attn_W_in': _L0_attn_in['W_in'], 'L0_attn_conv_w': _L0_attn_in['conv_w'], 'L0_attn_conv_b': _L0_attn_in['conv_b'], 'L0_attn_W_x': _L0_attn_in['W_x'], 'L0_attn_W_dt': _L0_attn_in['W_dt'], 'L0_attn_b_dt': _L0_attn_in['b_dt'], 'L0_attn_A_log': _L0_attn_in['A_log'], 'L0_attn_D_skip': _L0_attn_in['D_skip'], 'L0_attn_W_out': _L0_attn_in['W_out'], 'L0_xattn_W_out': _L0_xattn_in['W_out'], 'L0_ffn_router_W': _L0_ffn_in['router_W'], 'L0_ffn_router_b': _L0_ffn_in['router_b'], 'L0_ffn_ln_g': _L0_ffn_in['ln_g'], 'L0_ffn_ln_b': _L0_ffn_in['ln_b'], 'L0_ffn_W1': _L0_ffn_in['W1'], 'L0_ffn_b1': _L0_ffn_in['b1'], 'L0_ffn_W2': _L0_ffn_in['W2'], 'L0_ffn_b2': _L0_ffn_in['b2'], 'L1_attn_wq': _L1_attn_in['wq'], 'L1_attn_bq': _L1_attn_in['bq'], 'L1_attn_wk': _L1_attn_in['wk'], 'L1_attn_bk': _L1_attn_in['bk'], 'L1_attn_wv': _L1_attn_in['wv'], 'L1_attn_bv': _L1_attn_in['bv'], 'L1_attn_wo': _L1_attn_in['wo'], 'L1_attn_bo': _L1_attn_in['bo'], 'L1_attn_rel_emb': _L1_attn_in['rel_emb'], 'L1_attn_grep_w': _L1_attn_in['grep_w'], 'L1_attn_grep_b': _L1_attn_in['grep_b'], 'L1_attn_grep_a': _L1_attn_in['grep_a'], 'L1_xattn_w_q': _L1_xattn_in['w_q'], 'L1_xattn_w_k': _L1_xattn_in['w_k'], 'L1_xattn_w_v': _L1_xattn_in['w_v'], 'L1_xattn_w_o': _L1_xattn_in['w_o'], 'L1_ffn_Wg': _L1_ffn_in['Wg'], 'L1_ffn_W1': _L1_ffn_in['W1'], 'L1_ffn_W2': _L1_ffn_in['W2'], 'L1_ffn_W3': _L1_ffn_in['W3']}

def reference(x, ctx_1024, L0_attn_gamma, L0_attn_beta, L0_attn_W_in, L0_attn_conv_w, L0_attn_conv_b, L0_attn_W_x, L0_attn_W_dt, L0_attn_b_dt, L0_attn_A_log, L0_attn_D_skip, L0_attn_W_out, L0_xattn_W_out, L0_ffn_router_W, L0_ffn_router_b, L0_ffn_ln_g, L0_ffn_ln_b, L0_ffn_W1, L0_ffn_b1, L0_ffn_W2, L0_ffn_b2, L1_attn_wq, L1_attn_bq, L1_attn_wk, L1_attn_bk, L1_attn_wv, L1_attn_bv, L1_attn_wo, L1_attn_bo, L1_attn_rel_emb, L1_attn_grep_w, L1_attn_grep_b, L1_attn_grep_a, L1_xattn_w_q, L1_xattn_w_k, L1_xattn_w_v, L1_xattn_w_o, L1_ffn_Wg, L1_ffn_W1, L1_ffn_W2, L1_ffn_W3):
    import jax
    import jax.numpy as jnp

    def _L0_attn_ref(x, gamma, beta, W_in, conv_w, conv_b, W_x, W_dt, b_dt, A_log, D_skip, W_out):
        import jax, jax.numpy as jnp
        import numpy as np
        BATCH, SEQ, D_MODEL = (4, 512, 256)
        D_INNER, D_STATE, D_CONV, DT_RANK = (2 * D_MODEL, 16, 4, D_MODEL // 16)
        LN_EPS = 1e-05

        def _mamba_core(xn, W_in, conv_w, conv_b, W_x, W_dt, b_dt, A_log, D_skip, W_out):
            b, l, _ = xn.shape
            xz = xn @ W_in
            xi, z = jnp.split(xz, 2, axis=-1)
            xp = jnp.pad(xi, ((0, 0), (D_CONV - 1, 0), (0, 0)))
            xc = sum((xp[:, k:k + l, :] * conv_w[:, k] for k in range(D_CONV))) + conv_b
            xc = jax.nn.silu(xc)
            dbl = xc @ W_x
            dt, Bm, Cm = jnp.split(dbl, [DT_RANK, DT_RANK + D_STATE], axis=-1)
            dt = jax.nn.softplus(dt @ W_dt + b_dt)
            A = -jnp.exp(A_log)

            def step(h, inputs):
                dt_t, B_t, C_t, x_t = inputs
                h = jnp.exp(dt_t[..., None] * A) * h + (dt_t * x_t)[..., None] * B_t[:, None, :]
                y = jnp.einsum('bdn,bn->bd', h, C_t)
                return (h, y)
            h0 = jnp.zeros((b, D_INNER, D_STATE), xc.dtype)
            _, ys = jax.lax.scan(step, h0, (dt.transpose(1, 0, 2), Bm.transpose(1, 0, 2), Cm.transpose(1, 0, 2), xc.transpose(1, 0, 2)))
            y = ys.transpose(1, 0, 2) + D_skip * xc
            y = y * jax.nn.silu(z)
            return y @ W_out
        mu = x.mean(-1, keepdims=True)
        var = x.var(-1, keepdims=True)
        xn = (x - mu) * jax.lax.rsqrt(var + LN_EPS) * gamma + beta
        out = _mamba_core(xn, W_in, conv_w, conv_b, W_x, W_dt, b_dt, A_log, D_skip, W_out)
        return x + out

    def _L0_xattn_ref(q, k, v, W_out):
        import jax, jax.numpy as jnp
        import numpy as np
        B, S, D_MODEL, N_HEADS = (4, 512, 256, 16)
        HEAD_DIM = D_MODEL // N_HEADS
        scale = 1.0 / jnp.sqrt(jnp.float32(HEAD_DIM))
        scores = jnp.einsum('bqd,bkd->bqk', q, k) * scale
        attn = jax.nn.softmax(scores, axis=-1)
        out = jnp.einsum('bqk,bkd->bqd', attn, v)
        return jnp.einsum('bsd,ed->bse', out, W_out)

    def _L0_ffn_ref(x, router_W, router_b, ln_g, ln_b, W1, b1, W2, b2):
        import jax, jax.numpy as jnp
        import numpy as np
        B, S, H, E, K = (2, 512, 256, 8, 2)
        FF = 4 * H
        EPS = 1e-05
        logits = x @ router_W + router_b
        w, idx = jax.lax.top_k(logits, K)
        w = jax.nn.softmax(w, axis=-1)
        gates = jnp.einsum('bske,bsk->bse', jax.nn.one_hot(idx, E, dtype=x.dtype), w)
        mu = jnp.mean(x, axis=-1, keepdims=True)
        var = jnp.mean(jnp.square(x - mu), axis=-1, keepdims=True)
        xhat = (x - mu) * jax.lax.rsqrt(var + EPS)
        h = xhat[:, :, None, :] * ln_g + ln_b
        a = jax.nn.gelu(jnp.einsum('bseh,ehf->bsef', h, W1) + b1, approximate=False)
        y = jnp.einsum('bsef,efh->bseh', a, W2) + b2
        y = y + x[:, :, None, :]
        out = jnp.einsum('bseh,bse->bsh', y, gates)
        return out

    def _L1_attn_ref(query, wq, bq, wk, bk, wv, bv, wo, bo, rel_emb, grep_w, grep_b, grep_a):
        import jax, jax.numpy as jnp
        import numpy as np
        import math
        E = 256
        H = 16
        Dh = E // H
        B = 4
        T = 256
        NUM_BUCKETS = 80
        MAX_DIST = 200
        SCALING = Dh ** (-0.5)
        ALPHA = 32.0

        def _rel_bucket(rel):
            nb = NUM_BUCKETS // 2
            buckets = (rel > 0).astype(jnp.int32) * nb
            rel = jnp.abs(rel)
            max_exact = nb // 2
            is_small = rel < max_exact
            large = max_exact + (jnp.log(jnp.maximum(rel, 1).astype(jnp.float32) / max_exact) / math.log(MAX_DIST / max_exact) * (nb - max_exact)).astype(jnp.int32)
            large = jnp.minimum(large, nb - 1)
            return buckets + jnp.where(is_small, rel, large)
        tgt_len, bsz, _ = query.shape
        q0 = query @ wq.T + bq
        k = query @ wk.T + bk
        v = query @ wv.T + bv
        q = q0 * (SCALING / ALPHA)

        def split(x):
            return x.reshape(tgt_len, bsz, H, Dh).transpose(1, 2, 0, 3)
        qh, kh, vh = (split(q), split(k), split(v))
        aw = jnp.einsum('bhtd,bhsd->bhts', qh, kh)
        aw = (aw - aw.max(axis=-1, keepdims=True)) * ALPHA
        pos = jnp.arange(tgt_len)
        buckets = _rel_bucket(pos[None, :] - pos[:, None])
        pb = rel_emb[buckets].transpose(2, 0, 1)
        ql = split(q0)
        g = (ql @ grep_w.T + grep_b).reshape(bsz, H, tgt_len, 2, 4).sum(-1)
        g = jax.nn.sigmoid(g)
        gate_a, gate_b = (g[..., 0:1], g[..., 1:2])
        gate = gate_a * (gate_b * grep_a - 1.0) + 2.0
        aw = aw + gate * pb[None]
        probs = jax.nn.softmax(aw, axis=-1)
        attn = jnp.einsum('bhts,bhsd->bhtd', probs, vh)
        attn = attn.transpose(2, 0, 1, 3).reshape(tgt_len, bsz, E)
        return attn @ wo.T + bo

    def _L1_xattn_ref(q, k, v, w_q, w_k, w_v, w_o):
        import jax, jax.numpy as jnp
        import numpy as np
        D_MODEL = 256
        N_HEADS = 16
        D_HEAD = D_MODEL // N_HEADS
        CAUSAL = True
        B, T, _ = q.shape
        Tk = k.shape[1]
        qh = jnp.einsum('btd,ed->bte', q, w_q).reshape(B, T, N_HEADS, D_HEAD).transpose(0, 2, 1, 3)
        kh = jnp.einsum('btd,ed->bte', k, w_k).reshape(B, Tk, N_HEADS, D_HEAD).transpose(0, 2, 1, 3)
        vh = jnp.einsum('btd,ed->bte', v, w_v).reshape(B, Tk, N_HEADS, D_HEAD).transpose(0, 2, 1, 3)
        scores = jnp.einsum('bhqd,bhkd->bhqk', qh, kh) / np.sqrt(D_HEAD).astype(jnp.float32)
        if CAUSAL:
            mask = jnp.triu(jnp.ones((T, Tk), dtype=bool), k=1)
            scores = jnp.where(mask[None, None], -jnp.inf, scores)
        attn = jax.nn.softmax(scores, axis=-1)
        out = jnp.einsum('bhqk,bhkd->bhqd', attn, vh)
        out = out.transpose(0, 2, 1, 3).reshape(B, T, D_MODEL)
        return jnp.einsum('btd,ed->bte', out, w_o)

    def _L1_ffn_ref(x, Wg, W1, W2, W3):
        import jax, jax.numpy as jnp
        import numpy as np
        B, T, C, H, E = (4, 512, 256, 512, 8)
        CAPACITY_FACTOR = 1.0
        b, t, c = x.shape
        e = Wg.shape[0]
        n = b * t
        capacity = max(1, int(CAPACITY_FACTOR * n / e))
        x_flat = x.reshape(n, c)
        scores = (x_flat @ Wg.T).T
        top_vals, token_idx = jax.lax.top_k(scores, capacity)
        token_w = jax.nn.softmax(top_vals, axis=-1)
        xg = x_flat[token_idx]
        h = jax.nn.silu(jnp.einsum('eic,ehc->eih', xg, W1)) * jnp.einsum('eic,ehc->eih', xg, W3)
        y = jnp.einsum('eih,ech->eic', h, W2) * token_w[..., None]
        out = jnp.zeros_like(x_flat).at[token_idx.reshape(-1)].add(y.reshape(-1, c))
        return out.reshape(b, t, c)
    x = _layernorm(x + _L0_attn_ref(x, L0_attn_gamma, L0_attn_beta, L0_attn_W_in, L0_attn_conv_w, L0_attn_conv_b, L0_attn_W_x, L0_attn_W_dt, L0_attn_b_dt, L0_attn_A_log, L0_attn_D_skip, L0_attn_W_out), axis=-1)
    x = _layernorm(x + _L0_xattn_ref(x, ctx_1024, ctx_1024, L0_xattn_W_out), axis=-1)
    x = _layernorm(x + _L0_ffn_ref(x, L0_ffn_router_W, L0_ffn_router_b, L0_ffn_ln_g, L0_ffn_ln_b, L0_ffn_W1, L0_ffn_b1, L0_ffn_W2, L0_ffn_b2), axis=-1)
    x = _layernorm(x + _L1_attn_ref(x, L1_attn_wq, L1_attn_bq, L1_attn_wk, L1_attn_bk, L1_attn_wv, L1_attn_bv, L1_attn_wo, L1_attn_bo, L1_attn_rel_emb, L1_attn_grep_w, L1_attn_grep_b, L1_attn_grep_a), axis=-1)
    x = _layernorm(x + _L1_xattn_ref(x, ctx_1024, ctx_1024, L1_xattn_w_q, L1_xattn_w_k, L1_xattn_w_v, L1_xattn_w_o), axis=-1)
    x = _layernorm(x + _L1_ffn_ref(x, L1_ffn_Wg, L1_ffn_W1, L1_ffn_W2, L1_ffn_W3), axis=-1)
    return x

_drawn_inputs = setup_inputs


def setup_inputs(seed=0):
    import zlib

    import numpy as np

    out = dict(_drawn_inputs(seed))
    spreads = {'L0_attn_gamma': (1.0, 0.2),
     'L0_attn_beta': (0.0, 0.1),
     'L0_attn_conv_b': (0.0, 0.1),
     'L0_attn_D_skip': (1.0, 0.2),
     'L0_ffn_router_b': (0.0, 0.1),
     'L0_ffn_ln_g': (1.0, 0.2),
     'L0_ffn_ln_b': (0.0, 0.36),
     'L0_ffn_b1': (0.0, 0.353),
     'L0_ffn_b2': (0.0, 0.1),
     'L1_attn_bq': (0.0, 0.1),
     'L1_attn_bk': (0.0, 0.1),
     'L1_attn_bv': (0.0, 0.279),
     'L1_attn_bo': (0.0, 0.1),
     'L1_attn_grep_b': (0.0, 0.1),
     'L1_attn_grep_a': (1.0, 0.2)}
    factors = {'L1_ffn_Wg': 8.0, 'L1_ffn_W1': 8.0, 'L1_ffn_W2': 8.0, 'L1_ffn_W3': 8.0}
    for name, (base, spread) in spreads.items():
        noise = np.random.default_rng([zlib.crc32(name.encode()), seed]).standard_normal(out[name].shape)
        drawn = base * np.exp(spread * noise) if base else spread * noise
        out[name] = jnp.asarray(drawn.astype(out[name].dtype))
    for name, factor in factors.items():
        out[name] = (out[name] * factor).astype(out[name].dtype)
    return out
```

```python
from contextlib import ExitStack, contextmanager

import concourse.bass as bass
import numpy as np
from concourse import mybir

F32 = mybir.dt.float32
BF16 = mybir.dt.bfloat16
I32 = mybir.dt.int32
U32 = mybir.dt.uint32
ALU = mybir.AluOpType
ACT = mybir.ActivationFunctionType
AX_X = mybir.AxisListType.X

P = 128
S = 2048
D = 256
DB = D // P
TILES = S // P
GT = 4
GS = GT * P
GROUPS = S // GS
EPS = 1e-5


@contextmanager
def semaphores(nc, name):
    taken = []

    def sem(n):
        taken.append(nc.alloc_semaphore(f"{name}_{n}"))
        return taken[-1]

    yield sem
    nc.clear_and_free_semaphores(taken)
    nc.all_engine_barrier()


def make_identity(nc, keep):
    zeroed = keep.enter_context(nc.semaphore("ident_zeroed"))
    built = keep.enter_context(nc.semaphore("ident_built"))
    ident = keep.enter_context(nc.sbuf_tensor("ident", [P, P], F32))
    eps = keep.enter_context(nc.sbuf_tensor("eps", [P, 1], F32))
    with nc.Block() as block:
        @block.gpsimd
        def _(pool):
            nc.gpsimd.memset(ident[:], 0.0).then_inc(zeroed, 1)
            pool.wait_ge(zeroed, 1)
            nc.gpsimd.affine_select(out=ident[:], in_=ident[:], compare_op=ALU.not_equal, fill=1.0,
                                    base=0, pattern=[[-1, P]], channel_multiplier=1).then_inc(built, 1)
            nc.gpsimd.memset(eps[:], EPS).then_inc(built, 1)
            pool.wait_ge(built, 2)
    return ident, built, eps


def normalise(nc, name, X, xT, ident, hat=None, affine=None):
    ident, ident_built, eps = ident
    H = 2
    with ExitStack() as ctx:
        def sb(n, shape, dt=F32):
            return ctx.enter_context(nc.sbuf_tensor(f"{name}_{n}", shape, dt))

        sem = ctx.enter_context(semaphores(nc, name))
        turned = [ctx.enter_context(nc.psum_tensor(f"{name}_turned{h}", [P, DB, GS], F32)) for h in range(H)]
        normed = [sb(f"normed{h}", [P, GT, D]) for h in range(H)]
        stats = sb("stats", [P, TILES, 6])
        mean2, diff, spread, diff2, spread1, var, root, rstd, shift = (
            sb(n, [P, TILES]) for n in ("mean2", "diff", "spread", "diff2", "spread1", "var", "root", "rstd", "shift"))
        stats_ready, small, root_ready, shift_ready = sem("stats_ready"), sem("small"), sem("root_ready"), sem("shift_ready")
        normed_by_act, normed_by_dve = sem("normed_by_act"), sem("normed_by_dve")
        turned_ready, X_written, xT_written = sem("turned_ready"), sem("X_written"), sem("xT_written")

        with nc.Block() as block:
            @block.vector
            def _(dve):
                with dve.Fori(0, GROUPS) as g:
                    for t in range(GT):
                        nc.vector.bn_stats(stats[:, bass.ds(g * GT + t, 1), :].rearrange("p a b -> p (a b)"),
                                           X[:, bass.ds(g * GT + t, 1), :].rearrange("p a b -> p (a b)")).then_inc(stats_ready, 1)
                dve.wait_ge(stats_ready, TILES)
                nc.vector.tensor_tensor(mean2[:], stats[:, :, 1], stats[:, :, 4], ALU.add).then_inc(small, 1)
                nc.vector.tensor_tensor(diff[:], stats[:, :, 1], stats[:, :, 4], ALU.subtract).then_inc(small, 1)
                nc.vector.tensor_tensor(spread[:], stats[:, :, 2], stats[:, :, 5], ALU.add).then_inc(small, 1)
                dve.wait_ge(small, 3)
                nc.vector.tensor_tensor(diff2[:], diff[:], diff[:], ALU.mult).then_inc(small, 1)
                nc.vector.tensor_scalar(spread1[:], spread[:], 1.0 / D, None, ALU.mult).then_inc(small, 1)
                dve.wait_ge(small, 5)
                nc.vector.scalar_tensor_tensor(out=var[:], in0=diff2[:], scalar=0.25, in1=spread1[:], op0=ALU.mult,
                                               op1=ALU.add).then_inc(small, 1)
                dve.wait_ge(root_ready, 1)
                nc.vector.reciprocal(rstd[:], root[:]).then_inc(small, 1)
                dve.wait_ge(small, 7)
                nc.vector.scalar_tensor_tensor(out=shift[:], in0=mean2[:], scalar=-0.5, in1=rstd[:],
                                               op0=ALU.mult, op1=ALU.mult).then_inc(shift_ready, 1)
                dve.wait_ge(shift_ready, 1)
                with dve.Fori(0, GROUPS // H) as i:
                    for h in range(H):
                        for t in range(GT // 2, GT):
                            tile = bass.ds((i * H + h) * GT + t, 1)
                            to = normed[h][:, t, :] if hat is None else hat[:, tile, :].rearrange("p a b -> p (a b)")
                            nc.vector.tensor_scalar(to, X[:, tile, :].rearrange("p a b -> p (a b)"),
                                                    rstd[:, tile], shift[:, tile], ALU.mult, ALU.add).then_inc(normed_by_dve, 1)
                    if hat is None:
                        dve.wait_ge(turned_ready, i * H + H)
                    if hat is None and affine is None:
                        dve.wait_ge(X_written, i * H + H)
                dve.wait_ge(normed_by_dve, TILES // 2)

            @block.scalar
            def _(act):
                act.wait_ge(small, 6)
                nc.scalar.activation(root[:], var[:], ACT.Sqrt, bias=eps[:]).then_inc(root_ready, 1)
                act.wait_ge(shift_ready, 1)
                with act.Fori(0, GROUPS // H) as i:
                    for h in range(H):
                        for t in range(GT // 2):
                            tile = bass.ds((i * H + h) * GT + t, 1)
                            to = normed[h][:, t, :] if hat is None else hat[:, tile, :].rearrange("p a b -> p (a b)")
                            nc.scalar.activation(to, X[:, tile, :].rearrange("p a b -> p (a b)"), ACT.Identity,
                                                 bias=shift[:, tile], scale=rstd[:, tile]).then_inc(normed_by_act, 1)
                    for h in range(H if hat is None else 0):
                        act.wait_ge(turned_ready, i * H + (h + 1))
                        if affine is None:
                            nc.scalar.activation(xT[:, :, bass.ds((i * H + h) * GS, GS)], turned[h][:], ACT.Identity).then_inc(xT_written, 1)
                        else:
                            for b in range(DB):
                                last = nc.scalar.activation(xT[:, b, bass.ds((i * H + h) * GS, GS)], turned[h][:, b, :], ACT.Identity,
                                                            bias=affine[1][:, b:b + 1], scale=affine[0][:, b:b + 1])
                            last.then_inc(xT_written, 1)
                    if hat is None and affine is None:
                        act.wait_ge(X_written, i * H + H)
                act.wait_ge(normed_by_act, TILES // 2)

            if hat is not None:
                return

            @block.tensor
            def _(pe):
                with pe.Fori(0, GROUPS // H) as i:
                    for h in range(H):
                        pe.wait_ge(normed_by_act, (i * H + (h + 1)) * (GT // 2))
                        pe.wait_ge(normed_by_dve, (i * H + (h + 1)) * (GT // 2))
                        for f in range(DB):
                            for t in range(GT):
                                last = nc.tensor.transpose(turned[h][:, f, t * P:(t + 1) * P],
                                                           normed[h][:, t, f * P:(f + 1) * P], ident[:])
                        last.then_inc(turned_ready, 1)
                    pe.wait_ge(xT_written, i * H + H)

            if affine is not None:
                return

            @block.gpsimd
            def _(pool):
                with pool.Fori(0, GROUPS // H) as i:
                    for h in range(H):
                        pool.wait_ge(normed_by_act, (i * H + (h + 1)) * (GT // 2))
                        pool.wait_ge(normed_by_dve, (i * H + (h + 1)) * (GT // 2))
                        nc.gpsimd.tensor_copy(X[:, bass.ds((i * H + h) * GT, GT), :], normed[h][:]).then_inc(X_written, 1)
                pool.wait_ge(X_written, GROUPS)


def state_space(nc, X, xT, constants, w):
    ident = constants[0]
    DI = w["W_out"].shape[1] * P
    IB = DI // P
    NS = w["A_log"].shape[-1]
    TAPS = w["conv_w"].shape[-1]
    RANK = w["W_dt"].shape[0]
    C = 1024
    CHUNKS = S // C
    spread_dram = nc.dram_tensor("mamba_spread", [2 * NS, S], F32).ap()

    with ExitStack() as outer:
        def keep(n, shape, dt=F32):
            return outer.enter_context(nc.sbuf_tensor(f"mamba_{n}", shape, dt))

        inner = keep("inner", [P, IB, S + TAPS - 1])
        x = keep("x", [P, IB, S])
        dt = keep("dt", [P, IB, S])
        w_out = keep("w_out", [P, IB, D])
        w_gate = keep("w_gate", [P, DB, DI])
        gamma, beta = keep("gamma", [P, DB]), keep("beta", [P, DB])
        conv_w, conv_b, b_dt, skip = keep("conv_w", [P, IB, TAPS]), keep("conv_b", [P, IB]), keep("b_dt", [P, IB]), keep("skip", [P, IB])
        a_log = keep("a_log", [P, IB, NS])
        rate = keep("rate", [P, IB, NS])
        diag = keep("diag", [P, IB, P])
        wide_loaded = outer.enter_context(nc.semaphore("mamba_wide_loaded"))
        params = outer.enter_context(nc.semaphore("mamba_params"))
        x_loaded = outer.enter_context(nc.semaphore("mamba_x_loaded"))
        PARAMS = 7
        dtx = inner[:, :, TAPS - 1:]
        y = dtx

        with nc.Block() as block:
            @block.sync
            def _(sp):
                for to, what in ((gamma, "gamma"), (beta, "beta"), (conv_w, "conv_w"), (conv_b, "conv_b"), (b_dt, "b_dt"),
                                 (skip, "D_skip"), (a_log, "A_log")):
                    sp.dma_start(to[:], w[what]).then_inc(params, 16)
                sp.dma_start(w_out[:], w["W_out"]).then_inc(wide_loaded, 16)
                sp.dma_start(w_gate[:], w["W_in"][:, :, DI:2 * DI]).then_inc(wide_loaded, 16)
                sp.wait_ge(params, PARAMS * 16)

        normalise(nc, "mamba_norm", X, xT, constants, affine=(gamma, beta))

        with ExitStack() as ctx:
            def sb(n, shape, dt_=F32):
                return ctx.enter_context(nc.sbuf_tensor(f"mamba_{n}", shape, dt_))

            sem = ctx.enter_context(semaphores(nc, "mamba"))

            w_in = sb("w_in", [P, DB, DI])
            w_x = sb("w_x", [P, IB, RANK + 2 * NS])
            w_dt = sb("w_dt", [RANK, DI])
            small = sb("small", [RANK + 2 * NS, S])
            ps = ctx.enter_context(nc.psum_tensor("mamba_ps", [P, 8, 512], F32))
            w_loaded, inner_ps, inner_kept, padded, conv_done, convolved, x_ready, a_ready, rate_ready = (
                sem(n) for n in ("w_loaded", "inner_ps", "inner_kept", "padded", "conv_done", "convolved", "x_ready", "a_ready", "rate_ready"))
            small_ps, small_kept, small_stored, dt_ps, positive, lengthened, magnitude, logged, dt_ready, dtx_ready = (
                sem(n) for n in ("small_ps", "small_kept", "small_stored", "dt_ps", "positive", "lengthened", "magnitude", "logged", "dt_ready", "dtx_ready"))

            with nc.Block() as block:
                @block.sync
                def _(sp):
                    for to, what in ((w_in[:], w["W_in"][:, :, 0:DI]), (w_x[:], w["W_x"]), (w_dt[:], w["W_dt"])):
                        sp.dma_start(to, what).then_inc(w_loaded, 16)
                    sp.wait_ge(small_kept, GROUPS)
                    sp.dma_start(spread_dram, small[RANK:, :]).then_inc(small_stored, 16)
                    sp.wait_ge(small_stored, 16)

                @block.tensor
                def _(pe):
                    pe.wait_ge(w_loaded, 48)
                    with pe.Fori(0, GROUPS // 2) as i:
                        for h in range(2):
                            for m in range(IB):
                                for b in range(DB):
                                    last = nc.tensor.matmul(ps[:, h * IB + m, :], w_in[:, b, m * P:(m + 1) * P],
                                                            xT[:, b, bass.ds((i * 2 + h) * GS, GS)], start=(b == 0), stop=(b == DB - 1))
                            last.then_inc(inner_ps, 1)
                        pe.wait_ge(inner_kept, i * 2 + 2)
                    for m in range(IB):
                        pe.wait_ge(x_ready, m + 1)
                        for g in range(GROUPS):
                            last = nc.tensor.matmul(ps[0:RANK + 2 * NS, g, :], w_x[:, m, :], x[:, m, g * GS:(g + 1) * GS],
                                                    start=(m == 0), stop=(m == IB - 1))
                    last.then_inc(small_ps, 1)
                    for m in range(IB):
                        half = 4 * ((m + 1) % 2)
                        if m == 0:
                            pe.wait_ge(small_kept, GROUPS)
                        if m >= 2:
                            pe.wait_ge(positive, m - 1)
                            pe.wait_ge(magnitude, m - 1)
                        for g in range(GROUPS):
                            last = nc.tensor.matmul(ps[:, half + g, :], w_dt[:, m * P:(m + 1) * P], small[0:RANK, g * GS:(g + 1) * GS],
                                                    start=True, stop=True)
                        last.then_inc(dt_ps, 1)

                @block.scalar
                def _(act):
                    with act.Fori(0, GROUPS // 2) as i:
                        for h in range(2):
                            act.wait_ge(inner_ps, i * 2 + (h + 1))
                            nc.scalar.activation(inner[:, :, bass.ds((i * 2 + h) * GS + (TAPS - 1), GS)], ps[:, h * IB:(h + 1) * IB, :],
                                                 ACT.Identity).then_inc(inner_kept, 1)
                    for m in range(IB):
                        act.wait_ge(convolved, m + 1)
                        nc.scalar.activation(x[:, m, :], dt[:, m, :], ACT.Silu, bias=conv_b[:, m:m + 1]).then_inc(x_ready, 1)
                    act.wait_ge(small_ps, 1)
                    for g in range(GROUPS):
                        nc.scalar.activation(small[:, g * GS:(g + 1) * GS], ps[0:RANK + 2 * NS, g, :], ACT.Identity).then_inc(small_kept, 1)
                    for m in range(IB):
                        half = 4 * ((m + 1) % 2)
                        act.wait_ge(positive, m + 1)
                        nc.scalar.activation(dt[:, m, :], ps[:, half:half + 4, :].rearrange("p a b -> p (a b)"), ACT.Abs,
                                             bias=b_dt[:, m:m + 1]).then_inc(magnitude, 1)
                    act.wait_ge(magnitude, IB)
                    nc.scalar.activation(dt[:], dt[:], ACT.Exp, scale=-1.0).then_inc(a_ready, 1)
                    nc.scalar.activation(rate[:], a_log[:], ACT.Exp).then_inc(rate_ready, 1)
                    act.wait_ge(a_ready, 1)
                    nc.scalar.activation(dt[:], dt[:], ACT.Ln, bias=1.0).then_inc(logged, 1)

                @block.vector
                def _(dve):
                    nc.vector.memset(inner[:, :, 0:TAPS - 1], 0.0).then_inc(padded, 1)
                    dve.wait_ge(padded, 1)
                    dve.wait_ge(inner_kept, GROUPS)
                    for m in range(IB):
                        nc.vector.tensor_scalar(diag[:, m, :], ident[:], skip[:, m:m + 1], None, ALU.mult).then_inc(padded, 1)
                        nc.vector.tensor_scalar(dt[:, m, :], inner[:, m, 0:S], conv_w[:, m, 0:1], None, ALU.mult).then_inc(conv_done, 1)
                        for k in range(1, TAPS):
                            dve.wait_ge(conv_done, m * (TAPS - 1) + k)
                            nc.vector.scalar_tensor_tensor(out=dt[:, m, :], in0=inner[:, m, k:k + S], scalar=conv_w[:, m, k:k + 1],
                                                           in1=dt[:, m, :], op0=ALU.mult, op1=ALU.add).then_inc(
                                                               convolved if k == TAPS - 1 else conv_done, 1)
                    for m in range(IB):
                        half = 4 * ((m + 1) % 2)
                        dve.wait_ge(dt_ps, m + 1)
                        nc.vector.tensor_scalar(dtx[:, m, :], ps[:, half:half + 4, :].rearrange("p a b -> p (a b)"), b_dt[:, m:m + 1], 0.0,
                                                ALU.add, ALU.max).then_inc(positive, 1)
                    dve.wait_ge(rate_ready, 1)
                    nc.vector.tensor_scalar(rate[:], rate[:], -1.0, None, ALU.mult).then_inc(rate_ready, 1)
                    dve.wait_ge(logged, 1)
                    dve.wait_ge(positive, IB)
                    for m in range(IB):
                        nc.vector.tensor_tensor(dt[:, m, :], dt[:, m, :], dtx[:, m, :], ALU.add).then_inc(dt_ready, 1)
                    for m in range(IB):
                        dve.wait_ge(dt_ready, m + 1)
                        nc.vector.tensor_tensor(dtx[:, m, :], dt[:, m, :], x[:, m, :], ALU.mult).then_inc(dtx_ready, 1)
                    dve.wait_ge(dtx_ready, IB)

        with ExitStack() as ctx:
            def sb(n, shape, dt_=F32):
                return ctx.enter_context(nc.sbuf_tensor(f"mamba_{n}", shape, dt_))

            sem = ctx.enter_context(semaphores(nc, "mamba"))

            decay = [sb(f"decay{h}", [P, C]) for h in range(2)]
            drive = [sb(f"drive{h}", [P, C]) for h in range(2)]
            state = [sb(f"state{h}", [P, C]) for h in range(2)]
            read = [sb(f"read{h}", [P, C]) for h in range(2)]
            b_all = [sb(f"b_all{h}", [P, C]) for h in range(2)]
            c_all = [sb(f"c_all{h}", [P, C]) for h in range(2)]
            carry = sb("carry", [P, NS, IB])
            y_ps = ctx.enter_context(nc.psum_tensor("mamba_y_ps", [P, IB, C], F32))
            b_loaded = [sem(f"b_loaded{h}") for h in range(2)]
            c_loaded = [sem(f"c_loaded{h}") for h in range(2)]
            decay_ready, drive_dve, drive_pool, state_ready, read_ready, summed, carry_zeroed, carried, y_kept = (
                sem(n) for n in ("decay_ready", "drive_dve", "drive_pool", "state_ready", "read_ready", "summed", "carry_zeroed", "carried",
                                 "y_kept"))
            PER = NS * IB
            BY_DVE = IB - 1

            def states(eng, c, body):
                with eng.Fori(0, NS // 2) as i:
                    for h in range(2):
                        body(i * 2 + h, h, i)

            with nc.Block() as block:
                @block.sync
                def _(sp):
                    def load(c, state_no, h):
                        cols = slice(c * C, (c + 1) * C)
                        sp.dma_start(b_all[h][:], spread_dram[bass.ds(state_no, 1), cols].broadcast_to([P, C])).then_inc(b_loaded[h], 16)
                        sp.dma_start(c_all[h][:], spread_dram[bass.ds(state_no + NS, 1), cols].broadcast_to([P, C])).then_inc(c_loaded[h], 16)
                    for c in range(CHUNKS):
                        for h in range(2):
                            if c:
                                sp.wait_ge(read_ready, c * PER - (1 - h) * IB + 2)
                            load(c, h, h)
                        with sp.Fori(0, NS // 2 - 1) as i:
                            for h in range(2):
                                sp.wait_ge(read_ready, i * (2 * IB) + (c * PER + (h + 1) * IB + 2))
                                load(c, i * 2 + (h + 2), h)

                @block.tensor
                def _(pe):
                    pe.sem_inc(summed, 2)
                    for c in range(CHUNKS):
                        for m in range(IB):
                            if c:
                                pe.wait_ge(y_kept, (c - 1) * IB + m + 1)
                            for q in range(C // 512):
                                nc.tensor.matmul(y_ps[:, m, q * 512:(q + 1) * 512], diag[:, m, :], x[:, m, c * C + q * 512:c * C + (q + 1) * 512],
                                                 start=True, stop=False, skip_group_check=True)

                        def body(state_no, h, i):
                            for m in range(IB):
                                pe.wait_ge(read_ready, state_no * IB + (c * PER + m + 1 + 2))
                                for q in range(C // 512):
                                    last = nc.tensor.matmul(y_ps[:, m, q * 512:(q + 1) * 512], ident[:], read[m % 2][:, q * 512:(q + 1) * 512],
                                                            start=False, stop=False, skip_group_check=True)
                                last.then_inc(summed, 1)
                        states(pe, c, body)

                @block.scalar
                def _(act):
                    for c in range(CHUNKS):
                        def body(state_no, h, i):
                            for m in range(IB):
                                act.wait_ge(state_ready, state_no * IB + (c * PER + m + 1))
                                nc.scalar.activation(decay[m % 2][:], dt[:, m, c * C:(c + 1) * C], ACT.Exp,
                                                     scale=rate[:, m, bass.ds(state_no, 1)]).then_inc(decay_ready, 1)
                        states(act, c, body)
                        for m in range(IB):
                            act.wait_ge(summed, (c + 1) * PER - IB + m + 1 + 2)
                            nc.scalar.activation(y[:, m, c * C:(c + 1) * C], y_ps[:, m, :], ACT.Identity).then_inc(y_kept, 1)
                    act.wait_ge(y_kept, CHUNKS * IB)

                @block.vector
                def _(dve):
                    dve.sem_inc(state_ready, 2)
                    nc.vector.memset(carry[:], 0.0).then_inc(carry_zeroed, 1)
                    dve.wait_ge(carry_zeroed, 1)
                    for c in range(CHUNKS):
                        def body(state_no, h, i):
                            def drive_of(m):
                                dve.wait_ge(state_ready, state_no * IB + (c * PER + m + 1))
                                nc.vector.tensor_tensor(drive[m % 2][:], dtx[:, m, c * C:(c + 1) * C], b_all[h][:], ALU.mult).then_inc(drive_dve, 1)

                            def scan(m):
                                if m < BY_DVE:
                                    dve.wait_ge(drive_dve, state_no * BY_DVE + (c * NS * BY_DVE + m + 1))
                                else:
                                    dve.wait_ge(drive_pool, state_no + (c * NS + 1))
                                dve.wait_ge(decay_ready, state_no * IB + (c * PER + m + 1))
                                dve.wait_ge(read_ready, state_no * IB + (c * PER + m + 1))
                                if c == 0:
                                    dve.wait_ge(carried, state_no * IB + (m + 1))
                                nc.vector.tensor_tensor_scan(state[m % 2][:], decay[m % 2][:], drive[m % 2][:],
                                                             carry[:, bass.ds(state_no, 1), m], ALU.mult, ALU.add).then_inc(state_ready, 1)

                            dve.wait_ge(b_loaded[h], i * 16 + (c * (NS // 2) * 16 + 16))
                            drive_of(0)
                            drive_of(1)
                            scan(0)
                            drive_of(2)
                            scan(1)
                            scan(2)
                            scan(3)
                        if c:
                            dve.wait_ge(carried, 2 + PER)
                        states(dve, c, body)

                @block.gpsimd
                def _(pool):
                    pool.sem_inc(read_ready, 2)
                    pool.sem_inc(carried, 2)
                    for c in range(CHUNKS):
                        def body(state_no, h, i):
                            pool.wait_ge(b_loaded[h], i * 16 + (c * (NS // 2) * 16 + 16))
                            pool.wait_ge(c_loaded[h], i * 16 + (c * (NS // 2) * 16 + 16))
                            for m in range(IB):
                                if m == IB - 2:
                                    pool.wait_ge(state_ready, state_no * IB + (c * PER + BY_DVE + 1))
                                    nc.gpsimd.tensor_tensor(drive[BY_DVE % 2][:], dtx[:, BY_DVE, c * C:(c + 1) * C], b_all[h][:],
                                                            ALU.mult).then_inc(drive_pool, 1)
                                pool.wait_ge(state_ready, state_no * IB + (c * PER + m + 1 + 2))
                                if c == 0:
                                    nc.gpsimd.tensor_copy(carry[:, bass.ds(state_no, 1), m], state[m % 2][:, C - 1:C]).then_inc(carried, 1)
                                pool.wait_ge(summed, state_no * IB + (c * PER + m + 1))
                                nc.gpsimd.tensor_tensor(read[m % 2][:], state[m % 2][:], c_all[h][:], ALU.mult).then_inc(read_ready, 1)
                        states(pool, c, body)

        with ExitStack() as ctx:
            def sb(n, shape, dt_=F32):
                return ctx.enter_context(nc.sbuf_tensor(f"mamba_{n}", shape, dt_))

            sem = ctx.enter_context(semaphores(nc, "mamba"))

            gate = [sb(f"gate{h}", [P, GS]) for h in range(2)]
            gated = [sb(f"gated{h}", [P, IB, GS]) for h in range(2)]
            gate_ps = [ctx.enter_context(nc.psum_tensor(f"mamba_gate_ps{h}", [P, GS], F32)) for h in range(2)]
            out_ps = [ctx.enter_context(nc.psum_tensor(f"mamba_out_ps{h}", [P, GT, D], F32)) for h in range(2)]
            gate_ready, gate_kept, gated_ready, out_ready, X_ready = (
                sem(n) for n in ("gate_ready", "gate_kept", "gated_ready", "out_ready", "X_ready"))

            with nc.Block() as block:
                @block.tensor
                def _(pe):
                    pe.wait_ge(wide_loaded, 32)
                    pe.sem_inc(gate_ready, 2)
                    with pe.Fori(0, GROUPS // 2) as i:
                        for h in range(2):
                            g = i * 2 + h
                            for m in range(IB):
                                pe.wait_ge(gate_kept, g * IB + (m + 1))
                                for b in range(DB):
                                    last = nc.tensor.matmul(gate_ps[m % 2][:], w_gate[:, b, m * P:(m + 1) * P], xT[:, b, bass.ds(g * GS, GS)],
                                                            start=(b == 0), stop=(b == DB - 1))
                                last.then_inc(gate_ready, 1)
                            pe.wait_ge(gated_ready, g * IB + (IB + 2))
                            for t in range(GT):
                                for m in range(IB):
                                    last = nc.tensor.matmul(out_ps[h][:, t, :], gated[h][:, m, t * P:(t + 1) * P], w_out[:, m, :],
                                                            start=(m == 0), stop=(m == IB - 1))
                            last.then_inc(out_ready, 1)
                        pe.wait_ge(X_ready, i * 2 + 2)

                @block.scalar
                def _(act):
                    act.sem_inc(gate_kept, 2)
                    with act.Fori(0, GROUPS // 2) as i:
                        for h in range(2):
                            g = i * 2 + h
                            for m in range(IB):
                                act.wait_ge(gate_ready, g * IB + (m + 1 + 2))
                                act.wait_ge(gated_ready, g * IB + (m + 1))
                                nc.scalar.activation(gate[m % 2][:], gate_ps[m % 2][:], ACT.Silu).then_inc(gate_kept, 1)

                @block.vector
                def _(dve):
                    dve.sem_inc(gated_ready, 2)
                    with dve.Fori(0, GROUPS // 2) as i:
                        for h in range(2):
                            g = i * 2 + h
                            for m in range(IB):
                                dve.wait_ge(gate_kept, g * IB + (m + 1 + 2))
                                nc.vector.tensor_tensor(gated[h][:, m, :], y[:, m, bass.ds(g * GS, GS)], gate[m % 2][:], ALU.mult).then_inc(gated_ready, 1)
                        for h in range(2):
                            g = i * 2 + h
                            dve.wait_ge(out_ready, g + 1)
                            x_g = X[:, bass.ds(g * GT, GT), :].rearrange("p a b -> p (a b)")
                            nc.vector.scalar_tensor_tensor(out=x_g, in0=x_g, scalar=2.0, in1=out_ps[h][:].rearrange("p a b -> p (a b)"),
                                                           op0=ALU.mult, op1=ALU.add).then_inc(X_ready, 1)
                    dve.wait_ge(X_ready, GROUPS)


def attend_context(nc, X, xT, ident, contextT, w_outT):
    ident = ident[0]
    SCALE = float(D // 16) ** -0.5
    K = contextT.shape[-1]
    KT = -(-K // P)
    sizes = [min(P, K - P * k) for k in range(KT)]
    CT = 4
    chunks = [range(c, min(c + CT, KT)) for c in range(0, KT, CT)]
    BY_ACT = [c for c in range(len(chunks)) if c % 2 == 0]
    BY_DVE = [c for c in range(len(chunks)) if c % 2]
    VT = 8
    with ExitStack() as ctx:
        def sb(n, shape, dt=F32):
            return ctx.enter_context(nc.sbuf_tensor(f"ctx_{n}", shape, dt))

        sem = ctx.enter_context(semaphores(nc, "ctx"))

        keysT = sb("keysT", [P, DB, K])
        wo = sb("wo", [P, DB, D])
        values = sb("values", [P, KT, D])
        query = [sb(f"query{h}", [P, DB, P]) for h in range(2)]
        probs = [sb(f"probs{h}", [P, K]) for h in range(2)]
        probsT = [sb(f"probsT{h}", [P, KT, P]) for h in range(2)]
        top = [sb(f"top{h}", [P, 1]) for h in range(2)]
        negtop = [sb(f"negtop{h}", [P, 1]) for h in range(2)]
        total = [sb(f"total{h}", [P, 1]) for h in range(2)]
        share = [sb(f"share{h}", [P, 1]) for h in range(2)]
        scores = ctx.enter_context(nc.psum_tensor("ctx_scores", [P, 4 * 512], F32))
        turned = [ctx.enter_context(nc.psum_tensor(f"ctx_turned{h}", [P, CT, P], F32)) for h in range(2)]
        mixed = [ctx.enter_context(nc.psum_tensor(f"ctx_mixed{h}", [P, 512], F32)) for h in range(2)]
        loaded, values_ready, values_kept = sem("loaded"), sem("values_ready"), sem("values_kept")
        query_ready, scores_ready, top_ready, negtop_ready = sem("query_ready"), sem("scores_ready"), sem("top_ready"), sem("negtop_ready")
        probs_ready, turned_ready, kept_by_act, kept_by_dve = sem("probs_ready"), sem("turned_ready"), sem("kept_by_act"), sem("kept_by_dve")
        mixed_ready, share_ready, added = sem("mixed_ready"), sem("share_ready"), sem("added")
        NC = len(chunks)

        def steps(eng, step):
            with eng.Fori(0, TILES // 2 - 1) as i:
                for h in range(2):
                    step(i * 2 + h, h, True)
            step(TILES - 2, 0, True)
            step(TILES - 1, 1, False)

        with nc.Block() as block:
            @block.sync
            def _(sp):
                sp.dma_start(keysT[:], contextT).then_inc(loaded, 16)
                sp.dma_start(wo[:], w_outT).then_inc(loaded, 16)
                sp.wait_ge(loaded, 32)

            @block.gpsimd
            def _(pool):
                for h in range(2):
                    nc.gpsimd.tensor_copy(query[h][:], xT[:, :, h * P:(h + 1) * P]).then_inc(query_ready, 1)
                with pool.Fori(0, TILES // 2 - 1) as i:
                    for h in range(2):
                        pool.wait_ge(scores_ready, i * 2 + (h + 1))
                        nc.gpsimd.tensor_copy(query[h][:], xT[:, :, bass.ds((i * 2 + (h + 2)) * P, P)]).then_inc(query_ready, 1)

            @block.tensor
            def _(pe):
                def score(k, h, part):
                    if part == 0:
                        pe.wait_ge(query_ready, k + 1)
                    for c in range(0, K, 512)[2 * part:2 * part + 2]:
                        n = min(512, K - c)
                        for b in range(DB):
                            last = nc.tensor.matmul(scores[:, c:c + n], query[h][:, b, :], keysT[:, b, c:c + n],
                                                    start=(b == 0), stop=(b == DB - 1))
                    if part == 1:
                        last.then_inc(scores_ready, 1)

                def turn(k, h, c):
                    if c >= 2:
                        if c % 2 == 0:
                            pe.wait_ge(kept_by_act, k * len(BY_ACT) + c // 2)
                        else:
                            pe.wait_ge(kept_by_dve, k * len(BY_DVE) + c // 2)
                    for t, kt in enumerate(chunks[c]):
                        last = nc.tensor.transpose(turned[c % 2][0:sizes[kt], t, :], probs[h][:, kt * P:kt * P + sizes[kt]], ident[:])
                    last.then_inc(turned_ready, 1)

                def mix(k, h, c):
                    if c % 2 == 0:
                        pe.wait_ge(kept_by_act, k * len(BY_ACT) + (c // 2 + 1))
                    else:
                        pe.wait_ge(kept_by_dve, k * len(BY_DVE) + (c // 2 + 1))
                    for kt in chunks[c]:
                        last = nc.tensor.matmul(mixed[h][:, 0:D], probsT[h][0:sizes[kt], kt, :], values[0:sizes[kt], kt, :],
                                                start=(kt == 0), stop=(kt == KT - 1))
                    if c == NC - 1:
                        last.then_inc(mixed_ready, 1)

                def step(k, h, more):
                    pe.wait_ge(probs_ready, k + 1)
                    turn(k, h, 0)
                    turn(k, h, 1)
                    if more:
                        score(k + 1, 1 - h, 0)
                    turn(k, h, 2)
                    turn(k, h, 3)
                    if more:
                        score(k + 1, 1 - h, 1)
                    for c in range(NC):
                        mix(k, h, c)

                pe.wait_ge(loaded, 32)
                for v in range(0, KT, VT):
                    if v:
                        pe.wait_ge(values_kept, 1)
                    for kt in range(v, min(v + VT, KT)):
                        for b in range(DB):
                            last = nc.tensor.matmul(scores[0:sizes[kt], (kt - v) * D:(kt - v + 1) * D],
                                                    keysT[:, b, kt * P:kt * P + sizes[kt]], wo[:, b, :],
                                                    start=(b == 0), stop=(b == DB - 1))
                    last.then_inc(values_ready, 1)
                pe.wait_ge(values_kept, 3)
                score(0, 0, 0)
                score(0, 0, 1)
                steps(pe, step)

            @block.vector
            def _(dve):
                def maximum(k, h):
                    dve.wait_ge(scores_ready, k + 1)
                    nc.vector.reduce_max(top[h][:], scores[:, 0:K], AX_X).then_inc(top_ready, 1)
                    dve.wait_ge(top_ready, k + 1)
                    nc.vector.tensor_scalar(negtop[h][:], top[h][:], -SCALE, None, ALU.mult).then_inc(negtop_ready, 1)

                def step(k, h, more):
                    for c in BY_DVE:
                        dve.wait_ge(turned_ready, k * NC + (c + 1))
                        n = len(chunks[c])
                        r = sizes[chunks[c][-1]] if n == 1 else P
                        nc.vector.tensor_copy(probsT[h][0:r, chunks[c][0]:chunks[c][0] + n, :],
                                              turned[c % 2][0:r, 0:n, :]).then_inc(kept_by_dve, 1)
                    if more:
                        maximum(k + 1, 1 - h)
                    dve.wait_ge(probs_ready, k + 1)
                    nc.vector.reciprocal(share[h][:], total[h][:]).then_inc(share_ready, 1)
                    dve.wait_ge(share_ready, k + 1)
                    dve.wait_ge(mixed_ready, k + 1)
                    x = X[:, bass.ds(k, 1), :].rearrange("p a b -> p (a b)")
                    nc.vector.scalar_tensor_tensor(out=x, in0=mixed[h][:, 0:D], scalar=share[h][:], in1=x,
                                                   op0=ALU.mult, op1=ALU.add).then_inc(added, 1)

                dve.wait_ge(values_ready, 1)
                nc.vector.tensor_copy(values[:, 0:VT, :].rearrange("p a b -> p (a b)"), scores[:]).then_inc(values_kept, 1)
                maximum(0, 0)
                steps(dve, step)
                dve.wait_ge(added, TILES)

            @block.scalar
            def _(act):
                act.wait_ge(values_ready, 2)
                nc.scalar.activation(values[:, VT:KT - 1, :].rearrange("p a b -> p (a b)"), scores[:, 0:(KT - 1 - VT) * D],
                                     ACT.Identity).then_inc(values_kept, 1)
                nc.scalar.activation(values[0:sizes[-1], KT - 1, :], scores[0:sizes[-1], (KT - 1 - VT) * D:(KT - VT) * D],
                                     ACT.Identity).then_inc(values_kept, 1)

                def softmax(k, h):
                    act.wait_ge(negtop_ready, k + 1)
                    nc.scalar.activation(probs[h][:], scores[:, 0:K], ACT.Exp, bias=negtop[h][:], scale=SCALE,
                                         accum_out=total[h][:]).then_inc(probs_ready, 1)

                def step(k, h, more):
                    for c in BY_ACT:
                        act.wait_ge(turned_ready, k * NC + (c + 1))
                        n = len(chunks[c])
                        r = sizes[chunks[c][-1]] if n == 1 else P
                        nc.scalar.activation(probsT[h][0:r, chunks[c][0]:chunks[c][0] + n, :], turned[c % 2][0:r, 0:n, :],
                                             ACT.Identity).then_inc(kept_by_act, 1)
                    if more:
                        softmax(k + 1, 1 - h)

                softmax(0, 0)
                steps(act, step)


def route_to_two(nc, X, xT, ident, w):
    constants, ident = ident, ident[0]
    E = w["router_b"].shape[0]
    FF = w["W1"].shape[-1]
    FB = FF // P
    NT = 2 * S // P + E - 1
    BIG = 3.0e38
    hat = xT[:].rearrange("p b s -> p (b s)").rearrange("p (t d) -> p t d", d=D)
    slots = nc.dram_tensor("route_slots", [NT * P, D], F32).ap()
    answers = nc.dram_tensor("route_answers", [NT * P, D], F32).ap()
    bias_dram = nc.dram_tensor("route_bias", [E, 3, FF + D], BF16).ap()

    with ExitStack() as outer:
        def keep(n, shape, dt=F32):
            return outer.enter_context(nc.sbuf_tensor(f"route_{n}", shape, dt))

        W1 = keep("W1", [P, E * DB, FF])
        W2 = keep("W2", [P, E * FB, D])
        gates = keep("gates", [P, 2, TILES])
        position = keep("position", [P, 2, TILES], U32)
        expert = keep("expert", [P, NT], I32)
        ln_g = keep("ln_g", [P, E, DB])
        ln_b = keep("ln_b", [P, E, DB])
        zero = keep("zero", [P, D])
        W1_loaded = outer.enter_context(nc.semaphore("route_W1_loaded"))
        W2_loaded = outer.enter_context(nc.semaphore("route_W2_loaded"))
        slots_zeroed = outer.enter_context(nc.semaphore("route_slots_zeroed"))

        with ExitStack() as ctx:
            def sb(n, shape, dt=F32):
                return ctx.enter_context(nc.sbuf_tensor(f"route_{n}", shape, dt))

            sem = ctx.enter_context(semaphores(nc, "route"))

            TE = [P, TILES, E]
            rw = sb("rw", [P, DB, E])
            rb = sb("rb", [E, 1])
            logitsT = sb("logitsT", [E, S])
            logits, rest, hit, where = sb("logits", TE), sb("rest", TE), sb("hit", TE), sb("where", TE)
            first, second = sb("first", TE), sb("second", TE)
            chosen = sb("chosen", TE, BF16)
            iota_e = sb("iota_e", [P, E])
            iota_t = sb("iota_t", [P, TILES])
            iota_n = sb("iota_n", [P, NT])
            before = sb("before", [P, P], BF16)
            ones = sb("ones", [P, P], BF16)
            best, runner, gap, egap, denom = (sb(n, [P, TILES]) for n in ("best", "runner", "gap", "egap", "denom"))
            over = sb("over", [P, E, TILES])
            cnt, tiles_of, upto, base, ones_e = (sb(n, [P, E]) for n in ("cnt", "tiles_of", "upto", "base", "ones_e"))
            slot = sb("slot", TE)
            slot1 = sb("slot1", [P, TILES])
            past = sb("past", [P, NT, E])
            nth = sb("nth", [P, NT])
            b12 = sb("b12", [E, FF + D])
            left = sb("left", [E, FF + D])
            parts = sb("parts", [E, 3, FF + D], BF16)
            logit_ps = ctx.enter_context(nc.psum_tensor("route_logit_ps", [E, 4, 512], F32))
            turned = ctx.enter_context(nc.psum_tensor("route_turned", [P, TILES, E], F32))
            prefix = ctx.enter_context(nc.psum_tensor("route_prefix", [P, TILES, E], F32))
            count = ctx.enter_context(nc.psum_tensor("route_count", [P, 512], F32))
            small_loaded, logits_ready, logitsT_kept, turned_ready = sem("small_loaded"), sem("logits_ready"), sem("logitsT_kept"), sem("turned_ready")
            iotas, chosen_ready, prefix_ready, zero_ready = sem("iotas"), sem("chosen_ready"), sem("prefix_ready"), sem("zero_ready")
            gap_ready, egap_ready, chained, parts_ready, parts_stored = sem("gap_ready"), sem("egap_ready"), sem("chained"), sem("parts_ready"), sem("parts_stored")

            with nc.Block() as block:
                @block.sync
                def _(sp):
                    for to, what in ((rw[:], w["router_W"]), (rb[:], w["router_b"]), (b12[:, 0:FF], w["b1"]), (b12[:, FF:FF + D], w["b2"]),
                                     (ln_g[:], w["ln_g"]), (ln_b[:], w["ln_b"])):
                        sp.dma_start(to, what).then_inc(small_loaded, 16)
                    sp.wait_ge(zero_ready, 1)
                    sp.dma_start(slots.rearrange("(p j) d -> p j d", p=P),
                                 zero[:].unsqueeze(1).broadcast_to([P, NT, D])).then_inc(slots_zeroed, 16)
                    sp.dma_start(W1[:].rearrange("p (e b) f -> p e b f", e=E), w["W1"]).then_inc(W1_loaded, 16)
                    sp.dma_start(W2[:].rearrange("p (e b) f -> p e b f", e=E), w["W2"]).then_inc(W2_loaded, 16)
                    sp.wait_ge(parts_ready, 1)
                    sp.dma_start(bias_dram, parts[:]).then_inc(parts_stored, 16)
                    sp.wait_ge(parts_stored, 16)

                @block.tensor
                def _(pe):
                    pe.wait_ge(small_loaded, 96)
                    for c in range(4):
                        for b in range(DB):
                            last = nc.tensor.matmul(logit_ps[:, c, :], rw[:, b, :], xT[:, b, c * 512:(c + 1) * 512],
                                                    start=(b == 0), stop=(b == DB - 1))
                    last.then_inc(logits_ready, 1)
                    pe.wait_ge(logitsT_kept, 1)
                    for t in range(TILES):
                        last = nc.tensor.transpose(turned[:, t, :], logitsT[:, t * P:(t + 1) * P], ident[0:E, 0:E])
                    last.then_inc(turned_ready, 1)
                    pe.wait_ge(chosen_ready, 1)
                    pe.wait_ge(iotas, 5)
                    nc.tensor.matmul(prefix[:], before[:], chosen[:], start=True, stop=False)
                    for t in range(TILES - 1):
                        last = nc.tensor.matmul(prefix[:, t + 1:, :], ones[:],
                                                chosen[:, t:t + 1, :].broadcast_to([P, TILES - 1 - t, E]),
                                                start=False, stop=(t == TILES - 2))
                    for t in range(TILES):
                        last = nc.tensor.matmul(count[:, 0:E], ones[:], chosen[:, t, :], start=(t == 0), stop=(t == TILES - 1))
                    last.then_inc(prefix_ready, 1)

                @block.gpsimd
                def _(pool):
                    nc.gpsimd.memset(zero[:], 0.0).then_inc(zero_ready, 1)
                    exact = dict(allow_small_or_imprecise_dtypes=True)
                    nc.gpsimd.iota(iota_e[:], [[1, E]], base=0, channel_multiplier=0, **exact).then_inc(iotas, 1)
                    nc.gpsimd.iota(iota_t[:], [[P, TILES]], base=0, channel_multiplier=0, **exact).then_inc(iotas, 1)
                    nc.gpsimd.iota(iota_n[:], [[1, NT]], base=0, channel_multiplier=0, **exact).then_inc(iotas, 1)
                    nc.gpsimd.memset(ones[:], 1.0).then_inc(iotas, 1)
                    pool.wait_ge(iotas, 4)
                    nc.gpsimd.affine_select(out=before[:], in_=ones[:], compare_op=ALU.is_gt, fill=0.0, base=0,
                                            pattern=[[1, P]], channel_multiplier=-1).then_inc(iotas, 1)

                @block.scalar
                def _(act):
                    act.wait_ge(logits_ready, 1)
                    act.wait_ge(small_loaded, 96)
                    nc.scalar.activation(logitsT[:].rearrange("p (a b) -> p a b", a=4), logit_ps[:], ACT.Identity,
                                         bias=rb[:]).then_inc(logitsT_kept, 1)
                    act.wait_ge(gap_ready, 1)
                    nc.scalar.activation(egap[:], gap[:], ACT.Exp).then_inc(egap_ready, 1)

                @block.vector
                def _(dve):
                    done = [0]

                    def link(ins):
                        done[0] += 1
                        ins.then_inc(chained, 1)
                        dve.wait_ge(chained, done[0])

                    V = nc.vector
                    dve.wait_ge(small_loaded, 96)
                    link(V.tensor_copy(parts[:, 0, :], b12[:]))
                    link(V.tensor_tensor(left[:], b12[:], parts[:, 0, :], ALU.subtract))
                    link(V.tensor_copy(parts[:, 1, :], left[:]))
                    link(V.tensor_tensor(b12[:], left[:], parts[:, 1, :], ALU.subtract))
                    V.tensor_copy(parts[:, 2, :], b12[:]).then_inc(parts_ready, 1)

                    dve.wait_ge(turned_ready, 1)
                    link(V.tensor_copy(logits[:], turned[:]))
                    dve.wait_ge(iotas, 5)

                    def pick(which, values, top):
                        link(V.tensor_reduce(top[:], values[:], AX_X, ALU.max))
                        link(V.tensor_tensor(hit[:], values[:], top[:].unsqueeze(2).broadcast_to(TE), ALU.is_equal))
                        link(V.tensor_scalar(where[:], iota_e[:].unsqueeze(1).broadcast_to(TE), -1.0, float(E), ALU.mult, ALU.add))
                        link(V.tensor_tensor(where[:], where[:], hit[:], ALU.mult))
                        link(V.tensor_reduce(denom[:], where[:], AX_X, ALU.max))
                        link(V.tensor_tensor(which[:], where[:], denom[:].unsqueeze(2).broadcast_to(TE), ALU.is_equal))

                    pick(first, logits, best)
                    link(V.scalar_tensor_tensor(out=rest[:].rearrange("p a b -> p (a b)"), in0=first[:].rearrange("p a b -> p (a b)"),
                                                scalar=-BIG, in1=logits[:].rearrange("p a b -> p (a b)"), op0=ALU.mult, op1=ALU.add))
                    pick(second, rest, runner)
                    V.tensor_tensor(chosen[:], first[:], second[:], ALU.add).then_inc(chosen_ready, 1)
                    V.tensor_tensor(gap[:], runner[:], best[:], ALU.subtract).then_inc(gap_ready, 1)
                    dve.wait_ge(egap_ready, 1)
                    link(V.tensor_scalar(denom[:], egap[:], 1.0, None, ALU.add))
                    link(V.reciprocal(gates[:, 0, :], denom[:]))
                    link(V.tensor_tensor(gates[:, 1, :], egap[:], gates[:, 0, :], ALU.mult))

                    dve.wait_ge(prefix_ready, 1)
                    link(V.tensor_copy(cnt[:], count[:, 0:E]))
                    ET = [P, E, TILES]
                    link(V.tensor_tensor(over[:], cnt[:].unsqueeze(2).broadcast_to(ET), iota_t[:].unsqueeze(1).broadcast_to(ET), ALU.is_gt))
                    link(V.tensor_reduce(tiles_of[:], over[:], AX_X, ALU.add))
                    link(V.memset(ones_e[:], 1.0))
                    link(V.tensor_tensor_scan(upto[:], ones_e[:], tiles_of[:], 0.0, ALU.mult, ALU.add))
                    link(V.tensor_tensor(base[:], upto[:], tiles_of[:], ALU.subtract))
                    link(V.tensor_scalar(base[:], base[:], float(P), None, ALU.mult))
                    link(V.tensor_tensor(slot[:], prefix[:], base[:].unsqueeze(1).broadcast_to(TE), ALU.add))
                    for n, which in enumerate((first, second)):
                        link(V.tensor_tensor(where[:], slot[:], which[:], ALU.mult))
                        link(V.tensor_reduce(slot1[:], where[:], AX_X, ALU.add))
                        link(V.tensor_copy(position[:, n, :], slot1[:]))
                    NE = [P, NT, E]
                    link(V.tensor_tensor(past[:], iota_n[:].unsqueeze(2).broadcast_to(NE), upto[:].unsqueeze(1).broadcast_to(NE), ALU.is_ge))
                    link(V.tensor_reduce(nth[:], past[:], AX_X, ALU.add))
                    link(V.tensor_scalar(nth[:], nth[:], float(E - 1), None, ALU.min))
                    link(V.tensor_copy(expert[:], nth[:]))

        normalise(nc, "route_hat", X, xT, constants, hat=hat)

        with ExitStack() as ctx:
            def sb(n, shape, dt=F32):
                return ctx.enter_context(nc.sbuf_tensor(f"route_{n}", shape, dt))

            def ps(n, shape, dt=F32):
                return ctx.enter_context(nc.psum_tensor(f"route_{n}", shape, dt))

            sem = ctx.enter_context(semaphores(nc, "route"))

            rows = [sb(f"rows{h}", [P, D]) for h in range(2)]
            rowsT = [sb(f"rowsT{h}", [P, DB, P]) for h in range(2)]
            biases = [sb(f"biases{h}", [3, FF + D], BF16) for h in range(2)]
            ones3 = sb("ones3", [3, P], BF16)
            hidden = [sb(f"hidden{h}", [P, FF]) for h in range(2)]
            hiddenT = sb("hiddenT", [P, FB, P])
            answer = [sb(f"answer{h}", [P, D]) for h in range(2)]
            turned_ps = ps("turned_ps", [P, 512])
            hidden_ps = [ps(f"hidden_ps{h}", [P, FF]) for h in range(2)]
            hiddenT_ps = ps("hiddenT_ps", [P, FB, P])
            answer_ps = ps("answer_ps", [P, 512])
            scattered, turned_ready, rowsT_ready = sem("scattered"), sem("turned_rows"), sem("rowsT_ready")
            rows_loaded = [sem(f"rows_loaded{h}") for h in range(2)]
            biases_loaded = [sem(f"biases_loaded{h}") for h in range(2)]
            product_ready, hidden_ready, hiddenT_ready, hiddenT_kept = sem("product_ready"), sem("hidden_ready"), sem("hiddenT_ready"), sem("hiddenT_kept")
            answer_ready, answer_kept, ones_ready = sem("answer_ready"), sem("answer_kept"), sem("ones_ready")
            stored = [sem(f"stored{h}") for h in range(2)]

            def steps(eng, step):
                loops = (NT - 2) // 2
                with eng.Fori(0, loops) as i:
                    for h in range(2):
                        step(i * 2 + h, i, h, 2)
                for k in range(2 * loops, NT):
                    step(k, k // 2, k % 2, NT - 1 - k)

            def expert_of(eng, k):
                return eng.value_load(expert[0:1, bass.ds(k, 1)], min_val=0, max_val=E - 1)

            with nc.Block() as block:
                @block.gpsimd
                def _(pool):
                    nc.gpsimd.memset(ones3[:], 1.0).then_inc(ones_ready, 1)
                    pool.wait_ge(slots_zeroed, 16)
                    for t in range(TILES):
                        for n in range(2):
                            nc.gpsimd.indirect_dma_start(slots, bass.IndirectOffsetOnAxis(ap=position[:, n, t:t + 1], axis=0),
                                                         hat[:, t, :], None).then_inc(scattered, 16)

                @block.sync
                def _(sp):
                    def load_rows(k, h):
                        sp.dma_start(rows[h][:], slots[bass.ds(k * P, P), :]).then_inc(rows_loaded[h], 16)

                    def load_biases(k, h):
                        e = expert_of(sp, k)
                        sp.dma_start(biases[h][:], bias_dram[bass.ds(e, 1), :, :].rearrange("a b c -> (a b) c")).then_inc(biases_loaded[h], 16)

                    def step(k, j, h, follow):
                        if follow >= 2:
                            sp.wait_ge(turned_ready, k + 1)
                            load_rows(k + 2, h)
                        sp.wait_ge(answer_kept, k + 1)
                        sp.dma_start(answers[bass.ds(k * P, P), :], answer[h][:]).then_inc(stored[h], 16)
                        if follow >= 2:
                            load_biases(k + 2, h)

                    sp.wait_ge(scattered, 2 * TILES * 16)
                    for h in range(2):
                        load_rows(h, h)
                        load_biases(h, h)
                    steps(sp, step)
                    sp.wait_ge(stored[0], (NT + 1) // 2 * 16)
                    sp.wait_ge(stored[1], NT // 2 * 16)

                @block.tensor
                def _(pe):
                    def turn(j, h):
                        pe.wait_ge(rows_loaded[h], j * 16 + 16)
                        for b in range(DB):
                            last = nc.tensor.transpose(turned_ps[:, b * P:(b + 1) * P], rows[h][:, b * P:(b + 1) * P], ident[:])
                        last.then_inc(turned_ready, 1)

                    def first_product(k, j, h, half):
                        e = expert_of(pe, k)
                        if half == 0:
                            pe.wait_ge(biases_loaded[h], j * 16 + 16)
                            pe.wait_ge(rowsT_ready, k * DB + DB)
                        n = slice(half * 512, half * 512 + 512)
                        nc.tensor.matmul(hidden_ps[h][:, n], ones3[:], biases[h][:, n], start=True, stop=False)
                        for b in range(DB):
                            last = nc.tensor.matmul(hidden_ps[h][:, n], rowsT[h][:, b, :],
                                                    W1[:, bass.ds(e * DB + b, 1), n].rearrange("p a b -> p (a b)"), start=False, stop=(b == DB - 1))
                        if half == 1:
                            last.then_inc(product_ready, 1)

                    def second_product(k, h):
                        e = expert_of(pe, k)
                        nc.tensor.matmul(answer_ps[:, 0:D], ones3[:], biases[h][:, FF:FF + D], start=True, stop=False)
                        for f in range(FB):
                            if f % (FB // 2) == 0:
                                pe.wait_ge(hiddenT_kept, k * 2 + (2 * f // FB + 1))
                            last = nc.tensor.matmul(answer_ps[:, 0:D], hiddenT[:, f, :],
                                                    W2[:, bass.ds(e * FB + f, 1), :].rearrange("p a b -> p (a b)"), start=False, stop=(f == FB - 1))
                        last.then_inc(answer_ready, 1)

                    def step(k, j, h, follow):
                        if follow >= 1:
                            first_product(k + 1, j + h, 1 - h, 0)
                        pe.wait_ge(hidden_ready, k * 1 + 1)
                        for f in range(FB):
                            last = nc.tensor.transpose(hiddenT_ps[:, f, :], hidden[h][:, f * P:(f + 1) * P], ident[:])
                            if f % (FB // 2) == FB // 2 - 1:
                                last.then_inc(hiddenT_ready, 1)
                        if follow >= 1:
                            first_product(k + 1, j + h, 1 - h, 1)
                        if follow >= 2:
                            turn(j + 1, h)
                        second_product(k, h)
                        pe.wait_ge(answer_kept, k + 1)

                    pe.wait_ge(ones_ready, 1)
                    pe.wait_ge(W1_loaded, 16)
                    pe.wait_ge(W2_loaded, 16)
                    turn(0, 0)
                    first_product(0, 0, 0, 0)
                    first_product(0, 0, 0, 1)
                    turn(0, 1)
                    steps(pe, step)

                @block.scalar
                def _(act):
                    def scale_rows(k, h):
                        e = expert_of(act, k)
                        act.wait_ge(turned_ready, k + 1)
                        for b in range(DB):
                            nc.scalar.activation(rowsT[h][:, b, :], turned_ps[:, b * P:(b + 1) * P], ACT.Identity,
                                                 bias=ln_b[:, bass.ds(e, 1), b], scale=ln_g[:, bass.ds(e, 1), b]).then_inc(rowsT_ready, 1)

                    def gelu(k, h):
                        act.wait_ge(product_ready, k + 1)
                        nc.scalar.activation(hidden[h][:], hidden_ps[h][:], ACT.Gelu).then_inc(hidden_ready, 1)

                    def step(k, j, h, follow):
                        if follow >= 1:
                            gelu(k + 1, 1 - h)
                        if follow >= 2:
                            scale_rows(k + 2, h)
                        act.wait_ge(answer_ready, k + 1)
                        nc.scalar.activation(answer[h][:], answer_ps[:, 0:D], ACT.Identity).then_inc(answer_kept, 1)
                        if follow >= 2:
                            act.wait_ge(stored[h], j * 16 + 16)

                    scale_rows(0, 0)
                    gelu(0, 0)
                    scale_rows(1, 1)
                    steps(act, step)

                @block.vector
                def _(dve):
                    def step(k, j, h, follow):
                        for half in range(2):
                            dve.wait_ge(hiddenT_ready, k * 2 + (half + 1))
                            f = slice(half * FB // 2, (half + 1) * FB // 2)
                            nc.vector.tensor_copy(hiddenT[:, f, :], hiddenT_ps[:, f, :]).then_inc(hiddenT_kept, 1)
                    steps(dve, step)

        with ExitStack() as ctx:
            fetched = [ctx.enter_context(nc.semaphore(f"route_fetched{t}")) for t in range(4)]
            weighed = ctx.enter_context(nc.semaphore("route_weighed"))
            added = ctx.enter_context(nc.semaphore("route_added"))
            summed = ctx.enter_context(nc.semaphore("route_summed"))
            first = ctx.enter_context(nc.semaphore("route_first"))
            second = ctx.enter_context(nc.semaphore("route_second"))
            own = ctx.enter_context(nc.sbuf_tensor("route_own", [P, TILES], F32))
            got = W1[:].rearrange("p a b -> p (a b)").rearrange("p (c d) -> p c d", d=D)
            with nc.Block() as block:
                @block.gpsimd
                def _(pool):
                    for t in range(TILES):
                        for n in range(2):
                            nc.gpsimd.indirect_dma_start(got[:, 2 * t + n, :], None, answers,
                                                         bass.IndirectOffsetOnAxis(ap=position[:, n, t:t + 1], axis=0)).then_inc(fetched[t // GT], 16)

                @block.vector
                def _(dve):
                    nc.vector.tensor_tensor(own[:], gates[:, 0, :], gates[:, 1, :], ALU.add).then_inc(summed, 1)
                    dve.wait_ge(summed, 1)
                    nc.vector.tensor_scalar(own[:], own[:], 1.0, None, ALU.add).then_inc(summed, 1)
                    dve.wait_ge(summed, 2)
                    for q in range(TILES // GT):
                        dve.wait_ge(fetched[q], 2 * GT * 16)
                        tiles = range(q * GT, (q + 1) * GT)
                        for t in tiles:
                            nc.vector.tensor_scalar(X[:, t, :], X[:, t, :], own[:, t:t + 1], None, ALU.mult).then_inc(weighed, 1)
                        for t in tiles:
                            dve.wait_ge(weighed, t + 1)
                            nc.vector.scalar_tensor_tensor(out=X[:, t, :], in0=got[:, 2 * t, :], scalar=gates[:, 0, t:t + 1],
                                                           in1=X[:, t, :], op0=ALU.mult, op1=ALU.add).then_inc(first, 1)
                        for t in tiles:
                            dve.wait_ge(first, t + 1)
                            nc.vector.scalar_tensor_tensor(out=X[:, t, :], in0=got[:, 2 * t + 1, :], scalar=gates[:, 1, t:t + 1],
                                                           in1=X[:, t, :], op0=ALU.mult, op1=ALU.add).then_inc(second, 1)
                    dve.wait_ge(second, TILES)
    normalise(nc, "route_norm", X, xT, constants)


def self_attention_of_one(nc, X, xT, ident, wv, woT, bv, bo):
    ident = ident[0]
    H = 2
    with ExitStack() as ctx:
        def sb(n, shape, dt=F32):
            return ctx.enter_context(nc.sbuf_tensor(f"one_{n}", shape, dt))

        sem = ctx.enter_context(semaphores(nc, "one"))

        wv_sb = sb("wv", [P, DB, D])
        woT_sb = sb("woT", [P, DB, D])
        bv_sb = sb("bv", [P, DB])
        bo_sb = sb("bo", [P, DB])
        both = sb("both", [P, DB, D])
        shift = sb("shift", [P, DB])
        branch = [sb(f"branch{h}", [P, DB, GS]) for h in range(H)]
        product = [ctx.enter_context(nc.psum_tensor(f"one_product{h}", [P, DB, GS], F32)) for h in range(H)]
        rows = [ctx.enter_context(nc.psum_tensor(f"one_rows{h}", [P, GT, D], F32)) for h in range(H)]
        loaded, both_ready, both_kept, shift_kept = sem("loaded"), sem("both_ready"), sem("both_kept"), sem("shift_kept")
        product_ready, branch_ready, rows_ready, rows_kept = sem("product_ready"), sem("branch_ready"), sem("rows_ready"), sem("rows_kept")

        with nc.Block() as block:
            @block.sync
            def _(sp):
                for to, what in ((wv_sb, wv), (woT_sb, woT), (bv_sb, bv), (bo_sb, bo)):
                    sp.dma_start(to[:], what).then_inc(loaded, 16)
                sp.wait_ge(loaded, 64)

            @block.tensor
            def _(pe):
                pe.wait_ge(loaded, 64)
                for i in range(DB):
                    for m in range(DB):
                        nc.tensor.matmul(product[0][:, 0, i * D:(i + 1) * D], wv_sb[:, m, i * P:(i + 1) * P],
                                         woT_sb[:, m, :], start=(m == 0), stop=(m == DB - 1))
                for o in range(DB):
                    for m in range(DB):
                        last = nc.tensor.matmul(product[0][:, 1, o:o + 1], woT_sb[:, m, o * P:(o + 1) * P],
                                                bv_sb[:, m:m + 1], start=(m == 0), stop=(m == DB - 1))
                last.then_inc(both_ready, 1)
                pe.wait_ge(both_kept, 1)
                pe.wait_ge(shift_kept, 1)
                with pe.Fori(0, GROUPS // H) as i:
                    for h in range(H):
                        for o in range(DB):
                            for b in range(DB):
                                last = nc.tensor.matmul(product[h][:, o, :], both[:, b, o * P:(o + 1) * P],
                                                        xT[:, b, bass.ds((i * H + h) * GS, GS)], start=(b == 0), stop=(b == DB - 1))
                        last.then_inc(product_ready, 1)
                    for h in range(H):
                        pe.wait_ge(branch_ready, (i * H + (h + 1)) * DB)
                        for t in range(GT):
                            for o in range(DB):
                                last = nc.tensor.transpose(rows[h][:, t, o * P:(o + 1) * P],
                                                           branch[h][:, o, t * P:(t + 1) * P], ident[:])
                        last.then_inc(rows_ready, 1)
                    pe.wait_ge(rows_kept, i * H + H)

            @block.vector
            def _(dve):
                dve.wait_ge(loaded, 64)
                dve.wait_ge(both_ready, 1)
                nc.vector.tensor_tensor(shift[:], product[0][:, 1, 0:DB], bo_sb[:], ALU.add).then_inc(shift_kept, 1)
                dve.wait_ge(shift_kept, 1)
                with dve.Fori(0, GROUPS // H) as i:
                    for h in range(H):
                        dve.wait_ge(product_ready, i * H + (h + 1))
                        for o in range(DB):
                            nc.vector.scalar_tensor_tensor(out=branch[h][:, o, :], in0=product[h][:, o, :],
                                                           scalar=shift[:, o:o + 1], in1=xT[:, o, bass.ds((i * H + h) * GS, GS)],
                                                           op0=ALU.add, op1=ALU.add).then_inc(branch_ready, 1)
                    dve.wait_ge(rows_ready, i * H + H)

            @block.scalar
            def _(act):
                act.wait_ge(both_ready, 1)
                nc.scalar.activation(both[:].rearrange("p i o -> p (i o)"), product[0][:, 0, :], ACT.Identity).then_inc(both_kept, 1)
                with act.Fori(0, GROUPS // H) as i:
                    for h in range(H):
                        act.wait_ge(rows_ready, i * H + (h + 1))
                        nc.scalar.activation(X[:, bass.ds((i * H + h) * GT, GT), :], rows[h][:], ACT.Identity).then_inc(rows_kept, 1)
                act.wait_ge(rows_kept, GROUPS)


def attend_heads(nc, X, xT, ident, w):
    constants, ident = ident, ident[0]
    HEADS = 16
    W = D // HEADS
    SCALE = float(W) ** -0.5
    K = w["contextT"].shape[-1]
    KT = -(-K // P)
    ksize = [min(P, K - P * k) for k in range(KT)]
    PARTS = 3
    PAIRS = [(0, 0), (0, 1), (0, 2), (1, 0), (1, 1), (2, 0)]
    ROWS = len(PAIRS) * W
    ALL = ROWS + PARTS
    QUAD = 4
    QUADS = HEADS // QUAD
    VW = 32
    BIG = -3.0e38
    q_dram = nc.dram_tensor("heads_q", [PARTS, D, S], BF16).ap()
    k_dram = nc.dram_tensor("heads_k", [PARTS, D, K], BF16).ap()
    m_dram = nc.dram_tensor("heads_m", [PARTS, HEADS, S], BF16).ap()

    with ExitStack() as outer:
        def keep(n, shape, dt=F32):
            return outer.enter_context(nc.sbuf_tensor(f"heads_{n}", shape, dt))

        values = keep("values", [P, KT, HEADS, W])
        w_o = keep("w_o", [P, DB, D])
        attended = keep("attended", [P, TILES, D])
        ident_b = keep("ident_b", [P, P], BF16)
        later = keep("later", [P, P], BF16)
        laterT = keep("laterT", [P, P], BF16)
        w_o_loaded = outer.enter_context(nc.semaphore("heads_w_o_loaded"))
        masks_made = outer.enter_context(nc.semaphore("heads_masks_made"))

        with ExitStack() as ctx:
            def sb(n, shape, dt=F32):
                return ctx.enter_context(nc.sbuf_tensor(f"heads_{n}", shape, dt))

            sem = ctx.enter_context(semaphores(nc, "heads"))

            keysT = sb("keysT", [P, DB, K])
            wq, wk, wv = sb("wq", [P, DB, D]), sb("wk", [P, DB, D]), sb("wv", [P, DB, D])
            parts = [sb(f"parts{h}", [P, PARTS, 512], BF16) for h in range(2)]
            rest = [sb(f"rest{h}", [P, 512]) for h in range(2)]
            product = [ctx.enter_context(nc.psum_tensor(f"heads_product{h}", [P, 512], F32)) for h in range(2)]
            value_ps = [ctx.enter_context(nc.psum_tensor(f"heads_value_ps{h}", [P, 512], F32)) for h in range(2)]
            loaded, product_ready, part1, rest1, part2, part3, value_ready, value_kept, zeroed = (
                sem(n) for n in ("loaded", "product_ready", "part1", "rest1", "part2", "part3", "value_ready", "value_kept", "zeroed"))
            parts_stored = [sem(f"parts_stored{h}") for h in range(2)]
            units = [(wq, xT, q_dram, o, c, min(512, S - c)) for o in range(DB) for c in range(0, S, 512)]
            units += [(wk, keysT, k_dram, o, c, min(512, K - c)) for o in range(DB) for c in range(0, K, 512)]
            N = len(units)

            with nc.Block() as block:
                @block.sync
                def _(sp):
                    for to, what in ((wq, w["w_qT"]), (keysT, w["contextT"]), (wk, w["w_kT"]), (wv, w["w_vT"])):
                        sp.dma_start(to[:], what).then_inc(loaded, 16)
                    sp.dma_start(w_o[:], w["w_oT"]).then_inc(w_o_loaded, 16)
                    for n, (_, _, dram, o, c, size) in enumerate(units):
                        sp.wait_ge(part3, n + 1)
                        sp.dma_start(dram[:, o * P:(o + 1) * P, c:c + size].rearrange("a p s -> p a s"),
                                     parts[n % 2][:, :, 0:size]).then_inc(parts_stored[n % 2], 16)
                    for h in range(2):
                        sp.wait_ge(parts_stored[h], N // 2 * 16)

                @block.gpsimd
                def _(pool):
                    nc.gpsimd.memset(ident_b[:], 0.0).then_inc(zeroed, 1)
                    nc.gpsimd.memset(later[:], 0.0).then_inc(zeroed, 1)
                    nc.gpsimd.memset(laterT[:], 0.0).then_inc(zeroed, 1)
                    pool.wait_ge(zeroed, 3)
                    nc.gpsimd.affine_select(out=ident_b[:], in_=ident_b[:], compare_op=ALU.not_equal, fill=1.0, base=0,
                                            pattern=[[-1, P]], channel_multiplier=1).then_inc(masks_made, 1)
                    nc.gpsimd.affine_select(out=later[:], in_=later[:], compare_op=ALU.is_ge, fill=BIG, base=0,
                                            pattern=[[-1, P]], channel_multiplier=1).then_inc(masks_made, 1)
                    nc.gpsimd.affine_select(out=laterT[:], in_=laterT[:], compare_op=ALU.is_ge, fill=BIG, base=0,
                                            pattern=[[1, P]], channel_multiplier=-1).then_inc(masks_made, 1)

                @block.tensor
                def _(pe):
                    pe.wait_ge(loaded, 64)
                    for n, (wt, src, _, o, c, size) in enumerate(units):
                        if n >= 2:
                            pe.wait_ge(rest1, n - 1)
                        for b in range(DB):
                            last = nc.tensor.matmul(product[n % 2][:, 0:size], wt[:, b, o * P:(o + 1) * P], src[:, b, c:c + size],
                                                    start=(b == 0), stop=(b == DB - 1))
                        last.then_inc(product_ready, 1)
                    for k in range(KT):
                        if k >= 2:
                            pe.wait_ge(value_kept, k - 1)
                        for b in range(DB):
                            last = nc.tensor.matmul(value_ps[k % 2][0:ksize[k], 0:D], keysT[:, b, k * P:k * P + ksize[k]], wv[:, b, :],
                                                    start=(b == 0), stop=(b == DB - 1))
                        last.then_inc(value_ready, 1)

                @block.scalar
                def _(act):
                    for n, (_, _, _, o, c, size) in enumerate(units):
                        h = n % 2
                        act.wait_ge(product_ready, n + 1)
                        if n >= 2:
                            act.wait_ge(parts_stored[h], n // 2 * 16)
                        nc.scalar.activation(parts[h][:, 0, 0:size], product[h][:, 0:size], ACT.Identity).then_inc(part1, 1)
                        act.wait_ge(rest1, n + 1)
                        nc.scalar.activation(parts[h][:, 1, 0:size], rest[h][:, 0:size], ACT.Identity).then_inc(part2, 1)
                    for k in range(KT):
                        act.wait_ge(value_ready, k + 1)
                        nc.scalar.activation(values[0:ksize[k], k, :, :].rearrange("p h w -> p (h w)"), value_ps[k % 2][0:ksize[k], 0:D],
                                             ACT.Identity).then_inc(value_kept, 1)

                @block.vector
                def _(dve):
                    for n, (_, _, _, o, c, size) in enumerate(units):
                        h = n % 2
                        dve.wait_ge(part1, n + 1)
                        nc.vector.tensor_tensor(rest[h][:, 0:size], product[h][:, 0:size], parts[h][:, 0, 0:size],
                                                ALU.subtract).then_inc(rest1, 1)
                        dve.wait_ge(part2, n + 1)
                        nc.vector.tensor_tensor(parts[h][:, 2, 0:size], rest[h][:, 0:size], parts[h][:, 1, 0:size],
                                                ALU.subtract).then_inc(part3, 1)

        with ExitStack() as ctx:
            def sb(n, shape, dt=F32):
                return ctx.enter_context(nc.sbuf_tensor(f"heads_{n}", shape, dt))

            sem = ctx.enter_context(semaphores(nc, "heads"))

            queries = [sb(f"max_q{h}", [ROWS, S], BF16) for h in range(2)]
            keys = [sb(f"max_k{h}", [ROWS, K], BF16) for h in range(2)]
            most = sb("most", [P, HEADS, TILES])
            HT = HEADS * TILES // P
            down = sb("down", [P, HT, P])
            down_parts = sb("down_parts", [P, PARTS, HT, P], BF16)
            down1, down2 = sb("down1", [P, HT, P]), sb("down2", [P, HT, P])
            scores = [ctx.enter_context(nc.psum_tensor(f"heads_max_scores{h}", [P, 2048], F32)) for h in range(2)]
            stack_loaded = [sem(f"max_loaded{h}") for h in range(2)]
            head_done, scores_ready, scores_free, most_ready, most_turned, chained, down_stored, down_made = (
                sem(n) for n in ("max_head_done", "max_scores_ready", "max_scores_free", "most_ready", "most_turned", "max_chained", "down_stored", "down_made"))

            with nc.Block() as block:
                @block.sync
                def _(sp):
                    def load(head, h):
                        rows = bass.ds(head * W, W)
                        for r, (a, b) in enumerate(PAIRS):
                            sp.dma_start(queries[h][r * W:(r + 1) * W, :], q_dram[a, rows, :]).then_inc(stack_loaded[h], 16)
                            sp.dma_start(keys[h][r * W:(r + 1) * W, :], k_dram[b, rows, :]).then_inc(stack_loaded[h], 16)
                    load(0, 0)
                    load(1, 1)
                    with sp.Fori(0, HEADS // 2 - 1) as i:
                        for h in range(2):
                            sp.wait_ge(head_done, i * 2 + (h + 1))
                            load(i * 2 + (h + 2), h)
                    sp.wait_ge(down_made, 1)
                    for a in range(PARTS):
                        sp.dma_start(m_dram[a].rearrange("(c h) (t q) -> (h t) c q", c=HT, q=P), down_parts[:, a, :, :]).then_inc(down_stored, 16)
                    sp.wait_ge(down_stored, PARTS * 16)

                @block.tensor
                def _(pe):
                    pe.wait_ge(masks_made, 3)
                    with pe.Fori(0, HEADS // 2) as i:
                        for h in range(2):
                            pe.wait_ge(stack_loaded[h], i * (2 * len(PAIRS) * 16) + 2 * len(PAIRS) * 16)
                            for t in range(TILES):
                                n = min((t + 1) * P, K)
                                diag = t * P < n
                                pe.wait_ge(scores_free, (i * 2 + h) * TILES + (t + 1))
                                for c in range(0, n, 512):
                                    m = min(512, n - c)
                                    masked = diag and c + m == n
                                    last = nc.tensor.matmul(scores[t % 2][:, c:c + m], queries[h][:, t * P:(t + 1) * P], keys[h][:, c:c + m],
                                                            start=True, stop=not masked)
                                if diag:
                                    last = nc.tensor.matmul(scores[t % 2][:, t * P:n], ident_b[:], later[:, 0:n - t * P],
                                                            start=False, stop=True)
                                last.then_inc(scores_ready, 1)
                            pe.wait_ge(scores_free, (i * 2 + h) * TILES + (TILES + 2))
                            pe.sem_inc(head_done, 1)
                    pe.wait_ge(most_ready, 1)
                    for c in range(HT):
                        last = nc.tensor.transpose(scores[0][:, c * P:(c + 1) * P],
                                                   most[:].rearrange("p h t -> p (h t)")[:, c * P:(c + 1) * P], ident[:])
                    last.then_inc(most_turned, 1)

                @block.vector
                def _(dve):
                    done = [0]

                    def link(ins):
                        done[0] += 1
                        ins.then_inc(chained, 1)
                        dve.wait_ge(chained, done[0])

                    dve.sem_inc(scores_free, 2)
                    with dve.Fori(0, HEADS // 2) as i:
                        for h in range(2):
                            for t in range(TILES):
                                n = min((t + 1) * P, K)
                                dve.wait_ge(scores_ready, (i * 2 + h) * TILES + (t + 1))
                                nc.vector.reduce_max(most[:, bass.ds(i * 2 + h, 1), t], scores[t % 2][:, 0:n], AX_X).then_inc(scores_free, 1)
                    dve.wait_ge(scores_free, HEADS * TILES + 2)
                    dve.sem_inc(most_ready, 1)
                    dve.wait_ge(most_turned, 1)
                    V = nc.vector
                    link(V.tensor_scalar(down[:].rearrange("p c q -> p (c q)"), scores[0][:, 0:HT * P], -1.0, None, ALU.mult))
                    link(V.tensor_copy(down_parts[:, 0, :, :], down[:]))
                    link(V.tensor_tensor(down1[:], down[:], down_parts[:, 0, :, :], ALU.subtract))
                    link(V.tensor_copy(down_parts[:, 1, :, :], down1[:]))
                    link(V.tensor_tensor(down2[:], down1[:], down_parts[:, 1, :, :], ALU.subtract))
                    V.tensor_copy(down_parts[:, 2, :, :], down2[:]).then_inc(down_made, 1)

        with ExitStack() as ctx:
            def sb(n, shape, dt=F32):
                return ctx.enter_context(nc.sbuf_tensor(f"heads_{n}", shape, dt))

            sem = ctx.enter_context(semaphores(nc, "heads"))

            queries = [[sb(f"q{h}_{j}", [ALL, S], BF16) for j in range(QUAD)] for h in range(2)]
            keys = [[sb(f"k{h}_{j}", [ALL, K], BF16) for j in range(QUAD)] for h in range(2)]
            probs = [sb(f"probs{h}", [P, QUAD, 512]) for h in range(2)]
            quad_values = sb("quad_values", [P, KT, QUAD, VW])
            mixed = sb("mixed", [P, 512])
            share = sb("share", [P, GT, QUAD])
            scores = [ctx.enter_context(nc.psum_tensor(f"heads_scores{p}", [P, 2, 512], F32)) for p in range(2)]
            mixed_ps = [ctx.enter_context(nc.psum_tensor(f"heads_mixed{h}", [P, 512], F32)) for h in range(2)]
            turned = ctx.enter_context(nc.psum_tensor("heads_turned", [P, GT, P], F32))
            stack_loaded = [sem(f"stack_loaded{h}") for h in range(2)]
            units = [(g, k) for g in range(GROUPS) for k in range(min(KT, (g + 1) * GT))]
            U = len(units)
            LOADS = QUAD * (2 * len(PAIRS) + 1)
            quad_done, ones_made, values_ready, values_free, scores_ready, probs_ready, probs_free = (
                sem(n) for n in ("quad_done", "ones_made", "values_ready", "values_free", "scores_ready", "probs_ready", "probs_free"))
            mixed_kept, turned_ready, share_ready, attended_ready = (
                sem(n) for n in ("mixed_kept", "turned_ready", "share_ready", "attended_ready"))

            with nc.Block() as block:
                @block.sync
                def _(sp):
                    def load(quad, h):
                        for j in range(QUAD):
                            rows = bass.ds((quad * QUAD + j) * W, W)
                            for r, (a, b) in enumerate(PAIRS):
                                sp.dma_start(queries[h][j][r * W:(r + 1) * W, :], q_dram[a, rows, :]).then_inc(stack_loaded[h], 16)
                                sp.dma_start(keys[h][j][r * W:(r + 1) * W, :], k_dram[b, rows, :]).then_inc(stack_loaded[h], 16)
                            sp.dma_start(queries[h][j][ROWS:ALL, :], m_dram[:, bass.ds(quad * QUAD + j, 1), :].rearrange("a b s -> (a b) s")).then_inc(stack_loaded[h], 16)
                    load(0, 0)
                    load(1, 1)
                    with sp.Fori(0, QUADS // 2 - 1) as i:
                        for h in range(2):
                            sp.wait_ge(quad_done, i * 2 + (h + 1))
                            load(i * 2 + (h + 2), h)

                @block.gpsimd
                def _(pool):
                    for h in range(2):
                        for j in range(QUAD):
                            nc.gpsimd.memset(keys[h][j][ROWS:ALL, :], 1.0).then_inc(ones_made, 1)
                            pool.wait_ge(ones_made, h * QUAD + (j + 1))
                    nc.gpsimd.memset(quad_values[:], 0.0).then_inc(ones_made, 1)
                    pool.wait_ge(ones_made, 2 * QUAD + 1)
                    nc.gpsimd.memset(quad_values[:, :, :, W:W + 1], 1.0).then_inc(ones_made, 1)
                    pool.sem_inc(values_free, 1)
                    with pool.Fori(0, QUADS) as quad:
                        pool.wait_ge(values_free, quad + 1)
                        for k0, k1, r in ((0, KT - 1, P), (KT - 1, KT, ksize[-1])):
                            nc.gpsimd.tensor_copy(quad_values[0:r, k0:k1, :, 0:W], values[0:r, k0:k1, bass.ds(quad * QUAD, QUAD), :]).then_inc(values_ready, 1)

                @block.tensor
                def _(pe):
                    pe.wait_ge(ones_made, 2 * QUAD + 2)
                    with pe.Fori(0, QUADS // 2) as i:
                        for h in range(2):
                            quad = i * 2 + h
                            pe.wait_ge(stack_loaded[h], i * (LOADS * 16) + LOADS * 16)
                            pe.wait_ge(values_ready, quad * 2 + 2)

                            def score(u):
                                g, k = units[u]
                                c = max(0, (k - g * GT) * P)
                                diag = k >= g * GT
                                m = ksize[k]
                                for p in range(2):
                                    pe.wait_ge(probs_ready, quad * (2 * U) + (2 * u + p + 1))
                                    for e in range(2):
                                        j = p * 2 + e
                                        last = nc.tensor.matmul(scores[p][0:m, e, c:512], keys[h][j][:, k * P:k * P + m],
                                                                queries[h][j][:, g * GS + c:(g + 1) * GS], start=True, stop=not diag)
                                        if diag:
                                            last = nc.tensor.matmul(scores[p][0:m, e, c:c + P], ident_b[:, 0:m], laterT[:],
                                                                    start=False, stop=True)
                                    last.then_inc(scores_ready, 1)

                            def mix(u):
                                g, k = units[u]
                                c = max(0, (k - g * GT) * P)
                                m = ksize[k]
                                end = u == U - 1 or units[u + 1][0] != g
                                pe.wait_ge(probs_ready, quad * (2 * U) + (2 * u + 2 + 2))
                                if k == 0:
                                    pe.wait_ge(mixed_kept, quad * GROUPS + (g + 1))
                                for j in range(QUAD):
                                    last = nc.tensor.matmul(mixed_ps[g % 2][j * VW:(j + 1) * VW, c:512], quad_values[0:m, k, j, :],
                                                            probs[u % 2][0:m, j, c:512], start=(k == 0), stop=end)
                                last.then_inc(probs_free, 1)
                                return g if end else None

                            def turn(g):
                                pe.wait_ge(mixed_kept, quad * GROUPS + (g + 1 + 2))
                                for t in range(GT):
                                    last = nc.tensor.transpose(turned[:, t, :], mixed[:, t * P:(t + 1) * P], ident[:])
                                last.then_inc(turned_ready, 1)

                            turn_next = None
                            for u in range(U + 1):
                                if u < U:
                                    score(u)
                                if turn_next is not None:
                                    turn(turn_next)
                                    turn_next = None
                                if u >= 1:
                                    turn_next = mix(u - 1)
                            turn(turn_next)
                            pe.wait_ge(attended_ready, quad * GROUPS + GROUPS)
                            pe.sem_inc(quad_done, 1)
                            pe.sem_inc(values_free, 1)

                @block.scalar
                def _(act):
                    act.sem_inc(probs_ready, 2)
                    act.wait_ge(ones_made, 1)
                    with act.Fori(0, QUADS) as quad:
                        for u, (g, k) in enumerate(units):
                            c = max(0, (k - g * GT) * P)
                            m = ksize[k]
                            act.wait_ge(probs_free, quad * U + (u + 1 + (u == 0) * (U % 2)))
                            for p in range(2):
                                act.wait_ge(scores_ready, quad * (2 * U) + (2 * u + p + 1))
                                nc.scalar.activation(probs[u % 2][0:m, 2 * p:2 * p + 2, c:512], scores[p][0:m, :, c:512], ACT.Exp,
                                                     scale=SCALE).then_inc(probs_ready, 1)

                @block.vector
                def _(dve):
                    dve.sem_inc(probs_free, 2)
                    dve.sem_inc(mixed_kept, 2)
                    with dve.Fori(0, QUADS) as quad:
                        for g in range(GROUPS):
                            dve.wait_ge(probs_free, quad * U + (units.index((g + 1, 0)) if g + 1 < GROUPS else U) + 2)
                            nc.vector.tensor_copy(mixed[:], mixed_ps[g % 2][:]).then_inc(mixed_kept, 1)
                            dve.wait_ge(turned_ready, quad * GROUPS + (g + 1))
                            o = turned[:].rearrange("p t (j v) -> p t j v", v=VW)
                            nc.vector.reciprocal(share[:], o[:, :, :, W]).then_inc(share_ready, 1)
                            dve.wait_ge(share_ready, quad * GROUPS + (g + 1))
                            for t in range(GT):
                                to = attended[:, g * GT + t, :].rearrange("p (a w) -> p a w", w=W)[:, bass.ds(quad * QUAD, QUAD), :]
                                nc.vector.tensor_tensor(to, o[:, t, :, 0:W], share[:, t, :].unsqueeze(2).broadcast_to([P, QUAD, W]),
                                                        ALU.mult).then_inc(attended_ready, 1)

        with ExitStack() as ctx:
            attendedT = [ctx.enter_context(nc.sbuf_tensor(f"heads_attendedT{h}", [P, DB, P], F32)) for h in range(2)]
            turned = [ctx.enter_context(nc.psum_tensor(f"heads_attended_ps{h}", [P, 512], F32)) for h in range(2)]
            out_ps = [ctx.enter_context(nc.psum_tensor(f"heads_out_ps{h}", [P, 512], F32)) for h in range(2)]
            turned_ready, turned_kept, out_ready, added = (
                ctx.enter_context(nc.semaphore(f"heads_{n}")) for n in ("attended_turned", "attendedT_kept", "out_ready", "added"))
            with nc.Block() as block:
                @block.tensor
                def _(pe):
                    pe.wait_ge(w_o_loaded, 16)
                    for t in range(TILES + 1):
                        if t < TILES:
                            if t >= 2:
                                pe.wait_ge(turned_kept, t - 1)
                            for b in range(DB):
                                last = nc.tensor.transpose(turned[t % 2][:, b * P:(b + 1) * P], attended[:, t, b * P:(b + 1) * P], ident[:])
                            last.then_inc(turned_ready, 1)
                        if t:
                            pe.wait_ge(turned_kept, t)
                            if t >= 3:
                                pe.wait_ge(added, t - 2)
                            h = (t - 1) % 2
                            for b in range(DB):
                                last = nc.tensor.matmul(out_ps[h][:, 0:D], attendedT[h][:, b, :], w_o[:, b, :], start=(b == 0), stop=(b == DB - 1))
                            last.then_inc(out_ready, 1)

                @block.scalar
                def _(act):
                    for t in range(TILES):
                        act.wait_ge(turned_ready, t + 1)
                        if t >= 2:
                            act.wait_ge(out_ready, t - 1)
                        nc.scalar.activation(attendedT[t % 2][:].rearrange("p b q -> p (b q)"), turned[t % 2][:, 0:D], ACT.Identity).then_inc(turned_kept, 1)

                @block.vector
                def _(dve):
                    for t in range(TILES):
                        dve.wait_ge(out_ready, t + 1)
                        nc.vector.tensor_tensor(X[:, t, :], out_ps[t % 2][:, 0:D], X[:, t, :], ALU.add).then_inc(added, 1)
                    dve.wait_ge(added, TILES)


def experts_choose(nc, X, xT, ident, w):
    constants, ident = ident, ident[0]
    E = w["WgT"].shape[-1]
    HF = w["W1T"].shape[-1]
    HB = HF // P
    CAP = S // E
    CB = CAP // P
    COPIES = P // E
    BITS = COPIES.bit_length() - 1
    PASSES = 32 // BITS
    INFO = 5
    rows_in = nc.dram_tensor("choice_rows_in", [S, D], F32).ap()
    rows_out = nc.dram_tensor("choice_rows_out", [S, D], F32).ap()

    with ExitStack() as outer:
        def keep(n, shape, dt=F32):
            return outer.enter_context(nc.sbuf_tensor(f"choice_{n}", shape, dt))

        token = keep("token", [P, E * CB], U32)
        weight = keep("weight", [P, E * CB])
        rows_stored = outer.enter_context(nc.semaphore("choice_rows_stored"))

        with ExitStack() as ctx:
            def sb(n, shape, dt=F32):
                return ctx.enter_context(nc.sbuf_tensor(f"choice_{n}", shape, dt))

            sem = ctx.enter_context(semaphores(nc, "choice"))

            wg = sb("wg", [P, DB, E])
            wg_rep = sb("wg_rep", [P, DB, E, COPIES])
            scores = sb("scores", [P, S])
            flags = sb("flags", [P, S], BF16)
            above, level, order, taken, rank, chances = (sb(n, [P, S]) for n in ("above", "level", "order", "taken", "rank", "chances"))
            shares = level
            ones = sb("ones", [P, S], BF16)
            part_i = sb("part_i", [P, 1], I32)
            step_i = sb("step_i", [P, 1], I32)
            step_pos = sb("step_pos", [P, 1])
            key, cand, unused, mask, bits, nibble = (sb(n, [P, 1], I32) for n in ("key", "cand", "unused", "mask", "bits", "nibble"))
            count, enough, found = sb("count", [P, 1]), sb("enough", [P, 1], BF16), sb("found", [P, 1])
            n_above, wanted, top, negtop, total, share = (sb(n, [P, 1]) for n in ("n_above", "wanted", "top", "negtop", "total", "share"))
            same = sb("same", [P, E, COPIES], BF16)
            slots1 = sb("slots1", [P, CAP], BF16)
            info = sb("info", [P, TILES, E, INFO], BF16)
            tile_no = sb("tile_no", [P, TILES])
            place_no = sb("place_no", [P, 1])
            rank_of = sb("rank_of", [P, TILES, E])
            chance = sb("chance", [P, TILES, E])
            rest1, rest2 = sb("rest1", [P, TILES, E]), sb("rest2", [P, TILES, E])
            hot = [sb(f"hot{h}", [P, CAP], BF16) for h in range(4)]
            slot_info = sb("slot_info", [P, E * CB, INFO])
            tok_f, tok_g, wsum = sb("tok_f", [P, E * CB]), sb("tok_g", [P, E * CB]), sb("wsum", [P, E * CB])
            score_ps = ctx.enter_context(nc.psum_tensor("choice_score_ps", [P, 4, 512], F32))
            nib_ps = ctx.enter_context(nc.psum_tensor("choice_nib_ps", [P, 512], F32))
            turned = [ctx.enter_context(nc.psum_tensor(f"choice_turned{h}", [P, 4, P], F32)) for h in range(2)]
            info_ps = ctx.enter_context(nc.psum_tensor("choice_info_ps", [P, E * CB, INFO], F32))
            loaded, wg_ready, scores_ready, scores_kept, made, same_ready = (sem(n) for n in ("loaded", "wg_ready", "scores_ready", "scores_kept", "made", "same_ready"))
            chained, enough_ready, nibble_ready, negtop_ready, chances_ready = (sem(n) for n in ("chained", "enough_ready", "nibble_ready", "negtop_ready", "chances_ready"))
            rank_ready, turned_ready, turned_kept, hot_ready, hot_used, shares_ready = (
                sem(n) for n in ("rank_ready", "turned_ready", "turned_kept", "hot_ready", "hot_used", "shares_ready"))

            with nc.Block() as block:
                @block.sync
                def _(sp):
                    sp.dma_start(wg[:], w["WgT"]).then_inc(loaded, 16)
                    sp.dma_start(rows_in.rearrange("(t p) d -> p t d", p=P), X[:]).then_inc(rows_stored, 16)
                    sp.dma_start(rows_out.rearrange("(t p) d -> p t d", p=P), X[:]).then_inc(rows_stored, 16)

                @block.gpsimd
                def _(pool):
                    exact = dict(allow_small_or_imprecise_dtypes=True)
                    nc.gpsimd.iota(part_i[:], [[0, 1]], base=0, channel_multiplier=1).then_inc(made, 1)
                    nc.gpsimd.iota(tile_no[:], [[1, TILES]], base=0, channel_multiplier=0, **exact).then_inc(made, 1)
                    nc.gpsimd.iota(place_no[:], [[0, 1]], base=0, channel_multiplier=1, **exact).then_inc(made, 1)
                    nc.gpsimd.iota(slots1[:], [[1, CAP]], base=1, channel_multiplier=0, **exact).then_inc(made, 1)
                    nc.gpsimd.memset(ones[:], 1.0).then_inc(made, 1)
                    nc.gpsimd.memset(same[:], 1.0).then_inc(same_ready, 1)
                    pool.wait_ge(same_ready, 1)
                    nc.gpsimd.affine_select(out=same[:], in_=same[:], compare_op=ALU.is_ge, fill=0.0, base=0,
                                            pattern=[[-COPIES, E], [0, COPIES]], channel_multiplier=1).then_inc(same_ready, 1)
                    pool.wait_ge(same_ready, 2)
                    nc.gpsimd.affine_select(out=same[:], in_=same[:], compare_op=ALU.is_ge, fill=0.0, base=COPIES - 1,
                                            pattern=[[COPIES, E], [0, COPIES]], channel_multiplier=-1).then_inc(same_ready, 1)

                @block.tensor
                def _(pe):
                    pe.wait_ge(wg_ready, 1)
                    for c in range(4):
                        for b in range(DB):
                            last = nc.tensor.matmul(score_ps[:, c, :], wg_rep[:, b, :, :].rearrange("p e j -> p (e j)"),
                                                    xT[:, b, c * 512:(c + 1) * 512], start=(b == 0), stop=(b == DB - 1))
                    last.then_inc(scores_ready, 1)
                    pe.wait_ge(same_ready, 3)
                    for n in range(PASSES):
                        pe.wait_ge(enough_ready, n + 1)
                        nc.tensor.matmul(nib_ps[:, 0:1], same[:].rearrange("p e j -> p (e j)"), enough[:],
                                         start=True, stop=True).then_inc(nibble_ready, 1)
                    for n, (what, ready) in enumerate(((rank, rank_ready), (shares, shares_ready))):
                        pe.wait_ge(ready, 1)
                        for q in range(TILES // 4):
                            m = n * (TILES // 4) + q
                            if m >= 2:
                                pe.wait_ge(turned_kept, m - 1)
                            for t in range(4):
                                last = nc.tensor.transpose(turned[m % 2][:, t, :], what[:, (q * 4 + t) * P:(q * 4 + t + 1) * P], ident[:])
                            last.then_inc(turned_ready, 1)
                    for t in range(TILES):
                        for e in range(E):
                            m = t * E + e
                            pe.wait_ge(hot_ready, m + 1)
                            for c in range(CB):
                                last = nc.tensor.matmul(info_ps[:, e * CB + c, :], hot[m % 4][:, c * P:(c + 1) * P], info[:, t, e, :],
                                                        start=(m == 0 and c == 0), stop=(m == TILES * E - 1 and c == CB - 1),
                                                        skip_group_check=True)
                            last.then_inc(hot_used, 1)

                @block.scalar
                def _(act):
                    act.wait_ge(scores_ready, 1)
                    nc.scalar.activation(scores[:], score_ps[:].rearrange("p a b -> p (a b)"), ACT.Identity).then_inc(scores_kept, 1)
                    act.wait_ge(negtop_ready, 1)
                    nc.scalar.activation(chances[:], scores[:], ACT.Exp, bias=negtop[:]).then_inc(chances_ready, 1)

                @block.vector
                def _(dve):
                    done = [0]

                    def link(ins):
                        done[0] += 1
                        ins.then_inc(chained, 1)
                        dve.wait_ge(chained, done[0])

                    V = nc.vector
                    dve.wait_ge(loaded, 16)
                    V.tensor_copy(wg_rep[:], wg[:].unsqueeze(3).broadcast_to([P, DB, E, COPIES])).then_inc(wg_ready, 1)
                    dve.wait_ge(made, 5)
                    link(V.tensor_scalar(step_i[:], part_i[:], COPIES - 1, None, ALU.bitwise_and))
                    link(V.tensor_copy(step_pos[:], step_i[:]))
                    link(V.tensor_scalar(step_pos[:], step_pos[:], 0.0, None, ALU.is_gt))
                    link(V.memset(key[:], 0))
                    link(V.tensor_scalar(unused[:], step_pos[:], -1.0, 1.0, ALU.mult, ALU.add))
                    link(V.tensor_scalar(unused[:], unused[:], 31, None, ALU.logical_shift_left))

                    def decode():
                        link(V.tensor_scalar(mask[:], cand[:], 31, -1, ALU.arith_shift_right, ALU.bitwise_xor))
                        link(V.tensor_scalar(mask[:], mask[:], -2 ** 31, None, ALU.bitwise_or))
                        link(V.tensor_tensor(bits[:], mask[:], cand[:], ALU.bitwise_xor))

                    dve.wait_ge(scores_kept, 1)
                    link(V.tensor_reduce(top[:], scores[:], AX_X, ALU.max))
                    V.tensor_scalar(negtop[:], top[:], -1.0, None, ALU.mult).then_inc(negtop_ready, 1)
                    for n in range(PASSES):
                        shift = 32 - BITS * (n + 1)
                        link(V.scalar_tensor_tensor(out=cand[:], in0=step_i[:], scalar=shift, in1=key[:],
                                                    op0=ALU.logical_shift_left, op1=ALU.bitwise_or))
                        link(V.tensor_tensor(cand[:], cand[:], unused[:], ALU.bitwise_or))
                        decode()
                        link(V.tensor_scalar(flags[:], scores[:], bits[:].bitcast(F32), 0.0, ALU.is_ge, ALU.add, accum_out=count[:]))
                        V.tensor_scalar(enough[:], count[:], CAP - 0.5, step_pos[:], ALU.is_gt, ALU.mult).then_inc(enough_ready, 1)
                        dve.wait_ge(nibble_ready, n + 1)
                        link(V.tensor_copy(nibble[:], nib_ps[:, 0:1]))
                        link(V.scalar_tensor_tensor(out=key[:], in0=nibble[:], scalar=shift, in1=key[:],
                                                    op0=ALU.logical_shift_left, op1=ALU.bitwise_or))
                    link(V.tensor_copy(cand[:], key[:]))
                    decode()
                    link(V.tensor_copy(found[:], bits[:].bitcast(F32)))
                    link(V.tensor_scalar(above[:], scores[:], found[:], 0.0, ALU.is_gt, ALU.add, accum_out=n_above[:]))
                    link(V.tensor_scalar(level[:], scores[:], found[:], None, ALU.is_equal))
                    link(V.tensor_scalar(wanted[:], n_above[:], -1.0, CAP + 0.5, ALU.mult, ALU.add))
                    link(V.tensor_tensor_scan(order[:], ones[:], level[:], 0.0, ALU.mult, ALU.add))
                    link(V.scalar_tensor_tensor(out=taken[:], in0=order[:], scalar=wanted[:], in1=level[:], op0=ALU.is_lt, op1=ALU.mult))
                    link(V.tensor_tensor(taken[:], taken[:], above[:], ALU.add))
                    link(V.tensor_tensor_scan(order[:], ones[:], taken[:], 0.0, ALU.mult, ALU.add))
                    V.tensor_tensor(rank[:], order[:], taken[:], ALU.mult).then_inc(rank_ready, 1)
                    dve.wait_ge(chances_ready, 1)
                    link(V.tensor_tensor(above[:], chances[:], taken[:], ALU.mult))
                    link(V.tensor_reduce(total[:], above[:], AX_X, ALU.add))
                    link(V.reciprocal(share[:], total[:]))
                    V.tensor_scalar(shares[:], chances[:], share[:], None, ALU.mult).then_inc(shares_ready, 1)
                    for n, to in enumerate((rank_of, chance)):
                        for q in range(TILES // 4):
                            m = n * (TILES // 4) + q
                            dve.wait_ge(turned_ready, m + 1)
                            V.tensor_copy(to[:, q * 4:q * 4 + 4, :], turned[m % 2][:].rearrange("p t (e j) -> p t e j", j=COPIES)[:, :, :, 0]).then_inc(turned_kept, 1)
                    dve.wait_ge(turned_kept, TILES // 2)
                    TE = [P, TILES, E]
                    link(V.tensor_copy(info[:, :, :, 0], tile_no[:].unsqueeze(2).broadcast_to(TE)))
                    link(V.tensor_copy(info[:, :, :, 1], place_no[:].unsqueeze(2).broadcast_to(TE)))
                    link(V.tensor_copy(info[:, :, :, 2], chance[:]))
                    link(V.tensor_tensor(rest1[:], chance[:], info[:, :, :, 2], ALU.subtract))
                    link(V.tensor_copy(info[:, :, :, 3], rest1[:]))
                    link(V.tensor_tensor(rest2[:], rest1[:], info[:, :, :, 3], ALU.subtract))
                    link(V.tensor_copy(info[:, :, :, 4], rest2[:]))
                    for t in range(TILES):
                        for e in range(E):
                            m = t * E + e
                            if m >= 4:
                                dve.wait_ge(hot_used, m - 3)
                            V.tensor_scalar(hot[m % 4][:], slots1[:], rank_of[:, t, e:e + 1], None, ALU.is_equal).then_inc(hot_ready, 1)
                    dve.wait_ge(hot_used, TILES * E)
                    link(V.tensor_copy(slot_info[:], info_ps[:]))
                    link(V.tensor_scalar(tok_f[:], slot_info[:, :, 0], float(P), None, ALU.mult))
                    link(V.tensor_tensor(tok_g[:], tok_f[:], slot_info[:, :, 1], ALU.add))
                    link(V.tensor_copy(token[:], tok_g[:]))
                    link(V.tensor_tensor(wsum[:], slot_info[:, :, 2], slot_info[:, :, 3], ALU.add))
                    link(V.tensor_tensor(weight[:], wsum[:], slot_info[:, :, 4], ALU.add))

        with ExitStack() as ctx:
            def sb(n, shape, dt=F32):
                return ctx.enter_context(nc.sbuf_tensor(f"choice_{n}", shape, dt))

            def ps(n, shape, dt=F32):
                return ctx.enter_context(nc.psum_tensor(f"choice_{n}", shape, dt))

            sem = ctx.enter_context(semaphores(nc, "choice"))

            W1 = [sb(f"W1_{h}", [P, DB, HF]) for h in range(2)]
            W3 = [sb(f"W3_{h}", [P, DB, HF]) for h in range(2)]
            W2 = [sb(f"W2_{h}", [P, HB, D]) for h in range(2)]
            rows = [sb(f"rows{h}", [P, CB, D]) for h in range(2)]
            rowsT = [sb(f"rowsT{h}", [P, DB, CAP]) for h in range(2)]
            gate = sb("gate", [P, HB, CAP])
            hidden = [sb(f"hidden{h}", [P, HB, CAP]) for h in range(2)]
            answer = [sb(f"answer{h}", [P, CB, D]) for h in range(2)]
            rowsT_ps = ps("rowsT_ps", [P, DB, CAP])
            gate_ps = ps("gate_ps", [P, HB, CAP])
            up_ps = ps("up_ps", [P, HB, CAP])
            answer_ps = [ps(f"answer_ps{h}", [P, CB, D]) for h in range(2)]
            W_loaded = [sem(f"W_loaded{h}") for h in range(2)]
            fetched = [sem(f"fetched{h}") for h in range(2)]
            rowsT_ready, rowsT_kept, gate_ready, up_ready, gate_kept, hidden_ready, answer_ready, answer_kept, scattered = (
                sem(n) for n in ("rowsT_ready", "rowsT_kept", "gate_ready", "up_ready", "gate_kept", "hidden_ready", "answer_ready", "answer_kept", "scattered"))
            rows_back = sem("rows_back")

            with nc.Block() as block:
                @block.sync
                def _(sp):
                    def load(e, h):
                        for to, what in ((W1[h], w["W1T"]), (W3[h], w["W3T"]), (W2[h], w["W2T"])):
                            sp.dma_start(to[:], what[:, bass.ds(e, 1), :, :].rearrange("p a b c -> p (a b) c")).then_inc(W_loaded[h], 16)
                    load(0, 0)
                    load(1, 1)
                    with sp.Fori(0, E // 2 - 1) as i:
                        for h in range(2):
                            sp.wait_ge(answer_ready, i * 2 + (h + 1))
                            load(i * 2 + (h + 2), h)
                    sp.wait_ge(scattered, E * CB * 16)
                    sp.dma_start(X[:], rows_out.rearrange("(t p) d -> p t d", p=P)).then_inc(rows_back, 16)
                    sp.wait_ge(rows_back, 16)

                @block.gpsimd
                def _(pool):
                    def fetch(e):
                        for c in range(CB):
                            nc.gpsimd.indirect_dma_start(rows[e % 2][:, c, :], None, rows_in,
                                                         bass.IndirectOffsetOnAxis(ap=token[:, e * CB + c:e * CB + c + 1], axis=0)).then_inc(fetched[e % 2], 16)
                    pool.wait_ge(rows_stored, 32)
                    fetch(0)
                    fetch(1)
                    for e in range(E):
                        if e + 2 < E:
                            pool.wait_ge(rowsT_ready, e + 1)
                            fetch(e + 2)
                        pool.wait_ge(answer_kept, e * CB + CB)
                        if e:
                            pool.wait_ge(scattered, e * CB * 16)
                        for c in range(CB):
                            nc.gpsimd.indirect_dma_start(rows_out, bass.IndirectOffsetOnAxis(ap=token[:, e * CB + c:e * CB + c + 1], axis=0),
                                                         answer[e % 2][:, c, :], None, compute_op=ALU.add).then_inc(scattered, 16)

                @block.tensor
                def _(pe):
                    def turn(e, j, h):
                        pe.wait_ge(fetched[h], j * CB * 16 + CB * 16)
                        for b in range(DB):
                            for c in range(CB):
                                last = nc.tensor.transpose(rowsT_ps[:, b, c * P:(c + 1) * P], rows[h][:, c, b * P:(b + 1) * P], ident[:])
                        last.then_inc(rowsT_ready, 1)

                    def step(e, j, h, more):
                        pe.wait_ge(W_loaded[h], j * 48 + 48)
                        pe.wait_ge(rowsT_kept, e + 1)
                        for W, to, ready in ((W1, gate_ps, gate_ready), (W3, up_ps, up_ready)):
                            for f in range(HB):
                                for b in range(DB):
                                    last = nc.tensor.matmul(to[:, f, :], W[h][:, b, f * P:(f + 1) * P], rowsT[h][:, b, :],
                                                            start=(b == 0), stop=(b == DB - 1))
                            last.then_inc(ready, 1)
                        if more:
                            turn(e + 1, j + h, 1 - h)
                        pe.wait_ge(hidden_ready, e + 1)
                        for c in range(CB):
                            for f in range(HB):
                                last = nc.tensor.matmul(answer_ps[h][:, c, :], hidden[h][:, f, c * P:(c + 1) * P], W2[h][:, f, :],
                                                        start=(f == 0), stop=(f == HB - 1))
                        last.then_inc(answer_ready, 1)

                    turn(0, 0, 0)
                    with pe.Fori(0, E // 2 - 1) as i:
                        for h in range(2):
                            step(i * 2 + h, i, h, True)
                    step(E - 2, E // 2 - 1, 0, True)
                    step(E - 1, E // 2 - 1, 1, False)

                @block.scalar
                def _(act):
                    def keep_rows(e, h):
                        act.wait_ge(rowsT_ready, e + 1)
                        nc.scalar.activation(rowsT[h][:], rowsT_ps[:], ACT.Identity).then_inc(rowsT_kept, 1)

                    def step(e, h, more):
                        act.wait_ge(gate_ready, e + 1)
                        nc.scalar.activation(gate[:], gate_ps[:], ACT.Silu).then_inc(gate_kept, 1)
                        if more:
                            keep_rows(e + 1, 1 - h)
                        act.wait_ge(hidden_ready, e + 1)

                    keep_rows(0, 0)
                    with act.Fori(0, E // 2 - 1) as i:
                        for h in range(2):
                            step(i * 2 + h, h, True)
                    step(E - 2, 0, True)
                    step(E - 1, 1, False)

                @block.vector
                def _(dve):
                    for e in range(E):
                        h = e % 2
                        dve.wait_ge(up_ready, e + 1)
                        dve.wait_ge(gate_kept, e + 1)
                        nc.vector.tensor_tensor(hidden[h][:], gate[:], up_ps[:], ALU.mult).then_inc(hidden_ready, 1)
                        dve.wait_ge(answer_ready, e + 1)
                        if e >= 2:
                            dve.wait_ge(scattered, (e - 1) * CB * 16)
                        for c in range(CB):
                            nc.vector.tensor_scalar(answer[h][:, c, :], answer_ps[h][:, c, :], weight[:, e * CB + c:e * CB + c + 1],
                                                    None, ALU.mult).then_inc(answer_kept, 1)
    return constants


def load_tokens(nc, X, x):
    with nc.semaphore("tokens_loaded") as loaded, nc.Block() as block:
        @block.sync
        def _(sp):
            sp.dma_start(X[:], x).then_inc(loaded, 16)
            sp.wait_ge(loaded, 16)


def store_x(nc, X, out):
    stored = nc.semaphore("stored")
    with stored as stored:
        with nc.Block() as block:
            @block.sync
            def _(sp):
                sp.dma_start(out.rearrange("a (t p) d -> p (a t) d", p=P), X[:]).then_inc(stored, 16)
                sp.wait_ge(stored, 16)


def program(nc, a, out):
    with ExitStack() as keep:
        X = keep.enter_context(nc.sbuf_tensor("X", [P, TILES, D], F32))
        xT = keep.enter_context(nc.sbuf_tensor("xT", [P, DB, S], F32))
        ident = make_identity(nc, keep)
        load_tokens(nc, X, a["x"])
        names = ("gamma", "beta", "W_in", "conv_w", "conv_b", "W_x", "W_dt", "b_dt", "A_log", "D_skip", "W_out")
        state_space(nc, X, xT, ident, {n: a["L0_attn_" + n] for n in names})
        normalise(nc, "first_norm", X, xT, ident)
        attend_context(nc, X, xT, ident, a["contextT"], a["L0_xattn_W_outT"])
        normalise(nc, "context_norm", X, xT, ident)
        names = ("router_W", "router_b", "ln_g", "ln_b", "W1", "b1", "W2", "b2")
        route_to_two(nc, X, xT, ident, {n: a["L0_ffn_" + n] for n in names})
        self_attention_of_one(nc, X, xT, ident, a["L1_attn_wv"], a["L1_attn_woT"], a["L1_attn_bv"], a["L1_attn_bo"])
        normalise(nc, "one_norm", X, xT, ident)
        names = ("w_qT", "w_kT", "w_vT", "w_oT")
        attend_heads(nc, X, xT, ident, {n: a["L1_xattn_" + n] for n in names} | {"contextT": a["contextT"]})
        normalise(nc, "heads_norm", X, xT, ident)
        names = ("WgT", "W1T", "W2T", "W3T")
        experts_choose(nc, X, xT, ident, {n: a["L1_ffn_" + n] for n in names})
        normalise(nc, "last_norm", X, xT, ident, hat=X[:])
        store_x(nc, X, out)


def by_partition(a):
    a = a.reshape(*a.shape[:-2], a.shape[-2] // P, P, a.shape[-1])
    return np.ascontiguousarray(np.moveaxis(a, -2, 0))


def columns(v):
    v = v.reshape(*v.shape[:-1], v.shape[-1] // P, P)
    return np.ascontiguousarray(np.moveaxis(v, -1, 0))


def layout(i):
    t = lambda a: np.swapaxes(a, -1, -2)
    return {
        "x": by_partition(i["x"][0]),
        "contextT": by_partition(t(i["ctx_1024"][0])),
        "L0_xattn_W_outT": by_partition(t(i["L0_xattn_W_out"])),
        "L0_ffn_router_W": by_partition(i["L0_ffn_router_W"]),
        "L0_ffn_router_b": i["L0_ffn_router_b"].reshape(-1, 1),
        "L0_ffn_ln_g": columns(i["L0_ffn_ln_g"]),
        "L0_ffn_ln_b": columns(i["L0_ffn_ln_b"]),
        "L0_ffn_W1": by_partition(i["L0_ffn_W1"]),
        "L0_ffn_b1": i["L0_ffn_b1"],
        "L0_ffn_W2": by_partition(i["L0_ffn_W2"]),
        "L0_ffn_b2": i["L0_ffn_b2"],
        "L1_ffn_WgT": by_partition(t(i["L1_ffn_Wg"])),
        "L1_ffn_W1T": by_partition(t(i["L1_ffn_W1"])),
        "L1_ffn_W3T": by_partition(t(i["L1_ffn_W3"])),
        "L1_ffn_W2T": by_partition(t(i["L1_ffn_W2"])),
        "L1_xattn_w_qT": by_partition(t(i["L1_xattn_w_q"])),
        "L1_xattn_w_kT": by_partition(t(i["L1_xattn_w_k"])),
        "L1_xattn_w_vT": by_partition(t(i["L1_xattn_w_v"])),
        "L1_xattn_w_oT": by_partition(t(i["L1_xattn_w_o"])),
        "L0_attn_gamma": columns(i["L0_attn_gamma"]),
        "L0_attn_beta": columns(i["L0_attn_beta"]),
        "L0_attn_W_in": by_partition(i["L0_attn_W_in"]),
        "L0_attn_conv_w": by_partition(i["L0_attn_conv_w"]),
        "L0_attn_conv_b": columns(i["L0_attn_conv_b"]),
        "L0_attn_W_x": by_partition(i["L0_attn_W_x"]),
        "L0_attn_W_dt": i["L0_attn_W_dt"],
        "L0_attn_b_dt": columns(i["L0_attn_b_dt"]),
        "L0_attn_A_log": by_partition(i["L0_attn_A_log"]),
        "L0_attn_D_skip": columns(i["L0_attn_D_skip"]),
        "L0_attn_W_out": by_partition(i["L0_attn_W_out"]),
        "L1_attn_wv": by_partition(i["L1_attn_wv"]),
        "L1_attn_woT": by_partition(t(i["L1_attn_wo"])),
        "L1_attn_bv": columns(i["L1_attn_bv"]),
        "L1_attn_bo": columns(i["L1_attn_bo"]),
    }


def kernel(**inputs):
    import numpy as _np
    import concourse.bacc as _bacc
    from concourse import mybir as _mybir
    from concourse.bass_utils import run_bass_kernel_spmd as _run

    nc = _bacc.Bacc("TRN2", target_bir_lowering=False, num_devices=1)
    arrays, args = {}, {}
    for name, a in layout({n: _np.asarray(v) for n, v in inputs.items()}).items():
        a = _np.ascontiguousarray(a)
        arrays[f"in_{name}_dram"] = a
        args[name] = nc.dram_tensor(f"in_{name}_dram", a.shape, _mybir.dt.from_np(a.dtype), kind="ExternalInput").ap()
    out = nc.dram_tensor("out_0_dram", inputs["x"].shape, F32, kind="ExternalOutput").ap()
    program(nc, args, out)
    if not nc.is_finalized():
        nc.finalize()
    r = _run(nc, [arrays], core_ids=[0])
    return r.results[0]["out_0_dram"]
```

```python
from contextlib import ExitStack, contextmanager

import concourse.bass as bass
import numpy as np
from concourse import mybir

F32 = mybir.dt.float32
F32R = mybir.dt.float32r
BF16 = mybir.dt.bfloat16
I32 = mybir.dt.int32
U32 = mybir.dt.uint32
ALU = mybir.AluOpType
ACT = mybir.ActivationFunctionType
AX_X = mybir.AxisListType.X

P = 128
S = 2048
D = 256
DB = D // P
TILES = S // P
GT = 4
GS = GT * P
GROUPS = S // GS
EPS = 1e-5


@contextmanager
def semaphores(nc, name):
    taken = []

    def sem(n):
        taken.append(nc.alloc_semaphore(f"{name}_{n}"))
        return taken[-1]

    yield sem
    nc.clear_and_free_semaphores(taken)
    nc.all_engine_barrier()


def make_identity(nc, keep):
    zeroed = keep.enter_context(nc.semaphore("ident_zeroed"))
    built = keep.enter_context(nc.semaphore("ident_built"))
    ident = keep.enter_context(nc.sbuf_tensor("ident", [P, P], F32))
    eps = keep.enter_context(nc.sbuf_tensor("eps", [P, 1], F32))
    stats = keep.enter_context(nc.sbuf_tensor("stats", [P, TILES, 6], F32))
    with nc.Block() as block:
        @block.gpsimd
        def _(pool):
            nc.gpsimd.memset(ident[:], 0.0).then_inc(zeroed, 1)
            pool.wait_ge(zeroed, 1)
            nc.gpsimd.affine_select(out=ident[:], in_=ident[:], compare_op=ALU.not_equal, fill=1.0,
                                    base=0, pattern=[[-1, P]], channel_multiplier=1).then_inc(built, 1)
            nc.gpsimd.memset(eps[:], EPS).then_inc(built, 1)
            pool.wait_ge(built, 2)
    return ident, built, eps, stats


def tile_stats(nc, constants, X, t):
    def tile(a):
        return a[:, bass.ds(t, 1), :].rearrange("p a b -> p (a b)")

    return nc.vector.bn_stats(tile(constants[3]), tile(X))


def normalise(nc, name, X, xT, constants, to=None, affine=None, affine_loaded=None, arrived=None, out=None):
    ident, _, eps, stats = constants
    to = X if to is None else to
    BY_ACT = 1
    BY_DVE = GT - BY_ACT
    with ExitStack() as ctx:
        def sb(n, shape, dt=F32):
            return ctx.enter_context(nc.sbuf_tensor(f"{name}_{n}", shape, dt))

        sem = ctx.enter_context(semaphores(nc, name))

        turned = [ctx.enter_context(nc.psum_tensor(f"{name}_turned{g}", [P, DB, GS], F32)) for g in range(GROUPS if xT is not None else 0)]
        mean2, diff, spread, diff2, spread1, var, root, rstd, shift = (
            sb(n, [P, TILES]) for n in ("mean2", "diff", "spread", "diff2", "spread1", "var", "root", "rstd", "shift"))
        stats_ready, small, root_ready, shift_ready = sem("stats_ready"), sem("small"), sem("root_ready"), sem("shift_ready")
        normed_by_act, normed_by_dve = sem("normed_by_act"), sem("normed_by_dve")
        turned_ready, kept_by_act, kept_by_dve, stored = sem("turned_ready"), sem("kept_by_act"), sem("kept_by_dve"), sem("stored")

        def keep(activation, g, b):
            where = xT[:, b, g * GS:(g + 1) * GS]
            if activation:
                if affine is None:
                    return nc.scalar.activation(where, turned[g][:, b, :], ACT.Identity)
                return nc.scalar.activation(where, turned[g][:, b, :], ACT.Identity, bias=affine[1][:, b:b + 1], scale=affine[0][:, b:b + 1])
            if affine is None:
                return nc.vector.tensor_copy(where, turned[g][:, b, :])
            return nc.vector.tensor_scalar(where, turned[g][:, b, :], affine[0][:, b:b + 1], affine[1][:, b:b + 1], ALU.mult, ALU.add)

        with nc.Block() as block:
            @block.vector
            def _(dve):
                if arrived is not None:
                    for g in range(GROUPS):
                        dve.wait_ge(arrived[g], 16)
                        for t in range(g * GT, (g + 1) * GT):
                            nc.vector.bn_stats(stats[:, t, :], X[:, t, :]).then_inc(stats_ready, 1)
                    dve.wait_ge(stats_ready, TILES)
                nc.vector.tensor_tensor(mean2[:], stats[:, :, 1], stats[:, :, 4], ALU.add).then_inc(small, 1)
                nc.vector.tensor_tensor(diff[:], stats[:, :, 1], stats[:, :, 4], ALU.subtract).then_inc(small, 1)
                nc.vector.tensor_tensor(spread[:], stats[:, :, 2], stats[:, :, 5], ALU.add).then_inc(small, 1)
                dve.wait_ge(small, 3)
                nc.vector.tensor_tensor(diff2[:], diff[:], diff[:], ALU.mult).then_inc(small, 1)
                nc.vector.tensor_scalar(spread1[:], spread[:], 1.0 / D, None, ALU.mult).then_inc(small, 1)
                dve.wait_ge(small, 5)
                nc.vector.scalar_tensor_tensor(out=var[:], in0=diff2[:], scalar=0.25, in1=spread1[:], op0=ALU.mult,
                                               op1=ALU.add).then_inc(small, 1)
                dve.wait_ge(root_ready, 1)
                nc.vector.reciprocal(rstd[:], root[:]).then_inc(small, 1)
                dve.wait_ge(small, 7)
                nc.vector.scalar_tensor_tensor(out=shift[:], in0=mean2[:], scalar=-0.5, in1=rstd[:],
                                               op0=ALU.mult, op1=ALU.mult).then_inc(shift_ready, 1)
                dve.wait_ge(shift_ready, 1)
                if affine_loaded is not None:
                    dve.wait_ge(*affine_loaded)
                for g in range(GROUPS + 2):
                    if g < GROUPS:
                        for t in range(g * GT + BY_ACT, (g + 1) * GT):
                            nc.vector.tensor_scalar(to[:, t, :], X[:, t, :], rstd[:, t:t + 1], shift[:, t:t + 1],
                                                    ALU.mult, ALU.add).then_inc(normed_by_dve, 1)
                    if g >= 2 and xT is not None:
                        dve.wait_ge(turned_ready, (g - 1) * DB)
                        keep(False, g - 2, DB - 1).then_inc(kept_by_dve, 1)
                dve.wait_ge(normed_by_dve, BY_DVE * GROUPS)
                if xT is not None:
                    dve.wait_ge(kept_by_dve, GROUPS)

            @block.scalar
            def _(act):
                act.wait_ge(small, 6)
                nc.scalar.activation(root[:], var[:], ACT.Sqrt, bias=eps[:]).then_inc(root_ready, 1)
                act.wait_ge(shift_ready, 1)
                if affine_loaded is not None:
                    act.wait_ge(*affine_loaded)
                for g in range(GROUPS + 1):
                    if g < GROUPS:
                        for t in range(g * GT, g * GT + BY_ACT):
                            nc.scalar.activation(to[:, t, :], X[:, t, :], ACT.Identity, bias=shift[:, t:t + 1],
                                                 scale=rstd[:, t:t + 1]).then_inc(normed_by_act, 1)
                    if g >= 1 and xT is not None:
                        for b in range(DB - 1):
                            act.wait_ge(turned_ready, (g - 1) * DB + b + 1)
                            keep(True, g - 1, b).then_inc(kept_by_act, 1)
                act.wait_ge(normed_by_act, BY_ACT * GROUPS)
                if xT is not None:
                    act.wait_ge(kept_by_act, (DB - 1) * GROUPS)

            if out is not None:
                @block.sync
                def _(sp):
                    for g in range(GROUPS):
                        sp.wait_ge(normed_by_act, (g + 1) * BY_ACT)
                        sp.wait_ge(normed_by_dve, (g + 1) * BY_DVE)
                        sp.dma_start(out[:, g * GT:(g + 1) * GT, :], to[:, g * GT:(g + 1) * GT, :]).then_inc(stored, 16)
                    sp.wait_ge(stored, GROUPS * 16)

            if xT is None:
                return

            @block.tensor
            def _(pe):
                for g in range(GROUPS):
                    pe.wait_ge(normed_by_act, (g + 1) * BY_ACT)
                    pe.wait_ge(normed_by_dve, (g + 1) * BY_DVE)
                    for b in range(DB):
                        for t in range(GT):
                            last = nc.tensor.transpose(turned[g][:, b, t * P:(t + 1) * P], to[:, g * GT + t, b * P:(b + 1) * P], ident[:])
                        last.then_inc(turned_ready, 1)


def state_space(nc, X, xT, constants, w, x_arrived):
    ident = constants[0]
    DI = w["W_out"].shape[1] * P
    IB = DI // P
    NS = w["A_log"].shape[-1]
    TAPS = w["conv_w"].shape[-1]
    RANK = w["W_dt"].shape[0]
    C = 1024
    CHUNKS = S // C
    spread_dram = nc.dram_tensor("mamba_spread", [2 * NS, S], F32).ap()

    with ExitStack() as outer:
        def keep(n, shape, dt=F32):
            return outer.enter_context(nc.sbuf_tensor(f"mamba_{n}", shape, dt))

        inner = keep("inner", [P, IB, S + TAPS - 1])
        x = keep("x", [P, IB, S])
        dt = keep("dt", [P, IB, S])
        w_out = keep("w_out", [P, IB, D])
        w_gate = keep("w_gate", [P, DB, DI])
        gamma, beta = keep("gamma", [P, DB]), keep("beta", [P, DB])
        conv_w, conv_b, b_dt, skip = keep("conv_w", [P, IB, TAPS]), keep("conv_b", [P, IB]), keep("b_dt", [P, IB]), keep("skip", [P, IB])
        a_log = keep("a_log", [P, IB, NS])
        rate = keep("rate", [P, IB, NS])
        diag = keep("diag", [P, IB, P])
        wide_loaded = outer.enter_context(nc.semaphore("mamba_wide_loaded"))
        params = outer.enter_context(nc.semaphore("mamba_params"))
        PARAMS = 7
        dtx = inner[:, :, TAPS - 1:]
        y = dtx

        with nc.Block() as block:
            @block.sync
            def _(sp):
                for to, what in ((gamma, "gamma"), (beta, "beta"), (conv_w, "conv_w"), (conv_b, "conv_b"), (b_dt, "b_dt"),
                                 (skip, "D_skip"), (a_log, "A_log")):
                    sp.dma_start(to[:], w[what]).then_inc(params, 16)
                sp.dma_start(w_out[:], w["W_out"]).then_inc(wide_loaded, 16)
                sp.dma_start(w_gate[:], w["W_in"][:, :, DI:2 * DI]).then_inc(wide_loaded, 16)

        with ExitStack() as ctx:
            def sb(n, shape, dt_=F32):
                return ctx.enter_context(nc.sbuf_tensor(f"mamba_{n}", shape, dt_))

            loads, w_arrived = loads_ahead(nc, ctx, "mamba_first", {"w_in": w["W_in"][:, :, 0:DI], "w_x": w["W_x"], "w_dt": w["W_dt"]})
            w_in, w_x, w_dt = loads["w_in"], loads["w_x"], loads["w_dt"]
            normed = x[:].rearrange("p m s -> p (m s)")[:, 0:TILES * D].rearrange("p (t d) -> p t d", d=D)
            normalise(nc, "mamba_norm", X, xT, constants, to=normed, affine=(gamma, beta),
                      affine_loaded=(params, PARAMS * 16), arrived=x_arrived)

            sem = ctx.enter_context(semaphores(nc, "mamba"))

            small = sb("small", [RANK + 2 * NS, S])
            ps = ctx.enter_context(nc.psum_tensor("mamba_ps", [P, 8, 512], F32))
            inner_ps, inner_kept, padded, conv_done, convolved, x_ready, a_ready, rate_ready = (
                sem(n) for n in ("inner_ps", "inner_kept", "padded", "conv_done", "convolved", "x_ready", "a_ready", "rate_ready"))
            small_ps, small_kept, small_stored, dt_ps, positive, magnitude, logged, dt_ready, dtx_ready = (
                sem(n) for n in ("small_ps", "small_kept", "small_stored", "dt_ps", "positive", "magnitude", "logged", "dt_ready", "dtx_ready"))

            with nc.Block() as block:
                @block.sync
                def _(sp):
                    sp.wait_ge(small_kept, GROUPS)
                    sp.dma_start(spread_dram, small[RANK:, :]).then_inc(small_stored, 16)
                    sp.wait_ge(small_stored, 16)

                @block.tensor
                def _(pe):
                    pe.wait_ge(*w_arrived)
                    for m in range(IB):
                        half = 4 * (m % 2)
                        if m >= 2:
                            pe.wait_ge(inner_kept, m - 1)
                        for g in range(GROUPS):
                            for b in range(DB):
                                last = nc.tensor.matmul(ps[:, half + g, :], w_in[:, b, m * P:(m + 1) * P], xT[:, b, g * GS:(g + 1) * GS],
                                                        start=(b == 0), stop=(b == DB - 1))
                        last.then_inc(inner_ps, 1)
                    pe.wait_ge(inner_kept, IB - 1)
                    for m in range(IB):
                        pe.wait_ge(x_ready, m + 1)
                        for g in range(GROUPS):
                            last = nc.tensor.matmul(ps[0:RANK + 2 * NS, g, :], w_x[:, m, :], x[:, m, g * GS:(g + 1) * GS],
                                                    start=(m == 0), stop=(m == IB - 1))
                    last.then_inc(small_ps, 1)
                    for m in range(IB):
                        half = 4 * ((m + 1) % 2)
                        if m == 0:
                            pe.wait_ge(small_kept, GROUPS)
                        if m >= 2:
                            pe.wait_ge(positive, m - 1)
                            pe.wait_ge(magnitude, m - 1)
                        for g in range(GROUPS):
                            last = nc.tensor.matmul(ps[:, half + g, :], w_dt[:, m * P:(m + 1) * P], small[0:RANK, g * GS:(g + 1) * GS],
                                                    start=True, stop=True)
                        last.then_inc(dt_ps, 1)

                @block.scalar
                def _(act):
                    act.wait_ge(params, PARAMS * 16)
                    for m in range(IB + 1):
                        if m < IB:
                            act.wait_ge(inner_ps, m + 1)
                            nc.scalar.activation(inner[:, m, TAPS - 1:], ps[:, 4 * (m % 2):4 * (m % 2) + 4, :].rearrange("p a b -> p (a b)"),
                                                 ACT.Identity).then_inc(inner_kept, 1)
                        if m:
                            act.wait_ge(convolved, m)
                            nc.scalar.activation(x[:, m - 1, :], dt[:, m - 1, :], ACT.Silu, bias=conv_b[:, m - 1:m]).then_inc(x_ready, 1)
                    act.wait_ge(small_ps, 1)
                    for g in range(GROUPS):
                        nc.scalar.activation(small[:, g * GS:(g + 1) * GS], ps[0:RANK + 2 * NS, g, :], ACT.Identity).then_inc(small_kept, 1)
                    for m in range(IB):
                        half = 4 * ((m + 1) % 2)
                        act.wait_ge(positive, m + 1)
                        nc.scalar.activation(dt[:, m, :], ps[:, half:half + 4, :].rearrange("p a b -> p (a b)"), ACT.Abs,
                                             bias=b_dt[:, m:m + 1]).then_inc(magnitude, 1)
                        act.wait_ge(magnitude, m + 1)
                        nc.scalar.activation(dt[:, m, :], dt[:, m, :], ACT.Exp, scale=-1.0).then_inc(a_ready, 1)
                    nc.scalar.activation(rate[:], a_log[:], ACT.Exp).then_inc(rate_ready, 1)
                    for m in range(IB):
                        act.wait_ge(a_ready, m + 1)
                        nc.scalar.activation(dt[:, m, :], dt[:, m, :], ACT.Ln, bias=1.0).then_inc(logged, 1)

                @block.vector
                def _(dve):
                    dve.wait_ge(params, PARAMS * 16)
                    nc.vector.memset(inner[:, :, 0:TAPS - 1], 0.0).then_inc(padded, 1)
                    dve.wait_ge(padded, 1)
                    for m in range(IB):
                        dve.wait_ge(inner_kept, m + 1)
                        nc.vector.tensor_scalar(diag[:, m, :], ident[:], skip[:, m:m + 1], None, ALU.mult).then_inc(padded, 1)
                        nc.vector.tensor_scalar(dt[:, m, :], inner[:, m, 0:S], conv_w[:, m, 0:1], None, ALU.mult).then_inc(conv_done, 1)
                        for k in range(1, TAPS):
                            dve.wait_ge(conv_done, m * (TAPS - 1) + k)
                            nc.vector.scalar_tensor_tensor(out=dt[:, m, :], in0=inner[:, m, k:k + S], scalar=conv_w[:, m, k:k + 1],
                                                           in1=dt[:, m, :], op0=ALU.mult, op1=ALU.add).then_inc(
                                                               convolved if k == TAPS - 1 else conv_done, 1)
                    for m in range(IB):
                        half = 4 * ((m + 1) % 2)
                        dve.wait_ge(dt_ps, m + 1)
                        nc.vector.tensor_scalar(dtx[:, m, :], ps[:, half:half + 4, :].rearrange("p a b -> p (a b)"), b_dt[:, m:m + 1], 0.0,
                                                ALU.add, ALU.max).then_inc(positive, 1)
                    dve.wait_ge(rate_ready, 1)
                    nc.vector.tensor_scalar(rate[:], rate[:], -1.0, None, ALU.mult).then_inc(rate_ready, 1)
                    dve.wait_ge(positive, IB)
                    for m in range(IB):
                        dve.wait_ge(logged, m + 1)
                        nc.vector.tensor_tensor(dt[:, m, :], dt[:, m, :], dtx[:, m, :], ALU.add).then_inc(dt_ready, 1)
                        dve.wait_ge(dt_ready, m + 1)
                        nc.vector.tensor_tensor(dtx[:, m, :], dt[:, m, :], x[:, m, :], ALU.mult).then_inc(dtx_ready, 1)
                    dve.wait_ge(dtx_ready, IB)

        with ExitStack() as ctx:
            def sb(n, shape, dt_=F32):
                return ctx.enter_context(nc.sbuf_tensor(f"mamba_{n}", shape, dt_))

            sem = ctx.enter_context(semaphores(nc, "mamba"))

            NB = IB
            ND = 2
            decay = [sb(f"decay{m}", [P, C]) for m in range(ND)]
            drive = [sb(f"drive{m}", [P, C]) for m in range(ND)]
            state = [sb(f"state{m}", [P, C]) for m in range(NB)]
            read = [sb(f"read{m}", [P, C]) for m in range(NB)]
            b_all = [sb(f"b_all{h}", [P, C]) for h in range(2)]
            c_all = [sb(f"c_all{h}", [P, C]) for h in range(2)]
            carry = sb("carry", [P, NS, IB])
            y_ps = ctx.enter_context(nc.psum_tensor("mamba_y_ps", [P, IB, C], F32))
            b_loaded = [sem(f"b_loaded{h}") for h in range(2)]
            c_loaded = [sem(f"c_loaded{h}") for h in range(2)]
            decay_ready, drive_ready, state_ready, read_ready, summed, carry_zeroed, carried, y_kept = (
                sem(n) for n in ("decay_ready", "drive_ready", "state_ready", "read_ready", "summed", "carry_zeroed", "carried",
                                 "y_kept"))
            PER = NS * IB

            def states(eng, c, body):
                with eng.Fori(0, NS // 2) as i:
                    for h in range(2):
                        body(i * 2 + h, h, i)

            with nc.Block() as block:
                @block.sync
                def _(sp):
                    def load(c, state_no, h):
                        cols = slice(c * C, (c + 1) * C)
                        sp.dma_start(b_all[h][:], spread_dram[bass.ds(state_no, 1), cols].broadcast_to([P, C])).then_inc(b_loaded[h], 16)
                        sp.dma_start(c_all[h][:], spread_dram[bass.ds(state_no + NS, 1), cols].broadcast_to([P, C])).then_inc(c_loaded[h], 16)
                    for c in range(CHUNKS):
                        for h in range(2):
                            if c:
                                sp.wait_ge(read_ready, c * PER - (1 - h) * IB + NB)
                            load(c, h, h)
                        with sp.Fori(0, NS // 2 - 1) as i:
                            for h in range(2):
                                sp.wait_ge(read_ready, i * (2 * IB) + (c * PER + (h + 1) * IB + NB))
                                load(c, i * 2 + (h + 2), h)

                @block.tensor
                def _(pe):
                    pe.sem_inc(summed, NB)
                    for c in range(CHUNKS):
                        for m in range(IB):
                            if c:
                                pe.wait_ge(y_kept, (c - 1) * IB + m + 1)
                            for q in range(C // 512):
                                nc.tensor.matmul(y_ps[:, m, q * 512:(q + 1) * 512], diag[:, m, :], x[:, m, c * C + q * 512:c * C + (q + 1) * 512],
                                                 start=True, stop=False, skip_group_check=True)

                        def body(state_no, h, i):
                            for m in range(IB):
                                pe.wait_ge(read_ready, state_no * IB + (c * PER + m + 1 + NB))
                                for q in range(C // 512):
                                    last = nc.tensor.matmul(y_ps[:, m, q * 512:(q + 1) * 512], ident[:], read[m][:, q * 512:(q + 1) * 512],
                                                            start=False, stop=False, skip_group_check=True)
                                last.then_inc(summed, 1)
                        states(pe, c, body)

                @block.scalar
                def _(act):
                    for c in range(CHUNKS):
                        def body(state_no, h, i):
                            for m in range(IB):
                                act.wait_ge(state_ready, state_no * IB + (c * PER + m + 1 + NB - ND))
                                nc.scalar.activation(decay[m % ND][:], dt[:, m, c * C:(c + 1) * C], ACT.Exp,
                                                     scale=rate[:, m, bass.ds(state_no, 1)]).then_inc(decay_ready, 1)
                        states(act, c, body)
                        for m in range(IB):
                            act.wait_ge(summed, (c + 1) * PER - IB + m + 1 + NB)
                            nc.scalar.activation(y[:, m, c * C:(c + 1) * C], y_ps[:, m, :], ACT.Identity).then_inc(y_kept, 1)
                    act.wait_ge(y_kept, CHUNKS * IB)

                @block.vector
                def _(dve):
                    dve.sem_inc(state_ready, NB)
                    nc.vector.memset(carry[:], 0.0).then_inc(carry_zeroed, 1)
                    dve.wait_ge(carry_zeroed, 1)
                    for c in range(CHUNKS):
                        def body(state_no, h, i):
                            def drive_of(m):
                                dve.wait_ge(state_ready, state_no * IB + (c * PER + m + 1 + NB - ND))
                                nc.vector.tensor_tensor(drive[m % ND][:], dtx[:, m, c * C:(c + 1) * C], b_all[h][:], ALU.mult).then_inc(drive_ready, 1)

                            def scan(m):
                                dve.wait_ge(drive_ready, state_no * IB + (c * PER + m + 1))
                                dve.wait_ge(decay_ready, state_no * IB + (c * PER + m + 1))
                                dve.wait_ge(read_ready, state_no * IB + (c * PER + m + 1))
                                if c == 0:
                                    dve.wait_ge(carried, state_no * IB + (m + 1))
                                nc.vector.tensor_tensor_scan(state[m][:], decay[m % ND][:], drive[m % ND][:],
                                                             carry[:, bass.ds(state_no, 1), m], ALU.mult, ALU.add).then_inc(state_ready, 1)

                            dve.wait_ge(b_loaded[h], i * 16 + (c * (NS // 2) * 16 + 16))
                            drive_of(0)
                            drive_of(1)
                            scan(0)
                            drive_of(2)
                            scan(1)
                            drive_of(3)
                            scan(2)
                            scan(3)
                        if c:
                            dve.wait_ge(carried, NB + PER)
                        states(dve, c, body)

                @block.gpsimd
                def _(pool):
                    pool.sem_inc(read_ready, NB)
                    pool.sem_inc(carried, NB)
                    for c in range(CHUNKS):
                        def body(state_no, h, i):
                            pool.wait_ge(c_loaded[h], i * 16 + (c * (NS // 2) * 16 + 16))
                            for m in range(IB):
                                pool.wait_ge(state_ready, state_no * IB + (c * PER + m + 1 + NB))
                                if c == 0:
                                    nc.gpsimd.tensor_copy(carry[:, bass.ds(state_no, 1), m], state[m][:, C - 1:C]).then_inc(carried, 1)
                                pool.wait_ge(summed, state_no * IB + (c * PER + m + 1))
                                nc.gpsimd.tensor_tensor(read[m][:], state[m][:], c_all[h][:], ALU.mult).then_inc(read_ready, 1)
                        states(pool, c, body)

        with ExitStack() as ctx:
            def sb(n, shape, dt_=F32):
                return ctx.enter_context(nc.sbuf_tensor(f"mamba_{n}", shape, dt_))

            sem = ctx.enter_context(semaphores(nc, "mamba"))

            gate = [sb(f"gate{h}", [P, GS]) for h in range(2)]
            gated = [sb(f"gated{h}", [P, IB, GS]) for h in range(2)]
            gate_ps = [ctx.enter_context(nc.psum_tensor(f"mamba_gate_ps{h}", [P, GS], F32)) for h in range(2)]
            out_ps = [ctx.enter_context(nc.psum_tensor(f"mamba_out_ps{h}", [P, GT, D], F32)) for h in range(2)]
            gate_ready, gate_kept, gated_ready, out_ready, X_ready, stats_left = (
                sem(n) for n in ("gate_ready", "gate_kept", "gated_ready", "out_ready", "X_ready", "stats_left"))

            with nc.Block() as block:
                @block.tensor
                def _(pe):
                    pe.wait_ge(wide_loaded, 32)
                    pe.sem_inc(gate_ready, 2)
                    with pe.Fori(0, GROUPS // 2) as i:
                        for h in range(2):
                            g = i * 2 + h
                            for m in range(IB):
                                pe.wait_ge(gate_kept, g * IB + (m + 1))
                                for b in range(DB):
                                    last = nc.tensor.matmul(gate_ps[m % 2][:], w_gate[:, b, m * P:(m + 1) * P], xT[:, b, bass.ds(g * GS, GS)],
                                                            start=(b == 0), stop=(b == DB - 1))
                                last.then_inc(gate_ready, 1)
                            pe.wait_ge(gated_ready, g * IB + (IB + 2))
                            for t in range(GT):
                                for m in range(IB):
                                    last = nc.tensor.matmul(out_ps[h][:, t, :], gated[h][:, m, t * P:(t + 1) * P], w_out[:, m, :],
                                                            start=(m == 0), stop=(m == IB - 1))
                            last.then_inc(out_ready, 1)
                        pe.wait_ge(X_ready, i * 2 + 2)

                @block.scalar
                def _(act):
                    act.sem_inc(gate_kept, 2)
                    with act.Fori(0, GROUPS // 2) as i:
                        for h in range(2):
                            g = i * 2 + h
                            for m in range(IB):
                                act.wait_ge(gate_ready, g * IB + (m + 1 + 2))
                                act.wait_ge(gated_ready, g * IB + (m + 1))
                                nc.scalar.activation(gate[m % 2][:], gate_ps[m % 2][:], ACT.Silu).then_inc(gate_kept, 1)

                @block.vector
                def _(dve):
                    dve.sem_inc(gated_ready, 2)
                    with dve.Fori(0, GROUPS // 2) as i:
                        for h in range(2):
                            g = i * 2 + h
                            for m in range(IB):
                                dve.wait_ge(gate_kept, g * IB + (m + 1 + 2))
                                nc.vector.tensor_tensor(gated[h][:, m, :], y[:, m, bass.ds(g * GS, GS)], gate[m % 2][:], ALU.mult).then_inc(gated_ready, 1)
                        for h in range(2):
                            g = i * 2 + h
                            dve.wait_ge(out_ready, g + 1)
                            x_g = X[:, bass.ds(g * GT, GT), :].rearrange("p a b -> p (a b)")
                            nc.vector.scalar_tensor_tensor(out=x_g, in0=x_g, scalar=2.0, in1=out_ps[h][:].rearrange("p a b -> p (a b)"),
                                                           op0=ALU.mult, op1=ALU.add).then_inc(X_ready, 1)
                            dve.wait_ge(X_ready, g + 1)
                            for t in range(GT):
                                tile_stats(nc, constants, X, g * GT + t).then_inc(stats_left, 1)
                    dve.wait_ge(stats_left, TILES)


def attend_context(nc, X, xT, ident, w, w_arrived, ahead):
    constants, ident = ident, ident[0]
    SCALE = float(D // 16) ** -0.5
    keysT, wo = w["contextT"], w["w_outT"]
    K = keysT.shape[-1]
    KT = -(-K // P)
    sizes = [min(P, K - P * k) for k in range(KT)]
    CT = 4
    chunks = [range(c, min(c + CT, KT)) for c in range(0, KT, CT)]
    PRODUCTS = [(0, 0), (0, 1), (1, 0)]
    VT = 8
    with ExitStack() as ctx:
        def sb(n, shape, dt=F32):
            return ctx.enter_context(nc.sbuf_tensor(f"ctx_{n}", shape, dt))

        sem = ctx.enter_context(semaphores(nc, "ctx"))

        KE = K + K % 2
        keys = [sb(f"keys_{part}", [P, DB, KE], F32R) for part in ("high", "low")]
        values = [sb(f"values_{part}", [P, KT, D], F32R) for part in ("high", "low")]
        query = [[sb(f"query{h}_{part}", [P, DB, P], F32R) for part in ("high", "low")] for h in range(2)]
        query_whole = [sb(f"query_whole{h}", [P, DB, P]) for h in range(2)]
        probs = [keysT[:, h, :] for h in range(2)]
        probsT = [[sb(f"probsT{h}_{part}", [P, KT, P], F32R) for part in ("high", "low")] for h in range(2)]
        top = [sb(f"top{h}", [P, 1]) for h in range(2)]
        negtop = [sb(f"negtop{h}", [P, 1]) for h in range(2)]
        total = [sb(f"total{h}", [P, 1]) for h in range(2)]
        share = [sb(f"share{h}", [P, 1]) for h in range(2)]
        scores = ctx.enter_context(nc.psum_tensor("ctx_scores", [P, 4 * 512], F32))
        turned = [ctx.enter_context(nc.psum_tensor(f"ctx_turned{h}", [P, CT, P], F32)) for h in range(2)]
        mixed = [ctx.enter_context(nc.psum_tensor(f"ctx_mixed{h}", [P, 512], F32)) for h in range(2)]
        values_ready, values_kept = sem("values_ready"), sem("values_kept")
        query_ready, scores_ready, top_ready, negtop_ready = sem("query_ready"), sem("scores_ready"), sem("top_ready"), sem("negtop_ready")
        probs_ready, turned_ready, high_kept, low_kept = sem("probs_ready"), sem("turned_ready"), sem("high_kept"), sem("low_kept")
        keys_high, keys_low, values_high, query_high = sem("keys_high"), sem("keys_low"), sem("values_high"), sem("query_high")
        mixed_ready, share_ready, added, stats_left = sem("mixed_ready"), sem("share_ready"), sem("added"), sem("stats_left")
        NC = len(chunks)
        value_pieces = [(0, VT, P), (VT, KT - 1, P), (KT - 1, KT, sizes[-1])]

        def steps(eng, step):
            with eng.Fori(0, TILES // 2 - 1) as i:
                for h in range(2):
                    step(i * 2 + h, h, True)
            step(TILES - 2, 0, True)
            step(TILES - 1, 1, False)

        with nc.Block() as block:
            @block.sync
            def _(sp):
                for to, what, arrived in ahead:
                    sp.dma_start(to, what).then_inc(arrived, 16)

            @block.gpsimd
            def _(pool):
                def cut(k, h):
                    tile = xT[:, :, bass.ds(k * P, P)]
                    nc.gpsimd.tensor_copy(query_whole[h][:], tile).then_inc(query_high, 1)
                    nc.gpsimd.tensor_copy(query[h][0][:], tile).then_inc(query_high, 1)
                    pool.wait_ge(query_high, k * 2 + 2)
                    nc.gpsimd.tensor_tensor(query[h][1][:], query_whole[h][:], query[h][0][:], ALU.subtract).then_inc(query_ready, 1)

                for h in range(2):
                    cut(h, h)
                with pool.Fori(0, TILES // 2 - 1) as i:
                    for h in range(2):
                        pool.wait_ge(scores_ready, i * 2 + (h + 1))
                        cut(i * 2 + (h + 2), h)

            @block.tensor
            def _(pe):
                def score(k, h, part):
                    if part == 0:
                        pe.wait_ge(query_ready, k + 1)
                    for c in range(0, K, 512)[2 * part:2 * part + 2]:
                        n = min(512, KE - c)
                        terms = [(b, of_q, of_k) for b in range(DB) for of_q, of_k in PRODUCTS]
                        for term in terms:
                            b, of_q, of_k = term
                            last = nc.tensor.matmul(scores[:, c:c + n], query[h][of_q][:, b, :], keys[of_k][:, b, c:c + n],
                                                    start=(term == terms[0]), stop=(term == terms[-1]))
                    if part == 1:
                        last.then_inc(scores_ready, 1)

                def turn(k, h, c):
                    if c >= 2:
                        pe.wait_ge(low_kept, k * NC + (c - 1))
                    for t, kt in enumerate(chunks[c]):
                        last = nc.tensor.transpose(turned[c % 2][0:sizes[kt], t, :], probs[h][:, kt * P:kt * P + sizes[kt]], ident[:])
                    last.then_inc(turned_ready, 1)

                def mix(k, h, c):
                    pe.wait_ge(low_kept, k * NC + (c + 1))
                    for kt in chunks[c]:
                        for of_p, of_v in PRODUCTS:
                            last = nc.tensor.matmul(mixed[h][:, 0:D], probsT[h][of_p][0:sizes[kt], kt, :], values[of_v][0:sizes[kt], kt, :],
                                                    start=(kt == 0 and (of_p, of_v) == PRODUCTS[0]),
                                                    stop=(kt == KT - 1 and (of_p, of_v) == PRODUCTS[-1]))
                    if c == NC - 1:
                        last.then_inc(mixed_ready, 1)

                def step(k, h, more):
                    pe.wait_ge(probs_ready, k + 1)
                    turn(k, h, 0)
                    turn(k, h, 1)
                    if more:
                        score(k + 1, 1 - h, 0)
                    turn(k, h, 2)
                    turn(k, h, 3)
                    if more:
                        score(k + 1, 1 - h, 1)
                    for c in range(NC):
                        mix(k, h, c)

                pe.wait_ge(*w_arrived)
                for v in range(0, KT, VT):
                    if v:
                        pe.wait_ge(values_kept, 1)
                    for kt in range(v, min(v + VT, KT)):
                        for b in range(DB):
                            last = nc.tensor.matmul(scores[0:sizes[kt], (kt - v) * D:(kt - v + 1) * D],
                                                    keysT[:, b, kt * P:kt * P + sizes[kt]], wo[:, b, :],
                                                    start=(b == 0), stop=(b == DB - 1))
                    last.then_inc(values_ready, 1)
                pe.wait_ge(values_kept, 3)
                pe.wait_ge(keys_low, 1 + 2 * (KE - K))
                score(0, 0, 0)
                score(0, 0, 1)
                steps(pe, step)

            @block.vector
            def _(dve):
                dve.wait_ge(*w_arrived)
                def maximum(k, h):
                    dve.wait_ge(scores_ready, k + 1)
                    nc.vector.reduce_max(top[h][:], scores[:, 0:K], AX_X).then_inc(top_ready, 1)
                    dve.wait_ge(top_ready, k + 1)
                    nc.vector.tensor_scalar(negtop[h][:], top[h][:], -SCALE, None, ALU.mult).then_inc(negtop_ready, 1)

                def step(k, h, more):
                    for c in range(NC):
                        dve.wait_ge(high_kept, k * NC + (c + 1))
                        n = len(chunks[c])
                        r = sizes[chunks[c][-1]] if n == 1 else P
                        at = slice(chunks[c][0], chunks[c][0] + n)
                        nc.vector.tensor_tensor(probsT[h][1][0:r, at, :], turned[c % 2][0:r, 0:n, :], probsT[h][0][0:r, at, :],
                                                ALU.subtract).then_inc(low_kept, 1)
                    if more:
                        maximum(k + 1, 1 - h)
                    dve.wait_ge(probs_ready, k + 1)
                    nc.vector.reciprocal(share[h][:], total[h][:]).then_inc(share_ready, 1)
                    dve.wait_ge(share_ready, k + 1)
                    dve.wait_ge(mixed_ready, k + 1)
                    x = X[:, bass.ds(k, 1), :].rearrange("p a b -> p (a b)")
                    nc.vector.scalar_tensor_tensor(out=x, in0=mixed[h][:, 0:D], scalar=share[h][:], in1=x,
                                                   op0=ALU.mult, op1=ALU.add).then_inc(added, 1)
                    dve.wait_ge(added, k + 1)
                    tile_stats(nc, constants, X, k).then_inc(stats_left, 1)

                if KE > K:
                    for part in keys:
                        nc.vector.memset(part[:, :, K:KE].bitcast(F32), 0.0).then_inc(keys_low, 1)
                dve.wait_ge(keys_high, 1)
                nc.vector.tensor_tensor(keys[1][:, :, 0:K], keysT[:], keys[0][:, :, 0:K], ALU.subtract).then_inc(keys_low, 1)
                for n, (t0, t1, r) in enumerate(value_pieces):
                    dve.wait_ge(values_high, n + 1)
                    nc.vector.tensor_tensor(values[1][0:r, t0:t1, :].rearrange("p a b -> p (a b)"),
                                            scores[0:r, t0 % VT * D:(t0 % VT + t1 - t0) * D],
                                            values[0][0:r, t0:t1, :].rearrange("p a b -> p (a b)"), ALU.subtract).then_inc(values_kept, 1)
                maximum(0, 0)
                steps(dve, step)
                dve.wait_ge(stats_left, TILES)

            @block.scalar
            def _(act):
                act.wait_ge(*w_arrived)
                nc.scalar.activation(keys[0][:, :, 0:K], keysT[:], ACT.Identity).then_inc(keys_high, 1)
                for n, (t0, t1, r) in enumerate(value_pieces):
                    act.wait_ge(values_ready, min(n, 1) + 1)
                    nc.scalar.activation(values[0][0:r, t0:t1, :].rearrange("p a b -> p (a b)"),
                                         scores[0:r, t0 % VT * D:(t0 % VT + t1 - t0) * D], ACT.Identity).then_inc(values_high, 1)

                def softmax(k, h):
                    act.wait_ge(negtop_ready, k + 1)
                    nc.scalar.activation(probs[h], scores[:, 0:K], ACT.Exp, bias=negtop[h][:], scale=SCALE,
                                         accum_out=total[h][:]).then_inc(probs_ready, 1)

                def step(k, h, more):
                    for c in range(NC):
                        act.wait_ge(turned_ready, k * NC + (c + 1))
                        n = len(chunks[c])
                        r = sizes[chunks[c][-1]] if n == 1 else P
                        nc.scalar.activation(probsT[h][0][0:r, chunks[c][0]:chunks[c][0] + n, :], turned[c % 2][0:r, 0:n, :],
                                             ACT.Identity).then_inc(high_kept, 1)
                    if more:
                        softmax(k + 1, 1 - h)

                softmax(0, 0)
                steps(act, step)


def route_tiles(w):
    return 2 * S // P + w["router_b"].shape[0] - 1


def route_ahead(nc, keep, w):
    E, FF, NT = w["router_b"].shape[0], w["W1"].shape[-1], route_tiles(w)
    W1 = keep.enter_context(nc.sbuf_tensor("route_W1", [P, E * DB, FF], F32))
    zero = keep.enter_context(nc.sbuf_tensor("route_zero", [P, D], F32))
    slots = nc.dram_tensor("route_slots", [NT * P, D], F32).ap()
    rw = keep.enter_context(nc.sbuf_tensor("route_rw", [P, DB, E], F32))
    rb = keep.enter_context(nc.sbuf_tensor("route_rb", [E, 1], F32))
    W1_loaded = keep.enter_context(nc.semaphore("route_W1_loaded"))
    router_loaded = keep.enter_context(nc.semaphore("route_router_loaded"))
    slots_zeroed = keep.enter_context(nc.semaphore("route_slots_zeroed"))
    zero_ready = keep.enter_context(nc.semaphore("route_zero_ready"))
    with nc.Block() as block:
        @block.gpsimd
        def _(pool):
            nc.gpsimd.memset(zero[:], 0.0).then_inc(zero_ready, 1)
            pool.wait_ge(zero_ready, 1)
    ahead = [(rw[:], w["router_W"], router_loaded), (rb[:], w["router_b"], router_loaded),
             (W1[:].rearrange("p (e b) f -> p e b f", e=E), w["W1"], W1_loaded),
             (slots.rearrange("(p j) d -> p j d", p=P), zero[:].unsqueeze(1).broadcast_to([P, NT, D]), slots_zeroed)]
    return (W1, rw, rb, slots, W1_loaded, router_loaded, slots_zeroed), ahead


HEADS = 16
W = D // HEADS
PARTS = 3


def heads_ahead(nc, context):
    K = context.shape[-1]
    k_dram = nc.dram_tensor("heads_k", [PARTS, D, K], BF16).ap()
    v_dram = nc.dram_tensor("heads_v", [P, -(-K // P), D], F32).ap()
    return k_dram, v_dram


def route_to_two(nc, X, xT, ident, w, kept, heads, context, w_kT, w_vT):
    constants = ident
    ident, _, eps, stats = constants
    E = w["router_b"].shape[0]
    FF = w["W1"].shape[-1]
    FB = FF // P
    NT = route_tiles(w)
    W1, rw, rb, slots, W1_loaded, router_loaded, slots_zeroed = kept
    BIG = 3.0e38
    hat = xT[:].rearrange("p b s -> p (b s)").rearrange("p (t d) -> p t d", d=D)
    answers = nc.dram_tensor("route_answers", [NT * P, D], F32).ap()
    bias_dram = nc.dram_tensor("route_bias", [E, 3, FF + D], BF16).ap()

    with ExitStack() as outer:
        def keep(n, shape, dt=F32):
            return outer.enter_context(nc.sbuf_tensor(f"route_{n}", shape, dt))

        W2 = keep("W2", [P, E * FB, D])
        gates = keep("gates", [P, 2, TILES])
        position = keep("position", [P, 2, TILES], U32)
        expert = keep("expert", [P, NT], I32)
        ln_g = keep("ln_g", [P, E, DB])
        ln_b = keep("ln_b", [P, E, DB])
        W2_loaded = outer.enter_context(nc.semaphore("route_W2_loaded"))

        with ExitStack() as ctx:
            def sb(n, shape, dt=F32):
                return ctx.enter_context(nc.sbuf_tensor(f"route_{n}", shape, dt))

            sem = ctx.enter_context(semaphores(nc, "route"))

            TE = [P, TILES, E]
            logitsT = sb("logitsT", [E, S])
            logits, rest, hit, where = sb("logits", TE), sb("rest", TE), sb("hit", TE), sb("where", TE)
            first, second = sb("first", TE), sb("second", TE)
            chosen = sb("chosen", TE, BF16)
            iota_e = sb("iota_e", [P, E])
            iota_t = sb("iota_t", [P, TILES])
            iota_n = sb("iota_n", [P, NT])
            before = sb("before", [P, P], BF16)
            ones = sb("ones", [P, P], BF16)
            best, runner, gap, egap, denom = (sb(n, [P, TILES]) for n in ("best", "runner", "gap", "egap", "denom"))
            over = sb("over", [P, E, TILES])
            cnt, tiles_of, upto, base, ones_e = (sb(n, [P, E]) for n in ("cnt", "tiles_of", "upto", "base", "ones_e"))
            slot = sb("slot", TE)
            slot1 = sb("slot1", [P, TILES])
            past = sb("past", [P, NT, E])
            nth = sb("nth", [P, NT])
            b12 = sb("b12", [E, FF + D])
            left = sb("left", [E, FF + D])
            parts = sb("parts", [E, 3, FF + D], BF16)
            logit_ps = ctx.enter_context(nc.psum_tensor("route_logit_ps", [E, 4, 512], F32))
            turned = ctx.enter_context(nc.psum_tensor("route_turned", [P, TILES, E], F32))
            prefix = ctx.enter_context(nc.psum_tensor("route_prefix", [P, TILES, E], F32))
            count = ctx.enter_context(nc.psum_tensor("route_count", [P, 512], F32))
            small_loaded, logits_ready, logitsT_kept, turned_ready = sem("small_loaded"), sem("logits_ready"), sem("logitsT_kept"), sem("turned_ready")
            iotas, chosen_ready, prefix_ready, var_ready = sem("iotas"), sem("chosen_ready"), sem("prefix_ready"), sem("var_ready")
            root_ready, shift_ready, hat_ready = sem("root_ready"), sem("shift_ready"), sem("hat_ready")
            mean2, var, root, rstd, shift = (sb(n, [P, TILES]) for n in ("mean2", "var", "root", "rstd", "shift"))
            gap_ready, egap_ready, chained, parts_ready, parts_stored = sem("gap_ready"), sem("egap_ready"), sem("chained"), sem("parts_ready"), sem("parts_stored")

            with nc.Block() as block:
                @block.sync
                def _(sp):
                    for to, what in ((b12[:, 0:FF], w["b1"]), (b12[:, FF:FF + D], w["b2"]),
                                     (ln_g[:], w["ln_g"]), (ln_b[:], w["ln_b"])):
                        sp.dma_start(to, what).then_inc(small_loaded, 16)
                    sp.wait_ge(parts_ready, 5)
                    sp.wait_ge(small_loaded, 64)
                    sp.dma_start(bias_dram, parts[:]).then_inc(parts_stored, 16)
                    sp.dma_start(W2[:].rearrange("p (e b) f -> p e b f", e=E), w["W2"]).then_inc(W2_loaded, 16)
                    sp.wait_ge(parts_stored, 16)

                @block.tensor
                def _(pe):
                    pe.wait_ge(router_loaded, 32)
                    for c in range(4):
                        for b in range(DB):
                            last = nc.tensor.matmul(logit_ps[:, c, :], rw[:, b, :], xT[:, b, c * 512:(c + 1) * 512],
                                                    start=(b == 0), stop=(b == DB - 1))
                    last.then_inc(logits_ready, 1)
                    pe.wait_ge(logitsT_kept, 1)
                    for t in range(TILES):
                        last = nc.tensor.transpose(turned[:, t, :], logitsT[:, t * P:(t + 1) * P], ident[0:E, 0:E])
                    last.then_inc(turned_ready, 1)
                    pe.wait_ge(chosen_ready, 1)
                    pe.wait_ge(iotas, 5)
                    nc.tensor.matmul(prefix[:], before[:], chosen[:], start=True, stop=False)
                    for t in range(TILES - 1):
                        last = nc.tensor.matmul(prefix[:, t + 1:, :], ones[:],
                                                chosen[:, t:t + 1, :].broadcast_to([P, TILES - 1 - t, E]),
                                                start=False, stop=(t == TILES - 2))
                    for t in range(TILES):
                        last = nc.tensor.matmul(count[:, 0:E], ones[:], chosen[:, t, :], start=(t == 0), stop=(t == TILES - 1))
                    last.then_inc(prefix_ready, 1)

                @block.gpsimd
                def _(pool):
                    exact = dict(allow_small_or_imprecise_dtypes=True)
                    nc.gpsimd.iota(iota_e[:], [[1, E]], base=0, channel_multiplier=0, **exact).then_inc(iotas, 1)
                    nc.gpsimd.iota(iota_t[:], [[P, TILES]], base=0, channel_multiplier=0, **exact).then_inc(iotas, 1)
                    nc.gpsimd.iota(iota_n[:], [[1, NT]], base=0, channel_multiplier=0, **exact).then_inc(iotas, 1)
                    nc.gpsimd.memset(ones[:], 1.0).then_inc(iotas, 1)
                    pool.wait_ge(iotas, 4)
                    nc.gpsimd.affine_select(out=before[:], in_=ones[:], compare_op=ALU.is_gt, fill=0.0, base=0,
                                            pattern=[[1, P]], channel_multiplier=-1).then_inc(iotas, 1)
                    G = nc.gpsimd
                    pool.wait_ge(small_loaded, 64)
                    G.tensor_copy(parts[:, 0, :], b12[:]).then_inc(parts_ready, 1)
                    pool.wait_ge(parts_ready, 1)
                    G.tensor_tensor(left[:], b12[:], parts[:, 0, :], ALU.subtract).then_inc(parts_ready, 1)
                    pool.wait_ge(parts_ready, 2)
                    G.tensor_copy(parts[:, 1, :], left[:]).then_inc(parts_ready, 1)
                    pool.wait_ge(parts_ready, 3)
                    G.tensor_tensor(b12[:], left[:], parts[:, 1, :], ALU.subtract).then_inc(parts_ready, 1)
                    pool.wait_ge(parts_ready, 4)
                    G.tensor_copy(parts[:, 2, :], b12[:]).then_inc(parts_ready, 1)

                @block.scalar
                def _(act):
                    act.wait_ge(var_ready, 1)
                    nc.scalar.activation(root[:], var[:], ACT.Sqrt, bias=eps[:]).then_inc(root_ready, 1)
                    act.wait_ge(logits_ready, 1)
                    act.wait_ge(router_loaded, 32)
                    nc.scalar.activation(logitsT[:].rearrange("p (a b) -> p a b", a=4), logit_ps[:], ACT.Identity,
                                         bias=rb[:]).then_inc(logitsT_kept, 1)
                    act.wait_ge(shift_ready, 1)
                    for t in range(TILES):
                        nc.scalar.activation(hat[:, t, :], X[:, t, :], ACT.Identity, bias=shift[:, t:t + 1], scale=rstd[:, t:t + 1]).then_inc(hat_ready, 1)
                    act.wait_ge(gap_ready, 1)
                    nc.scalar.activation(egap[:], gap[:], ACT.Exp).then_inc(egap_ready, 1)
                    act.wait_ge(hat_ready, TILES)

                @block.vector
                def _(dve):
                    done = [0]

                    def link(ins):
                        done[0] += 1
                        ins.then_inc(chained, 1)
                        dve.wait_ge(chained, done[0])

                    V = nc.vector
                    for t in range(TILES):
                        last = V.bn_stats(stats[:, t, :], X[:, t, :])
                    link(last)
                    link(V.tensor_tensor(mean2[:], stats[:, :, 1], stats[:, :, 4], ALU.add))
                    link(V.tensor_tensor(slot1[:], stats[:, :, 1], stats[:, :, 4], ALU.subtract))
                    link(V.tensor_tensor(var[:], stats[:, :, 2], stats[:, :, 5], ALU.add))
                    link(V.tensor_tensor(slot1[:], slot1[:], slot1[:], ALU.mult))
                    link(V.tensor_scalar(var[:], var[:], 1.0 / D, None, ALU.mult))
                    V.scalar_tensor_tensor(out=var[:], in0=slot1[:], scalar=0.25, in1=var[:], op0=ALU.mult, op1=ALU.add).then_inc(var_ready, 1)
                    dve.wait_ge(root_ready, 1)
                    link(V.reciprocal(rstd[:], root[:]))
                    V.scalar_tensor_tensor(out=shift[:], in0=mean2[:], scalar=-0.5, in1=rstd[:], op0=ALU.mult, op1=ALU.mult).then_inc(shift_ready, 1)

                    dve.wait_ge(turned_ready, 1)
                    link(V.tensor_copy(logits[:], turned[:]))
                    dve.wait_ge(iotas, 5)

                    def pick(which, values, top):
                        link(V.tensor_reduce(top[:], values[:], AX_X, ALU.max))
                        link(V.tensor_tensor(hit[:], values[:], top[:].unsqueeze(2).broadcast_to(TE), ALU.is_equal))
                        link(V.tensor_scalar(where[:], iota_e[:].unsqueeze(1).broadcast_to(TE), -1.0, float(E), ALU.mult, ALU.add))
                        link(V.tensor_tensor(where[:], where[:], hit[:], ALU.mult))
                        link(V.tensor_reduce(denom[:], where[:], AX_X, ALU.max))
                        link(V.tensor_tensor(which[:], where[:], denom[:].unsqueeze(2).broadcast_to(TE), ALU.is_equal))

                    pick(first, logits, best)
                    link(V.scalar_tensor_tensor(out=rest[:].rearrange("p a b -> p (a b)"), in0=first[:].rearrange("p a b -> p (a b)"),
                                                scalar=-BIG, in1=logits[:].rearrange("p a b -> p (a b)"), op0=ALU.mult, op1=ALU.add))
                    pick(second, rest, runner)
                    V.tensor_tensor(chosen[:], first[:], second[:], ALU.add).then_inc(chosen_ready, 1)
                    V.tensor_tensor(gap[:], runner[:], best[:], ALU.subtract).then_inc(gap_ready, 1)
                    dve.wait_ge(egap_ready, 1)
                    link(V.tensor_scalar(denom[:], egap[:], 1.0, None, ALU.add))
                    link(V.reciprocal(gates[:, 0, :], denom[:]))
                    link(V.tensor_tensor(gates[:, 1, :], egap[:], gates[:, 0, :], ALU.mult))

                    dve.wait_ge(prefix_ready, 1)
                    link(V.tensor_copy(cnt[:], count[:, 0:E]))
                    ET = [P, E, TILES]
                    link(V.tensor_tensor(over[:], cnt[:].unsqueeze(2).broadcast_to(ET), iota_t[:].unsqueeze(1).broadcast_to(ET), ALU.is_gt))
                    link(V.tensor_reduce(tiles_of[:], over[:], AX_X, ALU.add))
                    link(V.memset(ones_e[:], 1.0))
                    link(V.tensor_tensor_scan(upto[:], ones_e[:], tiles_of[:], 0.0, ALU.mult, ALU.add))
                    link(V.tensor_tensor(base[:], upto[:], tiles_of[:], ALU.subtract))
                    link(V.tensor_scalar(base[:], base[:], float(P), None, ALU.mult))
                    link(V.tensor_tensor(slot[:], prefix[:], base[:].unsqueeze(1).broadcast_to(TE), ALU.add))
                    for n, which in enumerate((first, second)):
                        link(V.tensor_tensor(where[:], slot[:], which[:], ALU.mult))
                        link(V.tensor_reduce(slot1[:], where[:], AX_X, ALU.add))
                        link(V.tensor_copy(position[:, n, :], slot1[:]))
                    NE = [P, NT, E]
                    link(V.tensor_tensor(past[:], iota_n[:].unsqueeze(2).broadcast_to(NE), upto[:].unsqueeze(1).broadcast_to(NE), ALU.is_ge))
                    link(V.tensor_reduce(nth[:], past[:], AX_X, ALU.add))
                    link(V.tensor_scalar(nth[:], nth[:], float(E - 1), None, ALU.min))
                    link(V.tensor_copy(expert[:], nth[:]))

        with ExitStack() as ctx:
            def sb(n, shape, dt=F32):
                return ctx.enter_context(nc.sbuf_tensor(f"route_{n}", shape, dt))

            def ps(n, shape, dt=F32):
                return ctx.enter_context(nc.psum_tensor(f"route_{n}", shape, dt))

            sem = ctx.enter_context(semaphores(nc, "route"))

            rows = [sb(f"rows{h}", [P, D]) for h in range(2)]
            rowsT = [sb(f"rowsT{h}", [P, DB, P]) for h in range(2)]
            b1 = [sb(f"b1_{h}", [3, FF], BF16) for h in range(2)]
            b2 = [sb(f"b2_{h}", [3, D], BF16) for h in range(2)]
            ones3 = sb("ones3", [3, P], BF16)
            hidden = [sb(f"hidden{h}", [P, FF]) for h in range(2)]
            hiddenT = sb("hiddenT", [P, FB, P])
            answer = [sb(f"answer{h}", [P, D]) for h in range(2)]
            turned_ps = ps("turned_ps", [P, 512])
            hidden_ps = [ps(f"hidden_ps{h}", [P, FF]) for h in range(2)]
            hiddenT_ps = ps("hiddenT_ps", [P, FB, P])
            answer_ps = ps("answer_ps", [P, 512])
            scattered, turned_ready, rowsT_ready = sem("scattered"), sem("turned_rows"), sem("rowsT_ready")
            rows_loaded = [sem(f"rows_loaded{h}") for h in range(2)]
            b1_loaded = [sem(f"b1_loaded{h}") for h in range(2)]
            b2_loaded = [sem(f"b2_loaded{h}") for h in range(2)]
            product_ready, hidden_ready, hiddenT_ready, hiddenT_kept = sem("product_ready"), sem("hidden_ready"), sem("hiddenT_ready"), sem("hiddenT_kept")
            answer_ready, answer_kept, ones_ready = sem("answer_ready"), sem("answer_kept"), sem("ones_ready")
            stored = [sem(f"stored{h}") for h in range(2)]

            def steps(eng, step):
                loops = (NT - 2) // 2
                with eng.Fori(0, loops) as i:
                    for h in range(2):
                        step(i * 2 + h, i, h, 2)
                for k in range(2 * loops, NT):
                    step(k, k // 2, k % 2, NT - 1 - k)

            def expert_of(eng, k):
                return eng.value_load(expert[0:1, bass.ds(k, 1)], min_val=0, max_val=E - 1)

            with nc.Block() as block:
                @block.gpsimd
                def _(pool):
                    nc.gpsimd.memset(ones3[:], 1.0).then_inc(ones_ready, 1)
                    pool.wait_ge(slots_zeroed, 16)
                    for t in range(TILES):
                        for n in range(2):
                            nc.gpsimd.indirect_dma_start(slots, bass.IndirectOffsetOnAxis(ap=position[:, n, t:t + 1], axis=0),
                                                         hat[:, t, :], None).then_inc(scattered, 16)

                @block.sync
                def _(sp):
                    def load_rows(k, h):
                        sp.dma_start(rows[h][:], slots[bass.ds(k * P, P), :]).then_inc(rows_loaded[h], 16)

                    def load_b1(k, h):
                        e = expert_of(sp, k)
                        sp.dma_start(b1[h][:], bias_dram[bass.ds(e, 1), :, 0:FF].rearrange("a b c -> (a b) c")).then_inc(b1_loaded[h], 16)

                    def load_b2(k, h):
                        e = expert_of(sp, k)
                        sp.dma_start(b2[h][:], bias_dram[bass.ds(e, 1), :, FF:FF + D].rearrange("a b c -> (a b) c")).then_inc(b2_loaded[h], 16)

                    def step(k, j, h, follow):
                        if follow >= 2:
                            sp.wait_ge(turned_ready, k + 1)
                            load_rows(k + 2, h)
                            sp.wait_ge(product_ready, k + 1)
                            load_b1(k + 2, h)
                        sp.wait_ge(answer_kept, k + 2)
                        sp.dma_start(answers[bass.ds(k * P, P), :], answer[h][:]).then_inc(stored[h], 16)
                        if follow >= 2:
                            load_b2(k + 2, h)

                    sp.wait_ge(scattered, 2 * TILES * 16)
                    for h in range(2):
                        load_rows(h, h)
                        load_b1(h, h)
                        load_b2(h, h)
                    steps(sp, step)
                    sp.wait_ge(stored[0], (NT + 1) // 2 * 16 + 16)
                    sp.wait_ge(stored[1], NT // 2 * 16 + 16)

                @block.tensor
                def _(pe):
                    def turn(j, h):
                        pe.wait_ge(rows_loaded[h], j * 16 + 16)
                        for b in range(DB):
                            last = nc.tensor.transpose(turned_ps[:, b * P:(b + 1) * P], rows[h][:, b * P:(b + 1) * P], ident[:])
                        last.then_inc(turned_ready, 1)

                    def first_product(k, j, h, half):
                        e = expert_of(pe, k)
                        if half == 0:
                            pe.wait_ge(b1_loaded[h], j * 16 + 16)
                            pe.wait_ge(rowsT_ready, k * DB + DB)
                        n = slice(half * 512, half * 512 + 512)
                        nc.tensor.matmul(hidden_ps[h][:, n], ones3[:], b1[h][:, n], start=True, stop=False)
                        for b in range(DB):
                            last = nc.tensor.matmul(hidden_ps[h][:, n], rowsT[h][:, b, :],
                                                    W1[:, bass.ds(e * DB + b, 1), n].rearrange("p a b -> p (a b)"), start=False, stop=(b == DB - 1))
                        if half == 1:
                            last.then_inc(product_ready, 1)

                    def second_product(k, j, h):
                        e = expert_of(pe, k)
                        pe.wait_ge(answer_kept, k + 1)
                        pe.wait_ge(b2_loaded[h], j * 16 + 16)
                        nc.tensor.matmul(answer_ps[:, 0:D], ones3[:], b2[h][:], start=True, stop=False)
                        for f in range(FB):
                            if f % (FB // 2) == 0:
                                pe.wait_ge(hiddenT_kept, k * 2 + (2 * f // FB + 1))
                            last = nc.tensor.matmul(answer_ps[:, 0:D], hiddenT[:, f, :],
                                                    W2[:, bass.ds(e * FB + f, 1), :].rearrange("p a b -> p (a b)"), start=False, stop=(f == FB - 1))
                        last.then_inc(answer_ready, 1)

                    def step(k, j, h, follow):
                        if follow >= 1:
                            first_product(k + 1, j + h, 1 - h, 0)
                        pe.wait_ge(hidden_ready, k * 1 + 1)
                        for f in range(FB):
                            last = nc.tensor.transpose(hiddenT_ps[:, f, :], hidden[h][:, f * P:(f + 1) * P], ident[:])
                            if f % (FB // 2) == FB // 2 - 1:
                                last.then_inc(hiddenT_ready, 1)
                        if follow >= 1:
                            first_product(k + 1, j + h, 1 - h, 1)
                        if follow >= 2:
                            turn(j + 1, h)
                        second_product(k, j, h)

                    pe.wait_ge(ones_ready, 1)
                    pe.wait_ge(W1_loaded, 16)
                    turn(0, 0)
                    first_product(0, 0, 0, 0)
                    first_product(0, 0, 0, 1)
                    turn(0, 1)
                    pe.wait_ge(W2_loaded, 16)
                    steps(pe, step)

                @block.scalar
                def _(act):
                    def scale_rows(k, h):
                        e = expert_of(act, k)
                        act.wait_ge(turned_ready, k + 1)
                        for b in range(DB):
                            nc.scalar.activation(rowsT[h][:, b, :], turned_ps[:, b * P:(b + 1) * P], ACT.Identity,
                                                 bias=ln_b[:, bass.ds(e, 1), b], scale=ln_g[:, bass.ds(e, 1), b]).then_inc(rowsT_ready, 1)

                    def gelu(k, h):
                        act.wait_ge(product_ready, k + 1)
                        nc.scalar.activation(hidden[h][:], hidden_ps[h][:], ACT.Gelu).then_inc(hidden_ready, 1)

                    def step(k, j, h, follow):
                        if follow >= 1:
                            gelu(k + 1, 1 - h)
                        if follow >= 2:
                            scale_rows(k + 2, h)
                        act.wait_ge(stored[h], j * 16 + 16)
                        act.wait_ge(answer_ready, k + 1)
                        nc.scalar.activation(answer[h][:], answer_ps[:, 0:D], ACT.Identity).then_inc(answer_kept, 1)

                    act.sem_inc(answer_kept, 1)
                    act.sem_inc(stored[0], 16)
                    act.sem_inc(stored[1], 16)
                    scale_rows(0, 0)
                    gelu(0, 0)
                    scale_rows(1, 1)
                    steps(act, step)

                @block.vector
                def _(dve):
                    def step(k, j, h, follow):
                        for half in range(2):
                            dve.wait_ge(hiddenT_ready, k * 2 + (half + 1))
                            f = slice(half * FB // 2, (half + 1) * FB // 2)
                            nc.vector.tensor_copy(hiddenT[:, f, :], hiddenT_ps[:, f, :]).then_inc(hiddenT_kept, 1)
                    steps(dve, step)

        with ExitStack() as ctx:
            sem = ctx.enter_context(semaphores(nc, "combine"))
            fetched = [sem(f"fetched{t}") for t in range(TILES // GT)]
            weighed, first, second, summed, stats_left = (sem(n) for n in ("weighed", "first", "second", "summed", "stats_left"))
            own = ctx.enter_context(nc.sbuf_tensor("route_own", [P, TILES], F32))
            got = W1[:].rearrange("p a b -> p (a b)").rearrange("p (c d) -> p c d", d=D)

            k_dram, v_dram = heads
            K = context.shape[-1]
            KT = -(-K // P)
            ksize = [min(P, K - P * k) for k in range(KT)]
            keysT = W2[:].rearrange("p a b -> p (a b)")[:, 0:DB * K].rearrange("p (b k) -> p b k", b=DB)
            values = ctx.enter_context(nc.sbuf_tensor("combine_values", [P, KT, D], F32))
            B = 4
            wk, wv = (ctx.enter_context(nc.sbuf_tensor(f"heads_{n}", [P, DB, D], F32)) for n in ("wk", "wv"))
            parts = [ctx.enter_context(nc.sbuf_tensor(f"heads_kparts{h}", [P, PARTS, 512], BF16)) for h in range(B)]
            rest = [ctx.enter_context(nc.sbuf_tensor(f"heads_krest{h}", [P, 512], F32)) for h in range(B)]
            product = [ctx.enter_context(nc.psum_tensor(f"heads_kproduct{h}", [P, 512], F32)) for h in range(B)]
            value_ps = [ctx.enter_context(nc.psum_tensor(f"heads_value_ps{h}", [P, 512], F32)) for h in range(2)]
            loaded, product_ready, part1, rest1, part2, part3, value_ready, value_kept, values_stored = (
                sem(n) for n in ("loaded", "product_ready", "part1", "rest1", "part2", "part3", "value_ready", "value_kept", "values_stored"))
            parts_stored = [sem(f"parts_stored{h}") for h in range(B)]
            units = [(o, c, min(512, K - c)) for o in range(DB) for c in range(0, K, 512)]
            N = len(units)

            with nc.Block() as block:
                @block.sync
                def _(sp):
                    for to, what in ((keysT, context), (wk[:], w_kT), (wv[:], w_vT)):
                        sp.dma_start(to, what).then_inc(loaded, 16)
                    for n, (o, c, size) in enumerate(units):
                        sp.wait_ge(part3, n + 1)
                        sp.dma_start(k_dram[:, o * P:(o + 1) * P, c:c + size].rearrange("a p s -> p a s"),
                                     parts[n % B][:, :, 0:size]).then_inc(parts_stored[n % B], 16)
                    sp.wait_ge(value_kept, KT)
                    sp.dma_start(v_dram[:, 0:KT - 1, :], values[:, 0:KT - 1, :]).then_inc(values_stored, 16)
                    sp.dma_start(v_dram[0:ksize[-1], KT - 1, :], values[0:ksize[-1], KT - 1, :]).then_inc(values_stored, 16)
                    sp.wait_ge(values_stored, 32)
                    for h in range(B):
                        sp.wait_ge(parts_stored[h], (N + B - 1 - h) // B * 16)

                @block.gpsimd
                def _(pool):
                    for t in range(TILES):
                        for n in range(2):
                            nc.gpsimd.indirect_dma_start(got[:, 2 * t + n, :], None, answers,
                                                         bass.IndirectOffsetOnAxis(ap=position[:, n, t:t + 1], axis=0)).then_inc(fetched[t // GT], 16)

                @block.tensor
                def _(pe):
                    pe.wait_ge(loaded, 48)
                    for n in range(max(N, KT)):
                        if n < N:
                            o, c, size = units[n]
                            if n >= B:
                                pe.wait_ge(rest1, n - B + 1)
                            for b in range(DB):
                                last = nc.tensor.matmul(product[n % B][:, 0:size], wk[:, b, o * P:(o + 1) * P], keysT[:, b, c:c + size],
                                                        start=(b == 0), stop=(b == DB - 1))
                            last.then_inc(product_ready, 1)
                        if n < KT:
                            if n >= 2:
                                pe.wait_ge(value_kept, n - 1)
                            for b in range(DB):
                                last = nc.tensor.matmul(value_ps[n % 2][0:ksize[n], 0:D], keysT[:, b, n * P:n * P + ksize[n]], wv[:, b, :],
                                                        start=(b == 0), stop=(b == DB - 1))
                            last.then_inc(value_ready, 1)

                @block.scalar
                def _(act):
                    for n in range(max(N + 1, KT)):
                        if n < N:
                            act.wait_ge(product_ready, n + 1)
                            if n >= B:
                                act.wait_ge(parts_stored[n % B], n // B * 16)
                            size = units[n][2]
                            nc.scalar.activation(parts[n % B][:, 0, 0:size], product[n % B][:, 0:size], ACT.Identity).then_inc(part1, 1)
                        if n < KT:
                            act.wait_ge(value_ready, n + 1)
                            nc.scalar.activation(values[0:ksize[n], n, :], value_ps[n % 2][0:ksize[n], 0:D], ACT.Identity).then_inc(value_kept, 1)
                        if 1 <= n <= N:
                            size = units[n - 1][2]
                            act.wait_ge(rest1, n)
                            nc.scalar.activation(parts[(n - 1) % B][:, 1, 0:size], rest[(n - 1) % B][:, 0:size], ACT.Identity).then_inc(part2, 1)
                    act.wait_ge(value_kept, KT)

                @block.vector
                def _(dve):
                    def cut(n):
                        if n < N:
                            size = units[n][2]
                            dve.wait_ge(part1, n + 1)
                            nc.vector.tensor_tensor(rest[n % B][:, 0:size], product[n % B][:, 0:size], parts[n % B][:, 0, 0:size],
                                                    ALU.subtract).then_inc(rest1, 1)
                        if n:
                            size = units[n - 1][2]
                            dve.wait_ge(part2, n)
                            nc.vector.tensor_tensor(parts[(n - 1) % B][:, 2, 0:size], rest[(n - 1) % B][:, 0:size],
                                                    parts[(n - 1) % B][:, 1, 0:size], ALU.subtract).then_inc(part3, 1)

                    nc.vector.tensor_tensor(own[:], gates[:, 0, :], gates[:, 1, :], ALU.add).then_inc(summed, 1)
                    dve.wait_ge(summed, 1)
                    nc.vector.tensor_scalar(own[:], own[:], 1.0, None, ALU.add).then_inc(summed, 1)
                    dve.wait_ge(summed, 2)
                    Q = TILES // GT
                    for q in range(Q):
                        tiles = range(q * GT, (q + 1) * GT)
                        for t in tiles:
                            nc.vector.tensor_scalar(X[:, t, :], X[:, t, :], own[:, t:t + 1], None, ALU.mult).then_inc(weighed, 1)
                        for n in range(q * (N + 1) // Q, (q + 1) * (N + 1) // Q):
                            cut(n)
                        dve.wait_ge(fetched[q], 2 * GT * 16)
                        for t in tiles:
                            dve.wait_ge(weighed, t + 1)
                            nc.vector.scalar_tensor_tensor(out=X[:, t, :], in0=got[:, 2 * t, :], scalar=gates[:, 0, t:t + 1],
                                                           in1=X[:, t, :], op0=ALU.mult, op1=ALU.add).then_inc(first, 1)
                        for t in tiles:
                            dve.wait_ge(first, t + 1)
                            nc.vector.scalar_tensor_tensor(out=X[:, t, :], in0=got[:, 2 * t + 1, :], scalar=gates[:, 1, t:t + 1],
                                                           in1=X[:, t, :], op0=ALU.mult, op1=ALU.add).then_inc(second, 1)
                        for t in tiles:
                            dve.wait_ge(second, t + 1)
                            tile_stats(nc, constants, X, t).then_inc(stats_left, 1)
                    dve.wait_ge(stats_left, TILES)


def self_attention_of_one(nc, X, xT, ident, w, w_arrived):
    constants, ident = ident, ident[0]
    H = 2
    with ExitStack() as ctx:
        def sb(n, shape, dt=F32):
            return ctx.enter_context(nc.sbuf_tensor(f"one_{n}", shape, dt))

        sem = ctx.enter_context(semaphores(nc, "one"))

        wv_sb, woT_sb, bv_sb, bo_sb = w["wv"], w["woT"], w["bv"], w["bo"]
        both = sb("both", [P, DB, D])
        shift = sb("shift", [P, DB])
        branch = [sb(f"branch{h}", [P, DB, GS]) for h in range(H)]
        product = [ctx.enter_context(nc.psum_tensor(f"one_product{h}", [P, DB, GS], F32)) for h in range(H)]
        rows = [ctx.enter_context(nc.psum_tensor(f"one_rows{h}", [P, GT, D], F32)) for h in range(H)]
        both_ready, both_kept, shift_kept = sem("both_ready"), sem("both_kept"), sem("shift_kept")
        product_ready, branch_ready, rows_ready, rows_kept, stats_left = (
            sem(n) for n in ("product_ready", "branch_ready", "rows_ready", "rows_kept", "stats_left"))

        with nc.Block() as block:
            @block.tensor
            def _(pe):
                pe.wait_ge(*w_arrived)
                for i in range(DB):
                    for m in range(DB):
                        nc.tensor.matmul(product[0][:, 0, i * D:(i + 1) * D], wv_sb[:, m, i * P:(i + 1) * P],
                                         woT_sb[:, m, :], start=(m == 0), stop=(m == DB - 1))
                for o in range(DB):
                    for m in range(DB):
                        last = nc.tensor.matmul(product[0][:, 1, o:o + 1], woT_sb[:, m, o * P:(o + 1) * P],
                                                bv_sb[:, m:m + 1], start=(m == 0), stop=(m == DB - 1))
                last.then_inc(both_ready, 1)
                pe.wait_ge(both_kept, 1)
                pe.wait_ge(shift_kept, 1)
                with pe.Fori(0, GROUPS // H) as i:
                    for h in range(H):
                        for o in range(DB):
                            for b in range(DB):
                                last = nc.tensor.matmul(product[h][:, o, :], both[:, b, o * P:(o + 1) * P],
                                                        xT[:, b, bass.ds((i * H + h) * GS, GS)], start=(b == 0), stop=(b == DB - 1))
                        last.then_inc(product_ready, 1)
                    for h in range(H):
                        pe.wait_ge(branch_ready, (i * H + (h + 1)) * DB)
                        for t in range(GT):
                            for o in range(DB):
                                last = nc.tensor.transpose(rows[h][:, t, o * P:(o + 1) * P],
                                                           branch[h][:, o, t * P:(t + 1) * P], ident[:])
                        last.then_inc(rows_ready, 1)
                    pe.wait_ge(rows_kept, i * H + H)

            @block.vector
            def _(dve):
                dve.wait_ge(*w_arrived)
                dve.wait_ge(both_ready, 1)
                nc.vector.tensor_tensor(shift[:], product[0][:, 1, 0:DB], bo_sb[:], ALU.add).then_inc(shift_kept, 1)
                dve.wait_ge(shift_kept, 1)
                with dve.Fori(0, GROUPS // H) as i:
                    for h in range(H):
                        dve.wait_ge(product_ready, i * H + (h + 1))
                        for o in range(DB):
                            nc.vector.scalar_tensor_tensor(out=branch[h][:, o, :], in0=product[h][:, o, :],
                                                           scalar=shift[:, o:o + 1], in1=xT[:, o, bass.ds((i * H + h) * GS, GS)],
                                                           op0=ALU.add, op1=ALU.add).then_inc(branch_ready, 1)
                    for h in range(H):
                        dve.wait_ge(rows_kept, i * H + (h + 1))
                        for t in range(GT):
                            tile_stats(nc, constants, X, (i * H + h) * GT + t).then_inc(stats_left, 1)
                dve.wait_ge(stats_left, TILES)

            @block.scalar
            def _(act):
                act.wait_ge(both_ready, 1)
                nc.scalar.activation(both[:].rearrange("p i o -> p (i o)"), product[0][:, 0, :], ACT.Identity).then_inc(both_kept, 1)
                with act.Fori(0, GROUPS // H) as i:
                    for h in range(H):
                        act.wait_ge(rows_ready, i * H + (h + 1))
                        nc.scalar.activation(X[:, bass.ds((i * H + h) * GT, GT), :], rows[h][:], ACT.Identity).then_inc(rows_kept, 1)
                act.wait_ge(rows_kept, GROUPS)


def attend_heads(nc, X, xT, ident, heads, w_qT, w_oT, K):
    constants, ident = ident, ident[0]
    SCALE = float(W) ** -0.5
    KT = -(-K // P)
    ksize = [min(P, K - P * k) for k in range(KT)]
    PAIRS = [(0, 0), (0, 1), (0, 2), (1, 0), (1, 1), (2, 0)]
    ROWS = len(PAIRS) * W
    ALL = ROWS + PARTS
    QUAD = 4
    QUADS = HEADS // QUAD
    VW = 32
    BIG = -3.0e38
    k_dram, v_dram = heads
    q_dram = nc.dram_tensor("heads_q", [PARTS, D, S], BF16).ap()
    m_dram = nc.dram_tensor("heads_m", [GROUPS, PARTS * QUAD * GT, P], BF16).ap()

    with ExitStack() as outer:
        def keep(n, shape, dt=F32):
            return outer.enter_context(nc.sbuf_tensor(f"heads_{n}", shape, dt))

        w_o = keep("w_o", [P, DB, D])
        attended = keep("attended", [P, TILES, D])
        ident_b = keep("ident_b", [P, P], BF16)
        later = keep("later", [P, P], BF16)
        laterT = keep("laterT", [P, P], BF16)
        w_o_loaded = outer.enter_context(nc.semaphore("heads_w_o_loaded"))
        masks_made = outer.enter_context(nc.semaphore("heads_masks_made"))
        queries = [[keep(f"q{h}_{j}", [ALL, S], BF16) for j in range(QUAD)] for h in range(2)]
        keys = [[keep(f"k{h}_{j}", [ALL, K], BF16) for j in range(QUAD)] for h in range(2)]
        values = keep("values", [P, KT, D])
        values_loaded = outer.enter_context(nc.semaphore("heads_values_loaded"))
        quad_values = [keep(f"quad_values{h}", [P, KT, QUAD, VW]) for h in range(2)]
        stack_loaded = [outer.enter_context(nc.semaphore(f"heads_stack_loaded{h}")) for h in range(2)]
        ones_made = outer.enter_context(nc.semaphore("heads_ones_made"))

        def load_queries(sp, quad, h):
            for j in range(QUAD):
                for r, (a, _) in enumerate(PAIRS):
                    sp.dma_start(queries[h][j][r * W:(r + 1) * W, :],
                                 q_dram[a, bass.ds((quad * QUAD + j) * W, W), :]).then_inc(stack_loaded[h], 16)

        def load_keys(sp, quad, h):
            for j in range(QUAD):
                for r, (_, b) in enumerate(PAIRS):
                    sp.dma_start(keys[h][j][r * W:(r + 1) * W, :],
                                 k_dram[b, bass.ds((quad * QUAD + j) * W, W), :]).then_inc(stack_loaded[h], 16)

        with ExitStack() as ctx:
            def sb(n, shape, dt=F32):
                return ctx.enter_context(nc.sbuf_tensor(f"heads_{n}", shape, dt))

            sem = ctx.enter_context(semaphores(nc, "heads"))

            wq = sb("wq", [P, DB, D])
            parts = [sb(f"parts{h}", [P, PARTS, 512], BF16) for h in range(4)]
            rest = [sb(f"rest{h}", [P, 512]) for h in range(4)]
            product = [ctx.enter_context(nc.psum_tensor(f"heads_product{h}", [P, 512], F32)) for h in range(4)]
            loaded, product_ready, part1, rest1, part2, part3, zeroed = (
                sem(n) for n in ("loaded", "product_ready", "part1", "rest1", "part2", "part3", "zeroed"))
            parts_stored = [sem(f"parts_stored{h}") for h in range(4)]
            units = [(o, c) for o in range(DB) for c in range(0, S, 512)]
            N = len(units)
            B = len(parts)
            assert QUAD * W <= P and N == 2 * B

            with nc.Block() as block:
                @block.sync
                def _(sp):
                    sp.dma_start(wq[:], w_qT).then_inc(loaded, 16)
                    load_keys(sp, 0, 0)
                    for n, (o, c) in enumerate(units):
                        sp.wait_ge(part3, n + 1)
                        sp.dma_start(q_dram[:, o * P:(o + 1) * P, c:c + 512].rearrange("a p s -> p a s"),
                                     parts[n % B][:]).then_inc(parts_stored[n % B], 16)
                        if n == B - 1:
                            for h in range(B):
                                sp.wait_ge(parts_stored[h], 16)
                            load_queries(sp, 0, 0)
                    sp.dma_start(w_o[:], w_oT).then_inc(w_o_loaded, 16)
                    sp.dma_start(values[:, 0:KT - 1, :], v_dram[:, 0:KT - 1, :]).then_inc(values_loaded, 16)
                    sp.dma_start(values[0:ksize[-1], KT - 1, :], v_dram[0:ksize[-1], KT - 1, :]).then_inc(values_loaded, 16)
                    for h in range(B):
                        sp.wait_ge(parts_stored[h], N // B * 16)

                @block.gpsimd
                def _(pool):
                    nc.gpsimd.memset(ident_b[:], 0.0).then_inc(zeroed, 1)
                    nc.gpsimd.memset(later[:], 0.0).then_inc(zeroed, 1)
                    nc.gpsimd.memset(laterT[:], 0.0).then_inc(zeroed, 1)
                    pool.wait_ge(zeroed, 3)
                    nc.gpsimd.affine_select(out=ident_b[:], in_=ident_b[:], compare_op=ALU.not_equal, fill=1.0, base=0,
                                            pattern=[[-1, P]], channel_multiplier=1).then_inc(masks_made, 1)
                    nc.gpsimd.affine_select(out=later[:], in_=later[:], compare_op=ALU.is_ge, fill=BIG, base=0,
                                            pattern=[[-1, P]], channel_multiplier=1).then_inc(masks_made, 1)
                    nc.gpsimd.affine_select(out=laterT[:], in_=laterT[:], compare_op=ALU.is_ge, fill=BIG, base=0,
                                            pattern=[[1, P]], channel_multiplier=-1).then_inc(masks_made, 1)
                    pool.wait_ge(masks_made, 3)
                    for h in range(2):
                        for j in range(QUAD):
                            nc.gpsimd.memset(keys[h][j][ROWS:ALL, :], 1.0).then_inc(ones_made, 1)
                            pool.wait_ge(ones_made, h * QUAD + (j + 1))
                    for h in range(2):
                        nc.gpsimd.memset(quad_values[h][:], 0.0).then_inc(ones_made, 1)
                    pool.wait_ge(ones_made, 2 * QUAD + 2)
                    for h in range(2):
                        nc.gpsimd.memset(quad_values[h][:, :, :, W:W + 1], 1.0).then_inc(ones_made, 1)

                @block.tensor
                def _(pe):
                    pe.wait_ge(loaded, 16)
                    for n, (o, c) in enumerate(units):
                        if n >= B:
                            pe.wait_ge(rest1, n - B + 1)
                        for b in range(DB):
                            last = nc.tensor.matmul(product[n % B][:], wq[:, b, o * P:(o + 1) * P], xT[:, b, c:c + 512],
                                                    start=(b == 0), stop=(b == DB - 1))
                        last.then_inc(product_ready, 1)

                @block.scalar
                def _(act):
                    for n in range(N + 1):
                        if n < N:
                            act.wait_ge(product_ready, n + 1)
                            if n >= B:
                                act.wait_ge(parts_stored[n % B], n // B * 16)
                            nc.scalar.activation(parts[n % B][:, 0, :], product[n % B][:], ACT.Identity).then_inc(part1, 1)
                        if n:
                            act.wait_ge(rest1, n)
                            nc.scalar.activation(parts[(n - 1) % B][:, 1, :], rest[(n - 1) % B][:], ACT.Identity).then_inc(part2, 1)

                @block.vector
                def _(dve):
                    for n in range(N + 1):
                        if n < N:
                            dve.wait_ge(part1, n + 1)
                            nc.vector.tensor_tensor(rest[n % B][:], product[n % B][:], parts[n % B][:, 0, :], ALU.subtract).then_inc(rest1, 1)
                        if n:
                            dve.wait_ge(part2, n)
                            nc.vector.tensor_tensor(parts[(n - 1) % B][:, 2, :], rest[(n - 1) % B][:], parts[(n - 1) % B][:, 1, :],
                                                    ALU.subtract).then_inc(part3, 1)

        with ExitStack() as ctx:
            def sb(n, shape, dt=F32):
                return ctx.enter_context(nc.sbuf_tensor(f"heads_{n}", shape, dt))

            sem = ctx.enter_context(semaphores(nc, "heads"))

            probs = [sb(f"probs{h}", [P, QUAD, 512]) for h in range(2)]
            mixed = sb("mixed", [P, 512])
            share = sb("share", [P, GT, QUAD])
            QT = QUAD * GT
            partial = sb("partial", [P, QT, GROUPS])
            most = sb("most", [P, QT])
            most_rest = sb("most_rest", [P, QT])
            most_parts = sb("most_parts", [P, PARTS, QT], BF16)
            minus = [sb(f"minus{g}", [PARTS * QT, P], BF16) for g in range(GROUPS)]
            scores = [ctx.enter_context(nc.psum_tensor(f"heads_scores{p}", [P, 2, 512], F32)) for p in range(2)]
            mixed_ps = ctx.enter_context(nc.psum_tensor("heads_mixed_ps", [P, 512], F32))
            ROUND = 3
            turn_ps = [ctx.enter_context(nc.psum_tensor(f"heads_round{r}", [P, 512], F32)) for r in range(ROUND)]
            minus_stored = [sem(f"minus_stored{g}") for g in range(GROUPS)]
            minus_loaded = [sem(f"minus_loaded{g}") for g in range(GROUPS)]
            quad_done, values_ready, values_free, scores_ready, probs_ready, probs_free = (
                sem(n) for n in ("quad_done", "values_ready", "values_free", "scores_ready", "probs_ready", "probs_free"))
            mixed_kept, share_ready, piece_ready, piece_done, chained, most_ready = (
                sem(n) for n in ("mixed_kept", "share_ready", "piece_ready", "piece_done", "chained", "most_ready"))
            LOADS = QUAD * 2 * len(PAIRS)

            units = [(g, k) for g in range(GROUPS) for k in range(min(KT, (g + 1) * GT))]
            U = len(units)

            def pieces_of(t):
                n = min((t + 1) * P, K)
                size = -(-n // (t // GT + 1))
                return [(c, min(size, n - c)) for c in range(0, n, size)]

            AFTER = 3
            stream, waiting = [], []
            for g in range(GROUPS):
                group = [("max", g, (j, t), c) for c in range(g + 1) for t in range(GT) for j in range(QUAD)]
                stream += group[:AFTER] + [("minus", (g - 1) % GROUPS, None, None)] + group[AFTER:]
            LEAD = 80
            first = [piece for n, piece in enumerate(stream[:LEAD]) if n != AFTER]
            turn = [(0,) + piece for piece in stream[LEAD:]] + [(int(piece[:2] != ("minus", GROUPS - 1)),) + piece for piece in stream[:LEAD]]
            SLOTS = 4 * U
            TAIL = 4
            order, given = [], 0
            for u in range(U + 1):
                steps = [("score", u, 0), ("score", u, 1)] if u < U else []
                steps += [("mix", u - 1, 0), ("mix", u - 1, 1)] if u else [None, None]
                for s, step in enumerate(steps):
                    if s == 1 and u >= 2 and units[u - 1][0] != units[u - 2][0]:
                        order.append(("turn", units[u - 2][0]))
                    if step is not None:
                        order.append(step)
                        if step[0] == "mix" and step[2] == 1 and (u == U or units[u][0] != units[u - 1][0]):
                            order.append(("keep", units[u - 1][0]))
                    upto = (4 * u + s + 1) * (len(turn) - TAIL) // SLOTS if u < U else len(turn) - TAIL
                    while given < upto:
                        order.append(turn[given])
                        given += 1
            order += turn[given:] + [("turn", GROUPS - 1)]
            PIECES = len(turn) + GROUPS
            assert PIECES % ROUND == 0
            groups_first = [p[1] for p in first if p[0] == "minus"]
            groups_turn = [(p[0], p[2]) for p in turn if p[1] == "minus"]
            CHAIN = 4

            with nc.Block() as block:
                @block.sync
                def _(sp):
                    def load(quad, h):
                        load_queries(sp, quad, h)
                        load_keys(sp, quad, h)

                    def minus_to_queries(h, g, count, done):
                        sp.wait_ge(piece_done, done)
                        sp.dma_start(m_dram[g], minus[g][:]).then_inc(minus_stored[g], 16)
                        sp.wait_ge(minus_stored[g], count)
                        for j in range(QUAD):
                            sp.dma_start(queries[h][j][ROWS:ALL, g * GS:(g + 1) * GS],
                                         m_dram[g].rearrange("(a j t) q -> j a (t q)", a=PARTS, j=QUAD)[j]).then_inc(minus_loaded[g], 16)

                    def groups_of(h, quad):
                        n = len(first)
                        for step in order:
                            if step[0] in (0, 1, "turn"):
                                n += 1
                            if step[0] in (0, 1) and step[1] == "minus":
                                ahead, g = step[0], step[2]
                                minus_to_queries((h + ahead) % 2, g, quad * 16 + 16 * (1 + ahead), quad * PIECES + (n + ROUND))

                    for n, piece in enumerate(first):
                        if piece[0] == "minus":
                            minus_to_queries(0, piece[1], 16, n + 1 + ROUND)
                    load_queries(sp, 1, 1)
                    load_keys(sp, 1, 1)
                    groups_of(0, 0)
                    with sp.Fori(0, QUADS // 2 - 1) as i:
                        for h in range(2):
                            sp.wait_ge(quad_done, i * 2 + (h + 1))
                            load(i * 2 + (h + 2), h)
                            groups_of(1 - h, i * 2 + (h + 1))
                    sp.wait_ge(quad_done, QUADS - 1)
                    load(0, 0)
                    groups_of(1, QUADS - 1)
                    sp.wait_ge(stack_loaded[0], (QUADS // 2 + 1) * LOADS * 16)
                    for g in range(GROUPS):
                        sp.wait_ge(minus_loaded[g], (QUADS + (g in groups_first)) * QUAD * 16)

                @block.gpsimd
                def _(pool):
                    def copy_values(quad, h):
                        for k0, k1, r in ((0, KT - 1, P), (KT - 1, KT, ksize[-1])):
                            nc.gpsimd.tensor_copy(quad_values[h][0:r, k0:k1, :, 0:W],
                                                  values[0:r, k0:k1, :].rearrange("p k (a w) -> p k a w", w=W)[:, :, bass.ds(quad * QUAD, QUAD), :]).then_inc(
                                                      values_ready, 1)

                    pool.wait_ge(values_loaded, 32)
                    pool.sem_inc(values_free, 2)
                    with pool.Fori(0, QUADS // 2) as i:
                        for h in range(2):
                            pool.wait_ge(values_free, i * 2 + (h + 1))
                            copy_values(i * 2 + h, h)
                    pool.wait_ge(values_ready, 2 * QUADS)

                @block.tensor
                def _(pe):
                    def piece(n, h, g, at, c, groups_ready):
                        to = turn_ps[n[1] % ROUND]
                        pe.wait_ge(piece_done, n[0] + (n[1] + 1))
                        if at is None:
                            pe.wait_ge(most_ready, groups_ready)
                            last = nc.tensor.matmul(to[0:PARTS * QT, 0:P], most_parts[:].rearrange("p a q -> p (a q)"), ident_b[:],
                                                    start=True, stop=True)
                        else:
                            j, t = at
                            t += g * GT
                            c0, size = pieces_of(t)[c]
                            masked = t * P < c0 + size and c == g and t * P < K
                            last = nc.tensor.matmul(to[:, 0:size], queries[h][j][0:ROWS, t * P:(t + 1) * P], keys[h][j][0:ROWS, c0:c0 + size],
                                                    start=True, stop=not masked)
                            if masked:
                                last = nc.tensor.matmul(to[:, t * P - c0:size], ident_b[:], later[:, 0:c0 + size - t * P],
                                                        start=False, stop=True)
                        last.then_inc(piece_ready, 1)

                    pe.wait_ge(masks_made, 3)
                    pe.wait_ge(ones_made, 2 * QUAD + 4)
                    pe.wait_ge(stack_loaded[0], LOADS * 16)
                    for n, (kind, g, at, c) in enumerate(first):
                        piece((0, n), 0, g, at, c, g + 1)
                    with pe.Fori(0, QUADS // 2) as i:
                        for h in range(2):
                            quad = i * 2 + h
                            n = len(first)
                            for step in order:
                                if step[0] == "score":
                                    u, p = step[1:]
                                    g, k = units[u]
                                    c = max(0, (k - g * GT) * P)
                                    diag = k >= g * GT
                                    m = ksize[k]
                                    if k == 0 and p == 0:
                                        pe.wait_ge(minus_loaded[g], quad * (QUAD * 16) + QUAD * 16)
                                    pe.wait_ge(probs_ready, quad * (2 * U) + (2 * u + p + 1))
                                    for e in range(2):
                                        j = p * 2 + e
                                        last = nc.tensor.matmul(scores[p][0:m, e, c:512], keys[h][j][:, k * P:k * P + m],
                                                                queries[h][j][:, g * GS + c:(g + 1) * GS], start=True, stop=not diag)
                                        if diag:
                                            last = nc.tensor.matmul(scores[p][0:m, e, c:c + P], ident_b[:, 0:m], laterT[:],
                                                                    start=False, stop=True)
                                    last.then_inc(scores_ready, 1)
                                elif step[0] == "mix":
                                    u, p = step[1:]
                                    g, k = units[u]
                                    c = max(0, (k - g * GT) * P)
                                    m = ksize[k]
                                    end = u == U - 1 or units[u + 1][0] != g
                                    if u == 0 and p == 0:
                                        pe.wait_ge(values_ready, quad * 2 + 2)
                                    pe.wait_ge(probs_ready, quad * (2 * U) + (2 * u + p + 1 + 2))
                                    if k == 0 and p == 0:
                                        pe.wait_ge(mixed_kept, quad * GROUPS + (g + 1))
                                    for j in (p * 2, p * 2 + 1):
                                        last = nc.tensor.matmul(mixed_ps[j * VW:(j + 1) * VW, c:512], quad_values[h][0:m, k, j, :],
                                                                probs[u % 2][0:m, j, c:512], start=(k == 0), stop=end)
                                    if p == 1:
                                        last.then_inc(probs_free, 1)
                                elif step[0] == "turn":
                                    g = step[1]
                                    pe.wait_ge(mixed_kept, quad * GROUPS + (g + 1 + 1))
                                    pe.wait_ge(piece_done, quad * PIECES + (n + 1))
                                    for t in range(GT):
                                        last = nc.tensor.transpose(turn_ps[n % ROUND][:, t * P:(t + 1) * P], mixed[:, t * P:(t + 1) * P], ident[:])
                                    last.then_inc(piece_ready, 1)
                                    n += 1
                                elif step[0] != "keep":
                                    ahead, kind, g, at, c = step
                                    if step == turn[len(stream) - LEAD]:
                                        pe.wait_ge(stack_loaded[1 - h], i * (LOADS * 16) + (h + 1) * LOADS * 16)
                                    order_of = groups_turn.index((ahead, g)) if at is None else 0
                                    piece((quad * PIECES, n), (h + ahead) % 2, g, at, c, quad * GROUPS + (len(groups_first) + order_of + 1))
                                    n += 1
                            pe.sem_inc(quad_done, 1)
                            pe.sem_inc(values_free, 1)

                @block.scalar
                def _(act):
                    act.sem_inc(probs_ready, 2)
                    act.wait_ge(ones_made, 1)
                    with act.Fori(0, QUADS) as quad:
                        for u, (g, k) in enumerate(units):
                            c = max(0, (k - g * GT) * P)
                            m = ksize[k]
                            act.wait_ge(probs_free, quad * U + (u + 1 + (u == 0) * (U % 2)))
                            for p in range(2):
                                act.wait_ge(scores_ready, quad * (2 * U) + (2 * u + p + 1))
                                nc.scalar.activation(probs[u % 2][0:m, 2 * p:2 * p + 2, c:512], scores[p][0:m, :, c:512], ACT.Exp,
                                                     scale=SCALE).then_inc(probs_ready, 1)

                @block.vector
                def _(dve):
                    V = nc.vector

                    def piece(n, g, at, c, groups_before):
                        source = turn_ps[n[1] % ROUND]
                        dve.wait_ge(piece_ready, n[0] + (n[1] + 1))
                        if at is None:
                            V.tensor_scalar(minus[g][:], source[0:PARTS * QT, 0:P], -1.0, None, ALU.mult).then_inc(piece_done, 1)
                            return
                        j, t = at
                        size = pieces_of(g * GT + t)[c][1]
                        V.reduce_max(partial[:, j * GT + t, c:c + 1], source[:, 0:size], AX_X).then_inc(piece_done, 1)
                        if at == (QUAD - 1, GT - 1) and c == g:
                            dve.wait_ge(piece_done, n[0] + (n[1] + 1 + ROUND))
                            V.reduce_max(most[:], partial[:, :, 0:g + 1], AX_X).then_inc(chained, 1)
                            links = groups_before
                            dve.wait_ge(chained, links(1))
                            V.tensor_copy(most_parts[:, 0, :], most[:]).then_inc(chained, 1)
                            dve.wait_ge(chained, links(2))
                            V.tensor_tensor(most_rest[:], most[:], most_parts[:, 0, :], ALU.subtract).then_inc(chained, 1)
                            dve.wait_ge(chained, links(3))
                            V.tensor_copy(most_parts[:, 1, :], most_rest[:]).then_inc(chained, 1)
                            dve.wait_ge(chained, links(4))
                            V.tensor_tensor(most_parts[:, 2, :], most_rest[:], most_parts[:, 1, :], ALU.subtract).then_inc(most_ready, 1)

                    dve.sem_inc(piece_done, ROUND)
                    dve.sem_inc(probs_free, 2)
                    dve.sem_inc(mixed_kept, 1)
                    for n, (kind, g, at, c) in enumerate(first):
                        piece((0, n), g, at, c, lambda link, g=g: g * CHAIN + link)
                    with dve.Fori(0, QUADS // 2) as i:
                        for h in range(2):
                            quad = i * 2 + h
                            n = len(first)
                            cut = len([p for p in first if p[0] == "max" and p[2] == (QUAD - 1, GT - 1) and p[3] == p[1]])
                            for step in order:
                                if step[0] == "keep":
                                    g = step[1]
                                    dve.wait_ge(probs_free, quad * U + (units.index((g + 1, 0)) if g + 1 < GROUPS else U) + 2)
                                    V.tensor_copy(mixed[:], mixed_ps[:]).then_inc(mixed_kept, 1)
                                elif step[0] == "turn":
                                    g = step[1]
                                    dve.wait_ge(piece_ready, quad * PIECES + (n + 1))
                                    o = turn_ps[n % ROUND][:].rearrange("p (t j v) -> p t j v", t=GT, v=VW)
                                    V.reciprocal(share[:], o[:, :, :, W]).then_inc(share_ready, 1)
                                    dve.wait_ge(share_ready, quad * GROUPS + (g + 1))
                                    for t in range(GT):
                                        to = attended[:, g * GT + t, :].rearrange("p (a w) -> p a w", w=W)[:, bass.ds(quad * QUAD, QUAD), :]
                                        last = V.tensor_tensor(to, o[:, t, :, 0:W], share[:, t, :].unsqueeze(2).broadcast_to([P, QUAD, W]),
                                                               ALU.mult)
                                    last.then_inc(piece_done, 1)
                                    n += 1
                                elif step[0] in (0, 1):
                                    ahead, kind, g, at, c = step
                                    piece((quad * PIECES, n), g, at, c, lambda link, cut=cut, quad=quad: quad * (GROUPS * CHAIN) + (cut * CHAIN + link))
                                    if at == (QUAD - 1, GT - 1) and c == g:
                                        cut += 1
                                    n += 1
                    dve.wait_ge(piece_done, QUADS * PIECES + len(first) + ROUND)

        with ExitStack() as ctx:
            attendedT = [ctx.enter_context(nc.sbuf_tensor(f"heads_attendedT{h}", [P, DB, P], F32)) for h in range(2)]
            turned = [ctx.enter_context(nc.psum_tensor(f"heads_attended_ps{h}", [P, 512], F32)) for h in range(2)]
            out_ps = [ctx.enter_context(nc.psum_tensor(f"heads_out_ps{h}", [P, 512], F32)) for h in range(2)]
            turned_ready, turned_kept, out_ready, added, stats_left = (
                ctx.enter_context(nc.semaphore(f"heads_{n}")) for n in ("attended_turned", "attendedT_kept", "out_ready", "added", "stats_left"))
            with nc.Block() as block:
                @block.tensor
                def _(pe):
                    pe.wait_ge(w_o_loaded, 16)
                    for t in range(TILES + 1):
                        if t < TILES:
                            if t >= 2:
                                pe.wait_ge(turned_kept, t - 1)
                            for b in range(DB):
                                last = nc.tensor.transpose(turned[t % 2][:, b * P:(b + 1) * P], attended[:, t, b * P:(b + 1) * P], ident[:])
                            last.then_inc(turned_ready, 1)
                        if t:
                            pe.wait_ge(turned_kept, t)
                            if t >= 3:
                                pe.wait_ge(added, t - 2)
                            h = (t - 1) % 2
                            for b in range(DB):
                                last = nc.tensor.matmul(out_ps[h][:, 0:D], attendedT[h][:, b, :], w_o[:, b, :], start=(b == 0), stop=(b == DB - 1))
                            last.then_inc(out_ready, 1)

                @block.scalar
                def _(act):
                    for t in range(TILES):
                        act.wait_ge(turned_ready, t + 1)
                        if t >= 2:
                            act.wait_ge(out_ready, t - 1)
                        nc.scalar.activation(attendedT[t % 2][:].rearrange("p b q -> p (b q)"), turned[t % 2][:, 0:D], ACT.Identity).then_inc(turned_kept, 1)

                @block.vector
                def _(dve):
                    for t in range(TILES):
                        dve.wait_ge(out_ready, t + 1)
                        nc.vector.tensor_tensor(X[:, t, :], out_ps[t % 2][:, 0:D], X[:, t, :], ALU.add).then_inc(added, 1)
                        dve.wait_ge(added, t + 1)
                        tile_stats(nc, constants, X, t).then_inc(stats_left, 1)
                    dve.wait_ge(stats_left, TILES)


def experts_choose(nc, X, xT, ident, w, rows_back):
    constants, ident = ident, ident[0]
    E = w["WgT"].shape[-1]
    HF = w["W1T"].shape[-1]
    HB = HF // P
    CAP = S // E
    CB = CAP // P
    COPIES = P // E
    BITS = COPIES.bit_length() - 1
    PASSES = 32 // BITS
    INFO = 5
    rows_in = nc.dram_tensor("choice_rows_in", [S, D], F32).ap()
    rows_out = nc.dram_tensor("choice_rows_out", [S, D], F32).ap()

    with ExitStack() as outer:
        def keep(n, shape, dt=F32):
            return outer.enter_context(nc.sbuf_tensor(f"choice_{n}", shape, dt))

        token = keep("token", [P, E * CB], U32)
        weight = keep("weight", [P, E * CB])
        rows_stored = outer.enter_context(nc.semaphore("choice_rows_stored"))

        with ExitStack() as ctx:
            def sb(n, shape, dt=F32):
                return ctx.enter_context(nc.sbuf_tensor(f"choice_{n}", shape, dt))

            sem = ctx.enter_context(semaphores(nc, "choice"))

            wg = sb("wg", [P, DB, E])
            wg_rep = sb("wg_rep", [P, DB, E, COPIES])
            scores = sb("scores", [P, S])
            flags = sb("flags", [P, S], BF16)
            above, level, order, taken, rank, chances = (sb(n, [P, S]) for n in ("above", "level", "order", "taken", "rank", "chances"))
            shares = level
            ones = sb("ones", [P, S], BF16)
            part_i = sb("part_i", [P, 1], I32)
            step_i = sb("step_i", [P, 1], I32)
            step_pos = sb("step_pos", [P, 1])
            key, cand, unused, mask, bits, nibble = (sb(n, [P, 1], I32) for n in ("key", "cand", "unused", "mask", "bits", "nibble"))
            count, enough, found = sb("count", [P, 1]), sb("enough", [P, 1], BF16), sb("found", [P, 1])
            n_above, wanted, top, negtop, total, share = (sb(n, [P, 1]) for n in ("n_above", "wanted", "top", "negtop", "total", "share"))
            same = sb("same", [P, E, COPIES], BF16)
            slots1 = sb("slots1", [P, CAP], BF16)
            info = sb("info", [P, TILES, E, INFO], BF16)
            tile_no = sb("tile_no", [P, TILES])
            place_no = sb("place_no", [P, 1])
            rank_of = sb("rank_of", [P, TILES, E])
            chance = sb("chance", [P, TILES, E])
            rest1, rest2 = sb("rest1", [P, TILES, E]), sb("rest2", [P, TILES, E])
            hot = [sb(f"hot{h}", [P, CAP], BF16) for h in range(4)]
            slot_info = sb("slot_info", [P, E * CB, INFO])
            tok_f, tok_g, wsum = sb("tok_f", [P, E * CB]), sb("tok_g", [P, E * CB]), sb("wsum", [P, E * CB])
            score_ps = ctx.enter_context(nc.psum_tensor("choice_score_ps", [P, 4, 512], F32))
            nib_ps = ctx.enter_context(nc.psum_tensor("choice_nib_ps", [P, 512], F32))
            turned = [ctx.enter_context(nc.psum_tensor(f"choice_turned{h}", [P, 4, P], F32)) for h in range(2)]
            info_ps = ctx.enter_context(nc.psum_tensor("choice_info_ps", [P, E * CB, INFO], F32))
            loaded, wg_ready, scores_ready, scores_kept, made, same_ready = (sem(n) for n in ("loaded", "wg_ready", "scores_ready", "scores_kept", "made", "same_ready"))
            chained, enough_ready, nibble_ready, negtop_ready, chances_ready = (sem(n) for n in ("chained", "enough_ready", "nibble_ready", "negtop_ready", "chances_ready"))
            rank_ready, turned_ready, turned_kept, hot_ready, hot_used, shares_ready = (
                sem(n) for n in ("rank_ready", "turned_ready", "turned_kept", "hot_ready", "hot_used", "shares_ready"))

            with nc.Block() as block:
                @block.sync
                def _(sp):
                    sp.dma_start(wg[:], w["WgT"]).then_inc(loaded, 16)
                    sp.dma_start(rows_in.rearrange("(t p) d -> p t d", p=P), X[:]).then_inc(rows_stored, 16)
                    sp.dma_start(rows_out.rearrange("(t p) d -> p t d", p=P), X[:]).then_inc(rows_stored, 16)

                @block.gpsimd
                def _(pool):
                    exact = dict(allow_small_or_imprecise_dtypes=True)
                    nc.gpsimd.iota(part_i[:], [[0, 1]], base=0, channel_multiplier=1).then_inc(made, 1)
                    nc.gpsimd.iota(tile_no[:], [[1, TILES]], base=0, channel_multiplier=0, **exact).then_inc(made, 1)
                    nc.gpsimd.iota(place_no[:], [[0, 1]], base=0, channel_multiplier=1, **exact).then_inc(made, 1)
                    nc.gpsimd.iota(slots1[:], [[1, CAP]], base=1, channel_multiplier=0, **exact).then_inc(made, 1)
                    nc.gpsimd.memset(ones[:], 1.0).then_inc(made, 1)
                    nc.gpsimd.memset(same[:], 1.0).then_inc(same_ready, 1)
                    pool.wait_ge(same_ready, 1)
                    nc.gpsimd.affine_select(out=same[:], in_=same[:], compare_op=ALU.is_ge, fill=0.0, base=0,
                                            pattern=[[-COPIES, E], [0, COPIES]], channel_multiplier=1).then_inc(same_ready, 1)
                    pool.wait_ge(same_ready, 2)
                    nc.gpsimd.affine_select(out=same[:], in_=same[:], compare_op=ALU.is_ge, fill=0.0, base=COPIES - 1,
                                            pattern=[[COPIES, E], [0, COPIES]], channel_multiplier=-1).then_inc(same_ready, 1)

                @block.tensor
                def _(pe):
                    pe.wait_ge(wg_ready, 1)
                    for c in range(4):
                        for b in range(DB):
                            last = nc.tensor.matmul(score_ps[:, c, :], wg_rep[:, b, :, :].rearrange("p e j -> p (e j)"),
                                                    xT[:, b, c * 512:(c + 1) * 512], start=(b == 0), stop=(b == DB - 1))
                    last.then_inc(scores_ready, 1)
                    pe.wait_ge(same_ready, 3)
                    for n in range(PASSES):
                        pe.wait_ge(enough_ready, n + 1)
                        nc.tensor.matmul(nib_ps[:, 0:1], same[:].rearrange("p e j -> p (e j)"), enough[:],
                                         start=True, stop=True).then_inc(nibble_ready, 1)
                    for n, (what, ready) in enumerate(((rank, rank_ready), (shares, shares_ready))):
                        pe.wait_ge(ready, 1)
                        for q in range(TILES // 4):
                            m = n * (TILES // 4) + q
                            if m >= 2:
                                pe.wait_ge(turned_kept, m - 1)
                            for t in range(4):
                                last = nc.tensor.transpose(turned[m % 2][:, t, :], what[:, (q * 4 + t) * P:(q * 4 + t + 1) * P], ident[:])
                            last.then_inc(turned_ready, 1)
                    for t in range(TILES):
                        for e in range(E):
                            m = t * E + e
                            pe.wait_ge(hot_ready, m + 1)
                            for c in range(CB):
                                last = nc.tensor.matmul(info_ps[:, e * CB + c, :], hot[m % 4][:, c * P:(c + 1) * P], info[:, t, e, :],
                                                        start=(m == 0 and c == 0), stop=(m == TILES * E - 1 and c == CB - 1),
                                                        skip_group_check=True)
                            last.then_inc(hot_used, 1)

                @block.scalar
                def _(act):
                    act.wait_ge(scores_ready, 1)
                    nc.scalar.activation(scores[:], score_ps[:].rearrange("p a b -> p (a b)"), ACT.Identity).then_inc(scores_kept, 1)
                    act.wait_ge(negtop_ready, 1)
                    nc.scalar.activation(chances[:], scores[:], ACT.Exp, bias=negtop[:]).then_inc(chances_ready, 1)

                @block.vector
                def _(dve):
                    done = [0]

                    def link(ins):
                        done[0] += 1
                        ins.then_inc(chained, 1)
                        dve.wait_ge(chained, done[0])

                    V = nc.vector
                    dve.wait_ge(loaded, 16)
                    V.tensor_copy(wg_rep[:], wg[:].unsqueeze(3).broadcast_to([P, DB, E, COPIES])).then_inc(wg_ready, 1)
                    dve.wait_ge(made, 5)
                    link(V.tensor_scalar(step_i[:], part_i[:], COPIES - 1, None, ALU.bitwise_and))
                    link(V.tensor_copy(step_pos[:], step_i[:]))
                    link(V.tensor_scalar(step_pos[:], step_pos[:], 0.0, None, ALU.is_gt))
                    link(V.memset(key[:], 0))
                    link(V.tensor_scalar(unused[:], step_pos[:], -1.0, 1.0, ALU.mult, ALU.add))
                    link(V.tensor_scalar(unused[:], unused[:], 31, None, ALU.logical_shift_left))

                    def decode():
                        link(V.tensor_scalar(mask[:], cand[:], 31, -1, ALU.arith_shift_right, ALU.bitwise_xor))
                        link(V.tensor_scalar(mask[:], mask[:], -2 ** 31, None, ALU.bitwise_or))
                        link(V.tensor_tensor(bits[:], mask[:], cand[:], ALU.bitwise_xor))

                    dve.wait_ge(scores_kept, 1)
                    link(V.tensor_reduce(top[:], scores[:], AX_X, ALU.max))
                    V.tensor_scalar(negtop[:], top[:], -1.0, None, ALU.mult).then_inc(negtop_ready, 1)
                    for n in range(PASSES):
                        shift = 32 - BITS * (n + 1)
                        link(V.scalar_tensor_tensor(out=cand[:], in0=step_i[:], scalar=shift, in1=key[:],
                                                    op0=ALU.logical_shift_left, op1=ALU.bitwise_or))
                        link(V.tensor_tensor(cand[:], cand[:], unused[:], ALU.bitwise_or))
                        decode()
                        link(V.tensor_scalar(flags[:], scores[:], bits[:].bitcast(F32), 0.0, ALU.is_ge, ALU.add, accum_out=count[:]))
                        V.tensor_scalar(enough[:], count[:], CAP - 0.5, step_pos[:], ALU.is_gt, ALU.mult).then_inc(enough_ready, 1)
                        dve.wait_ge(nibble_ready, n + 1)
                        link(V.tensor_copy(nibble[:], nib_ps[:, 0:1]))
                        link(V.scalar_tensor_tensor(out=key[:], in0=nibble[:], scalar=shift, in1=key[:],
                                                    op0=ALU.logical_shift_left, op1=ALU.bitwise_or))
                    link(V.tensor_copy(cand[:], key[:]))
                    decode()
                    link(V.tensor_copy(found[:], bits[:].bitcast(F32)))
                    link(V.tensor_scalar(above[:], scores[:], found[:], 0.0, ALU.is_gt, ALU.add, accum_out=n_above[:]))
                    link(V.tensor_scalar(level[:], scores[:], found[:], None, ALU.is_equal))
                    link(V.tensor_scalar(wanted[:], n_above[:], -1.0, CAP + 0.5, ALU.mult, ALU.add))
                    link(V.tensor_tensor_scan(order[:], ones[:], level[:], 0.0, ALU.mult, ALU.add))
                    link(V.scalar_tensor_tensor(out=taken[:], in0=order[:], scalar=wanted[:], in1=level[:], op0=ALU.is_lt, op1=ALU.mult))
                    link(V.tensor_tensor(taken[:], taken[:], above[:], ALU.add))
                    link(V.tensor_tensor_scan(order[:], ones[:], taken[:], 0.0, ALU.mult, ALU.add))
                    V.tensor_tensor(rank[:], order[:], taken[:], ALU.mult).then_inc(rank_ready, 1)
                    dve.wait_ge(chances_ready, 1)
                    link(V.tensor_tensor(above[:], chances[:], taken[:], ALU.mult))
                    link(V.tensor_reduce(total[:], above[:], AX_X, ALU.add))
                    link(V.reciprocal(share[:], total[:]))
                    V.tensor_scalar(shares[:], chances[:], share[:], None, ALU.mult).then_inc(shares_ready, 1)
                    for n, to in enumerate((rank_of, chance)):
                        for q in range(TILES // 4):
                            m = n * (TILES // 4) + q
                            dve.wait_ge(turned_ready, m + 1)
                            V.tensor_copy(to[:, q * 4:q * 4 + 4, :], turned[m % 2][:].rearrange("p t (e j) -> p t e j", j=COPIES)[:, :, :, 0]).then_inc(turned_kept, 1)
                    dve.wait_ge(turned_kept, TILES // 2)
                    TE = [P, TILES, E]
                    link(V.tensor_copy(info[:, :, :, 0], tile_no[:].unsqueeze(2).broadcast_to(TE)))
                    link(V.tensor_copy(info[:, :, :, 1], place_no[:].unsqueeze(2).broadcast_to(TE)))
                    link(V.tensor_copy(info[:, :, :, 2], chance[:]))
                    link(V.tensor_tensor(rest1[:], chance[:], info[:, :, :, 2], ALU.subtract))
                    link(V.tensor_copy(info[:, :, :, 3], rest1[:]))
                    link(V.tensor_tensor(rest2[:], rest1[:], info[:, :, :, 3], ALU.subtract))
                    link(V.tensor_copy(info[:, :, :, 4], rest2[:]))
                    for t in range(TILES):
                        for e in range(E):
                            m = t * E + e
                            if m >= 4:
                                dve.wait_ge(hot_used, m - 3)
                            V.tensor_scalar(hot[m % 4][:], slots1[:], rank_of[:, t, e:e + 1], None, ALU.is_equal).then_inc(hot_ready, 1)
                    dve.wait_ge(hot_used, TILES * E)
                    link(V.tensor_copy(slot_info[:], info_ps[:]))
                    link(V.tensor_scalar(tok_f[:], slot_info[:, :, 0], float(P), None, ALU.mult))
                    link(V.tensor_tensor(tok_g[:], tok_f[:], slot_info[:, :, 1], ALU.add))
                    link(V.tensor_copy(token[:], tok_g[:]))
                    link(V.tensor_tensor(wsum[:], slot_info[:, :, 2], slot_info[:, :, 3], ALU.add))
                    link(V.tensor_tensor(weight[:], wsum[:], slot_info[:, :, 4], ALU.add))

        with ExitStack() as ctx:
            def sb(n, shape, dt=F32):
                return ctx.enter_context(nc.sbuf_tensor(f"choice_{n}", shape, dt))

            def ps(n, shape, dt=F32):
                return ctx.enter_context(nc.psum_tensor(f"choice_{n}", shape, dt))

            sem = ctx.enter_context(semaphores(nc, "choice"))

            W1 = [sb(f"W1_{h}", [P, DB, HF]) for h in range(2)]
            W3 = [sb(f"W3_{h}", [P, DB, HF]) for h in range(2)]
            W2 = [sb(f"W2_{h}", [P, HB, D]) for h in range(2)]
            rows = [sb(f"rows{h}", [P, CB, D]) for h in range(2)]
            rowsT = [sb(f"rowsT{h}", [P, DB, CAP]) for h in range(2)]
            gate = sb("gate", [P, HB, CAP])
            hidden = [sb(f"hidden{h}", [P, HB, CAP]) for h in range(2)]
            answer = [sb(f"answer{h}", [P, CB, D]) for h in range(2)]
            rowsT_ps = ps("rowsT_ps", [P, DB, CAP])
            gate_ps = ps("gate_ps", [P, HB, CAP])
            up_ps = ps("up_ps", [P, HB, CAP])
            answer_ps = [ps(f"answer_ps{h}", [P, CB, D]) for h in range(2)]
            W_loaded = [sem(f"W_loaded{h}") for h in range(2)]
            fetched = [sem(f"fetched{h}") for h in range(2)]
            rowsT_ready, rowsT_kept, gate_ready, up_ready, gate_kept, hidden_ready, answer_ready, answer_kept, scattered = (
                sem(n) for n in ("rowsT_ready", "rowsT_kept", "gate_ready", "up_ready", "gate_kept", "hidden_ready", "answer_ready", "answer_kept", "scattered"))

            with nc.Block() as block:
                @block.sync
                def _(sp):
                    def load(e, h):
                        for to, what in ((W1[h], w["W1T"]), (W3[h], w["W3T"]), (W2[h], w["W2T"])):
                            sp.dma_start(to[:], what[:, bass.ds(e, 1), :, :].rearrange("p a b c -> p (a b) c")).then_inc(W_loaded[h], 16)
                    load(0, 0)
                    load(1, 1)
                    with sp.Fori(0, E // 2 - 1) as i:
                        for h in range(2):
                            sp.wait_ge(answer_ready, i * 2 + (h + 1))
                            load(i * 2 + (h + 2), h)
                    sp.wait_ge(scattered, E * CB * 16)
                    for g in range(GROUPS):
                        sp.dma_start(X[:, g * GT:(g + 1) * GT, :], rows_out[g * GS:(g + 1) * GS, :].rearrange("(t p) d -> p t d", p=P)).then_inc(rows_back[g], 16)

                @block.gpsimd
                def _(pool):
                    def fetch(e):
                        for c in range(CB):
                            nc.gpsimd.indirect_dma_start(rows[e % 2][:, c, :], None, rows_in,
                                                         bass.IndirectOffsetOnAxis(ap=token[:, e * CB + c:e * CB + c + 1], axis=0)).then_inc(fetched[e % 2], 16)
                    pool.wait_ge(rows_stored, 32)
                    fetch(0)
                    fetch(1)
                    for e in range(E):
                        if e + 2 < E:
                            pool.wait_ge(rowsT_ready, e + 1)
                            fetch(e + 2)
                        pool.wait_ge(answer_kept, e * CB + CB)
                        if e:
                            pool.wait_ge(scattered, e * CB * 16)
                        for c in range(CB):
                            nc.gpsimd.indirect_dma_start(rows_out, bass.IndirectOffsetOnAxis(ap=token[:, e * CB + c:e * CB + c + 1], axis=0),
                                                         answer[e % 2][:, c, :], None, compute_op=ALU.add).then_inc(scattered, 16)

                @block.tensor
                def _(pe):
                    def turn(e, j, h):
                        pe.wait_ge(fetched[h], j * CB * 16 + CB * 16)
                        for b in range(DB):
                            for c in range(CB):
                                last = nc.tensor.transpose(rowsT_ps[:, b, c * P:(c + 1) * P], rows[h][:, c, b * P:(b + 1) * P], ident[:])
                        last.then_inc(rowsT_ready, 1)

                    def step(e, j, h, more):
                        pe.wait_ge(W_loaded[h], j * 48 + 48)
                        pe.wait_ge(rowsT_kept, e + 1)
                        for W, to, ready in ((W1, gate_ps, gate_ready), (W3, up_ps, up_ready)):
                            for f in range(HB):
                                for b in range(DB):
                                    last = nc.tensor.matmul(to[:, f, :], W[h][:, b, f * P:(f + 1) * P], rowsT[h][:, b, :],
                                                            start=(b == 0), stop=(b == DB - 1))
                            last.then_inc(ready, 1)
                        if more:
                            turn(e + 1, j + h, 1 - h)
                        pe.wait_ge(hidden_ready, e + 1)
                        for c in range(CB):
                            for f in range(HB):
                                last = nc.tensor.matmul(answer_ps[h][:, c, :], hidden[h][:, f, c * P:(c + 1) * P], W2[h][:, f, :],
                                                        start=(f == 0), stop=(f == HB - 1))
                        last.then_inc(answer_ready, 1)

                    turn(0, 0, 0)
                    with pe.Fori(0, E // 2 - 1) as i:
                        for h in range(2):
                            step(i * 2 + h, i, h, True)
                    step(E - 2, E // 2 - 1, 0, True)
                    step(E - 1, E // 2 - 1, 1, False)

                @block.scalar
                def _(act):
                    def keep_rows(e, h):
                        act.wait_ge(rowsT_ready, e + 1)
                        nc.scalar.activation(rowsT[h][:], rowsT_ps[:], ACT.Identity).then_inc(rowsT_kept, 1)

                    def step(e, h, more):
                        act.wait_ge(gate_ready, e + 1)
                        nc.scalar.activation(gate[:], gate_ps[:], ACT.Silu).then_inc(gate_kept, 1)
                        if more:
                            keep_rows(e + 1, 1 - h)
                        act.wait_ge(hidden_ready, e + 1)

                    keep_rows(0, 0)
                    with act.Fori(0, E // 2 - 1) as i:
                        for h in range(2):
                            step(i * 2 + h, h, True)
                    step(E - 2, 0, True)
                    step(E - 1, 1, False)

                @block.vector
                def _(dve):
                    for e in range(E):
                        h = e % 2
                        dve.wait_ge(up_ready, e + 1)
                        dve.wait_ge(gate_kept, e + 1)
                        nc.vector.tensor_tensor(hidden[h][:], gate[:], up_ps[:], ALU.mult).then_inc(hidden_ready, 1)
                        dve.wait_ge(answer_ready, e + 1)
                        if e >= 2:
                            dve.wait_ge(scattered, (e - 1) * CB * 16)
                        for c in range(CB):
                            nc.vector.tensor_scalar(answer[h][:, c, :], answer_ps[h][:, c, :], weight[:, e * CB + c:e * CB + c + 1],
                                                    None, ALU.mult).then_inc(answer_kept, 1)
    return constants


def loads_ahead(nc, keep, name, loads):
    arrived = keep.enter_context(nc.semaphore(f"{name}_arrived"))
    tensors = {n: keep.enter_context(nc.sbuf_tensor(f"{name}_{n}", list(what.shape), F32)) for n, what in loads.items()}
    with nc.Block() as block:
        @block.sync
        def _(sp):
            for n, what in loads.items():
                sp.dma_start(tensors[n][:], what).then_inc(arrived, 16)
    return tensors, (arrived, 16 * len(loads))


def load_tokens(nc, keep, X, x):
    arrived = [keep.enter_context(nc.semaphore(f"tokens_arrived{g}")) for g in range(GROUPS)]
    with nc.Block() as block:
        @block.sync
        def _(sp):
            for g in range(GROUPS):
                sp.dma_start(X[:, g * GT:(g + 1) * GT, :], x[:, g * GT:(g + 1) * GT, :]).then_inc(arrived[g], 16)
    return arrived


def program(nc, a, out):
    def weights(layer, *names):
        return {n: a[f"{layer}_{n}"] for n in names}

    with ExitStack() as keep:
        X = keep.enter_context(nc.sbuf_tensor("X", [P, TILES, D], F32))
        xT = keep.enter_context(nc.sbuf_tensor("xT", [P, DB, S], F32))
        constants = make_identity(nc, keep)
        heads = heads_ahead(nc, a["contextT"])

        x_arrived = load_tokens(nc, keep, X, a["x"])
        state_space(nc, X, xT, constants, weights("L0_attn", "gamma", "beta", "W_in", "conv_w", "conv_b", "W_x", "W_dt", "b_dt",
                                                  "A_log", "D_skip", "W_out"), x_arrived)
        with ExitStack() as route_keep:
            w = weights("L0_ffn", "router_W", "router_b", "ln_g", "ln_b", "W1", "b1", "W2", "b2")
            kept, ahead = route_ahead(nc, route_keep, w)
            with ExitStack() as context_keep:
                context = loads_ahead(nc, context_keep, "ctx", {"contextT": a["contextT"], "w_outT": a["L0_xattn_W_outT"]})
                normalise(nc, "first_norm", X, xT, constants)
                attend_context(nc, X, xT, constants, *context, ahead)
            normalise(nc, "context_norm", X, xT, constants)
            route_to_two(nc, X, xT, constants, w, kept, heads, a["contextT"], a["L1_xattn_w_kT"], a["L1_xattn_w_vT"])

        with ExitStack() as one_keep:
            one = loads_ahead(nc, one_keep, "one", weights("L1_attn", "wv", "woT", "bv", "bo"))
            normalise(nc, "route_norm", X, xT, constants)
            self_attention_of_one(nc, X, xT, constants, *one)
        normalise(nc, "one_norm", X, xT, constants)
        attend_heads(nc, X, xT, constants, heads, a["L1_xattn_w_qT"], a["L1_xattn_w_oT"], a["contextT"].shape[-1])
        normalise(nc, "heads_norm", X, xT, constants)
        rows_back = [keep.enter_context(nc.semaphore(f"rows_back{g}")) for g in range(GROUPS)]
        experts_choose(nc, X, xT, constants, weights("L1_ffn", "WgT", "W1T", "W2T", "W3T"), rows_back)
        normalise(nc, "last_norm", X, None, constants, arrived=rows_back, out=out.rearrange("a (t p) d -> p (a t) d", p=P))


def by_partition(a):
    a = a.reshape(*a.shape[:-2], a.shape[-2] // P, P, a.shape[-1])
    return np.ascontiguousarray(np.moveaxis(a, -2, 0))


def columns(v):
    v = v.reshape(*v.shape[:-1], v.shape[-1] // P, P)
    return np.ascontiguousarray(np.moveaxis(v, -1, 0))


def layout(i):
    t = lambda a: np.swapaxes(a, -1, -2)
    return {
        "x": by_partition(i["x"][0]),
        "contextT": by_partition(t(i["ctx_1024"][0])),
        "L0_xattn_W_outT": by_partition(t(i["L0_xattn_W_out"])),
        "L0_ffn_router_W": by_partition(i["L0_ffn_router_W"]),
        "L0_ffn_router_b": i["L0_ffn_router_b"].reshape(-1, 1),
        "L0_ffn_ln_g": columns(i["L0_ffn_ln_g"]),
        "L0_ffn_ln_b": columns(i["L0_ffn_ln_b"]),
        "L0_ffn_W1": by_partition(i["L0_ffn_W1"]),
        "L0_ffn_b1": i["L0_ffn_b1"],
        "L0_ffn_W2": by_partition(i["L0_ffn_W2"]),
        "L0_ffn_b2": i["L0_ffn_b2"],
        "L1_ffn_WgT": by_partition(t(i["L1_ffn_Wg"])),
        "L1_ffn_W1T": by_partition(t(i["L1_ffn_W1"])),
        "L1_ffn_W3T": by_partition(t(i["L1_ffn_W3"])),
        "L1_ffn_W2T": by_partition(t(i["L1_ffn_W2"])),
        "L1_xattn_w_qT": by_partition(t(i["L1_xattn_w_q"])),
        "L1_xattn_w_kT": by_partition(t(i["L1_xattn_w_k"])),
        "L1_xattn_w_vT": by_partition(t(i["L1_xattn_w_v"])),
        "L1_xattn_w_oT": by_partition(t(i["L1_xattn_w_o"])),
        "L0_attn_gamma": columns(i["L0_attn_gamma"]),
        "L0_attn_beta": columns(i["L0_attn_beta"]),
        "L0_attn_W_in": by_partition(i["L0_attn_W_in"]),
        "L0_attn_conv_w": by_partition(i["L0_attn_conv_w"]),
        "L0_attn_conv_b": columns(i["L0_attn_conv_b"]),
        "L0_attn_W_x": by_partition(i["L0_attn_W_x"]),
        "L0_attn_W_dt": i["L0_attn_W_dt"],
        "L0_attn_b_dt": columns(i["L0_attn_b_dt"]),
        "L0_attn_A_log": by_partition(i["L0_attn_A_log"]),
        "L0_attn_D_skip": columns(i["L0_attn_D_skip"]),
        "L0_attn_W_out": by_partition(i["L0_attn_W_out"]),
        "L1_attn_wv": by_partition(i["L1_attn_wv"]),
        "L1_attn_woT": by_partition(t(i["L1_attn_wo"])),
        "L1_attn_bv": columns(i["L1_attn_bv"]),
        "L1_attn_bo": columns(i["L1_attn_bo"]),
    }


def kernel(**inputs):
    import numpy as _np
    import concourse.bacc as _bacc
    from concourse import mybir as _mybir
    from concourse.bass_utils import run_bass_kernel_spmd as _run

    nc = _bacc.Bacc("TRN2", target_bir_lowering=False, num_devices=1)
    arrays, args = {}, {}
    for name, a in layout({n: _np.asarray(v) for n, v in inputs.items()}).items():
        a = _np.ascontiguousarray(a)
        arrays[f"in_{name}_dram"] = a
        args[name] = nc.dram_tensor(f"in_{name}_dram", a.shape, _mybir.dt.from_np(a.dtype), kind="ExternalInput").ap()
    out = nc.dram_tensor("out_0_dram", inputs["x"].shape, F32, kind="ExternalOutput").ap()
    program(nc, args, out)
    if not nc.is_finalized():
        nc.finalize()
    r = _run(nc, [arrays], core_ids=[0])
    return r.results[0]["out_0_dram"]
```
